# Optimizing a Trainium2 kernel written in Bass

```python
import numpy as np
import jax
import jax.numpy as jnp

def _softmax(x, axis=-1):
    return jax.nn.softmax(x, axis=axis)

def _gelu(x):
    return jax.nn.gelu(x, approximate=True)

def _silu(x):
    return jax.nn.silu(x)

def _sigmoid(x):
    return jax.nn.sigmoid(x)

def _layernorm(x, axis=-1, eps=1e-05):
    m = jnp.mean(x, axis=axis, keepdims=True)
    v = jnp.var(x, axis=axis, keepdims=True)
    return (x - m) / jnp.sqrt(v + eps)

def _scatter_add(tgt, idx, src, axis=0):
    return tgt.at[idx].add(src)

def _segment_sum(src, seg, n):
    return jax.ops.segment_sum(src, seg, n)
kernel_name = 'mk_seq_postln_d1_jaxref_r4_76dfff'

def setup_inputs(seed: int=0):
    np.random.seed(seed)
    _w = jnp.asarray

    def _L0_attn_setup():
        import jax, jax.numpy as jnp
        import numpy as np
        D_MODEL = 512
        NUM_HEADS = 16
        D_KV = D_MODEL // NUM_HEADS
        THETA = 10000.0
        N_LORA = 4
        RANK = 16
        BATCH = 2
        SEQ = 512

        def _adapter_ids(starts, batch):
            ids = jnp.searchsorted(starts, jnp.arange(batch), side='right') - 1
            return jnp.clip(ids, 0, starts.shape[0] - 1)

        def _multilora(x, ids, W, A, B):
            base = jnp.einsum('bsd,od->bso', x, W)
            Ai, Bi = (A[ids], B[ids])
            low = jnp.einsum('bsd,brd->bsr', x, Ai)
            return base + jnp.einsum('bsr,bor->bso', low, Bi)

        def _rope(x):
            d = x.shape[-1]
            pos = jnp.arange(x.shape[-2], dtype=jnp.float32)
            inv_freq = THETA ** (-jnp.arange(0, d, 2, dtype=jnp.float32) / d)
            ang = pos[:, None] * inv_freq[None, :]
            cos, sin = (jnp.cos(ang), jnp.sin(ang))
            x1, x2 = (x[..., 0::2], x[..., 1::2])
            o1 = x1 * cos - x2 * sin
            o2 = x1 * sin + x2 * cos
            return jnp.stack([o1, o2], axis=-1).reshape(x.shape)
        key = jax.random.key(seed)
        ks = jax.random.split(key, 16)
        s = 0.02
        inp = {'x': jax.random.normal(ks[0], (BATCH, SEQ, D_MODEL), jnp.float32), 'lora_start_indices': jnp.sort(jax.random.randint(ks[1], (N_LORA,), 0, BATCH)), 'Wq': jax.random.normal(ks[2], (D_MODEL, D_MODEL), jnp.float32) * s, 'Aq': jax.random.normal(ks[3], (N_LORA, RANK, D_MODEL), jnp.float32) * s, 'Bq': jax.random.normal(ks[4], (N_LORA, D_MODEL, RANK), jnp.float32) * s, 'Wk': jax.random.normal(ks[5], (D_MODEL, D_MODEL), jnp.float32) * s, 'Ak': jax.random.normal(ks[6], (N_LORA, RANK, D_MODEL), jnp.float32) * s, 'Bk': jax.random.normal(ks[7], (N_LORA, D_MODEL, RANK), jnp.float32) * s, 'Wv': jax.random.normal(ks[8], (D_MODEL, D_MODEL), jnp.float32) * s, 'Av': jax.random.normal(ks[9], (N_LORA, RANK, D_MODEL), jnp.float32) * s, 'Bv': jax.random.normal(ks[10], (N_LORA, D_MODEL, RANK), jnp.float32) * s, 'Wo': jax.random.normal(ks[11], (D_MODEL, D_MODEL), jnp.float32) * s, 'Ao': jax.random.normal(ks[12], (N_LORA, RANK, D_MODEL), jnp.float32) * s, 'Bo': jax.random.normal(ks[13], (N_LORA, D_MODEL, RANK), jnp.float32) * s}
        return inp
    _L0_attn_in = _L0_attn_setup()

    def _L0_ffn_setup():
        import jax, jax.numpy as jnp
        import numpy as np
        B_, S, D = (2, 512, 512)
        F_ = 2048
        R = 16
        H = 16
        HD = D // H
        MOD_SCALE = 0.1
        EPS = 1e-06

        def _rmsnorm(x, w):
            v = jnp.mean(x * x, axis=-1, keepdims=True)
            return x * jax.lax.rsqrt(v + EPS) * w

        def _attention(x, Wq, Wk, Wv, Wo):
            b, s, d = x.shape
            q = (x @ Wq.T).reshape(b, s, H, HD)
            k = (x @ Wk.T).reshape(b, s, H, HD)
            v = (x @ Wv.T).reshape(b, s, H, HD)
            scores = jnp.einsum('bqhd,bkhd->bhqk', q, k) / np.sqrt(HD).astype(np.float32)
            causal = jnp.tril(jnp.ones((s, s), bool))
            scores = jnp.where(causal, scores, jnp.finfo(scores.dtype).min)
            probs = jax.nn.softmax(scores, axis=-1)
            out = jnp.einsum('bhqk,bkhd->bqhd', probs, v).reshape(b, s, d)
            return out @ Wo.T
        key = jax.random.key(seed)
        ks = jax.random.split(key, 12)
        sd = 0.02
        return {'hidden_states': jax.random.normal(ks[0], (B_, S, D), jnp.float32), 'ln1_w': jnp.ones((D,), jnp.float32), 'ln2_w': jnp.ones((D,), jnp.float32), 'Wq': jax.random.normal(ks[1], (D, D), jnp.float32) * sd, 'Wk': jax.random.normal(ks[2], (D, D), jnp.float32) * sd, 'Wv': jax.random.normal(ks[3], (D, D), jnp.float32) * sd, 'Wo': jax.random.normal(ks[4], (D, D), jnp.float32) * sd, 'A': jax.random.normal(ks[5], (D, R), jnp.float32) * (0.01 / np.sqrt(D)), 'B': jax.random.normal(ks[6], (R, F_), jnp.float32) * (0.01 / np.sqrt(R)), 'W_in_base': jax.random.normal(ks[7], (F_, D), jnp.float32) * sd, 'W_up_base': jax.random.normal(ks[8], (F_, D), jnp.float32) * sd, 'W_down': jax.random.normal(ks[9], (D, F_), jnp.float32) * sd}
    _L0_ffn_in = _L0_ffn_setup()
    _d = {'L0_attn_x': _L0_attn_in['x'], 'L0_attn_lora_start_indices': _L0_attn_in['lora_start_indices'], 'L0_attn_Wq': _L0_attn_in['Wq'], 'L0_attn_Aq': _L0_attn_in['Aq'], 'L0_attn_Bq': _L0_attn_in['Bq'], 'L0_attn_Wk': _L0_attn_in['Wk'], 'L0_attn_Ak': _L0_attn_in['Ak'], 'L0_attn_Bk': _L0_attn_in['Bk'], 'L0_attn_Wv': _L0_attn_in['Wv'], 'L0_attn_Av': _L0_attn_in['Av'], 'L0_attn_Bv': _L0_attn_in['Bv'], 'L0_attn_Wo': _L0_attn_in['Wo'], 'L0_attn_Ao': _L0_attn_in['Ao'], 'L0_attn_Bo': _L0_attn_in['Bo'], 'L0_ffn_ln1_w': _L0_ffn_in['ln1_w'], 'L0_ffn_ln2_w': _L0_ffn_in['ln2_w'], 'L0_ffn_Wq': _L0_ffn_in['Wq'], 'L0_ffn_Wk': _L0_ffn_in['Wk'], 'L0_ffn_Wv': _L0_ffn_in['Wv'], 'L0_ffn_Wo': _L0_ffn_in['Wo'], 'L0_ffn_A': _L0_ffn_in['A'], 'L0_ffn_B': _L0_ffn_in['B'], 'L0_ffn_W_in_base': _L0_ffn_in['W_in_base'], 'L0_ffn_W_up_base': _L0_ffn_in['W_up_base'], 'L0_ffn_W_down': _L0_ffn_in['W_down']}
    _x0 = _d['L0_attn_x']
    _d['L0_attn_x'] = jax.random.normal(jax.random.fold_in(jax.random.key(seed), 1), (8, 512, 512), dtype=_x0.dtype)
    del _x0
    return _d

def reference(L0_attn_x, L0_attn_lora_start_indices, L0_attn_Wq, L0_attn_Aq, L0_attn_Bq, L0_attn_Wk, L0_attn_Ak, L0_attn_Bk, L0_attn_Wv, L0_attn_Av, L0_attn_Bv, L0_attn_Wo, L0_attn_Ao, L0_attn_Bo, L0_ffn_ln1_w, L0_ffn_ln2_w, L0_ffn_Wq, L0_ffn_Wk, L0_ffn_Wv, L0_ffn_Wo, L0_ffn_A, L0_ffn_B, L0_ffn_W_in_base, L0_ffn_W_up_base, L0_ffn_W_down):

    def _L0_attn_ref(x, lora_start_indices, Wq, Aq, Bq, Wk, Ak, Bk, Wv, Av, Bv, Wo, Ao, Bo):
        import jax, jax.numpy as jnp
        import numpy as np
        D_MODEL = 512
        NUM_HEADS = 16
        D_KV = D_MODEL // NUM_HEADS
        THETA = 10000.0
        N_LORA = 4
        RANK = 16
        BATCH = 2
        SEQ = 512

        def _adapter_ids(starts, batch):
            ids = jnp.searchsorted(starts, jnp.arange(batch), side='right') - 1
            return jnp.clip(ids, 0, starts.shape[0] - 1)

        def _multilora(x, ids, W, A, B):
            base = jnp.einsum('bsd,od->bso', x, W)
            Ai, Bi = (A[ids], B[ids])
            low = jnp.einsum('bsd,brd->bsr', x, Ai)
            return base + jnp.einsum('bsr,bor->bso', low, Bi)

        def _rope(x):
            d = x.shape[-1]
            pos = jnp.arange(x.shape[-2], dtype=jnp.float32)
            inv_freq = THETA ** (-jnp.arange(0, d, 2, dtype=jnp.float32) / d)
            ang = pos[:, None] * inv_freq[None, :]
            cos, sin = (jnp.cos(ang), jnp.sin(ang))
            x1, x2 = (x[..., 0::2], x[..., 1::2])
            o1 = x1 * cos - x2 * sin
            o2 = x1 * sin + x2 * cos
            return jnp.stack([o1, o2], axis=-1).reshape(x.shape)
        b, s, _ = x.shape
        ids = _adapter_ids(lora_start_indices, b)
        Q = _multilora(x, ids, Wq, Aq, Bq)
        K = _multilora(x, ids, Wk, Ak, Bk)
        V = _multilora(x, ids, Wv, Av, Bv)
        split = lambda t: t.reshape(b, s, NUM_HEADS, D_KV).transpose(0, 2, 1, 3)
        Q, K, V = (split(Q), split(K), split(V))
        Q, K = (_rope(Q), _rope(K))
        scores = jnp.einsum('bhqd,bhkd->bhqk', Q, K) / jnp.sqrt(jnp.asarray(D_KV, x.dtype))
        causal = jnp.tril(jnp.ones((s, s), bool))
        scores = jnp.where(causal, scores, jnp.asarray(-jnp.inf, scores.dtype))
        attn = jax.nn.softmax(scores, axis=-1)
        out = jnp.einsum('bhqk,bhkd->bhqd', attn, V)
        out = out.transpose(0, 2, 1, 3).reshape(b, s, D_MODEL)
        return _multilora(out, ids, Wo, Ao, Bo)

    def _L0_ffn_ref(hidden_states, ln1_w, ln2_w, Wq, Wk, Wv, Wo, A, B, W_in_base, W_up_base, W_down):
        import jax, jax.numpy as jnp
        import numpy as np
        B_, S, D = (2, 512, 512)
        F_ = 2048
        R = 16
        H = 16
        HD = D // H
        MOD_SCALE = 0.1
        EPS = 1e-06

        def _rmsnorm(x, w):
            v = jnp.mean(x * x, axis=-1, keepdims=True)
            return x * jax.lax.rsqrt(v + EPS) * w

        def _attention(x, Wq, Wk, Wv, Wo):
            b, s, d = x.shape
            q = (x @ Wq.T).reshape(b, s, H, HD)
            k = (x @ Wk.T).reshape(b, s, H, HD)
            v = (x @ Wv.T).reshape(b, s, H, HD)
            scores = jnp.einsum('bqhd,bkhd->bhqk', q, k) / np.sqrt(HD).astype(np.float32)
            causal = jnp.tril(jnp.ones((s, s), bool))
            scores = jnp.where(causal, scores, jnp.finfo(scores.dtype).min)
            probs = jax.nn.softmax(scores, axis=-1)
            out = jnp.einsum('bhqk,bkhd->bqhd', probs, v).reshape(b, s, d)
            return out @ Wo.T
        residual = hidden_states
        x = _rmsnorm(hidden_states, ln1_w)
        attn = _attention(x, Wq, Wk, Wv, Wo)
        mod = MOD_SCALE * jnp.tanh(attn @ A)
        h = _rmsnorm(residual, ln2_w)
        gate_pre = h @ W_in_base.T + mod * (h @ A) @ B
        gate = jax.nn.silu(gate_pre)
        up = h @ W_up_base.T
        mlp_out = gate * up @ W_down.T
        return residual + mlp_out
    x = L0_attn_x
    x = _layernorm(x + _L0_attn_ref(x, L0_attn_lora_start_indices, L0_attn_Wq, L0_attn_Aq, L0_attn_Bq, L0_attn_Wk, L0_attn_Ak, L0_attn_Bk, L0_attn_Wv, L0_attn_Av, L0_attn_Bv, L0_attn_Wo, L0_attn_Ao, L0_attn_Bo), axis=-1)
    x = _layernorm(x + _L0_ffn_ref(x, L0_ffn_ln1_w, L0_ffn_ln2_w, L0_ffn_Wq, L0_ffn_Wk, L0_ffn_Wv, L0_ffn_Wo, L0_ffn_A, L0_ffn_B, L0_ffn_W_in_base, L0_ffn_W_up_base, L0_ffn_W_down), axis=-1)
    return x

_drawn_inputs = setup_inputs


def setup_inputs(seed=0):
    import zlib

    import numpy as np

    out = dict(_drawn_inputs(seed))
    spreads = {'L0_ffn_ln1_w': (1.0, 0.6), 'L0_ffn_ln2_w': (1.0, 0.6)}
    factors = {'L0_attn_Wq': 8.0,
     'L0_attn_Aq': 8.0,
     'L0_attn_Bq': 8.0,
     'L0_attn_Wk': 8.0,
     'L0_attn_Ak': 8.0,
     'L0_attn_Bk': 8.0,
     'L0_attn_Av': 8.0,
     'L0_attn_Bv': 8.0,
     'L0_attn_Ao': 8.0,
     'L0_attn_Bo': 8.0,
     'L0_ffn_Wq': 200.0,
     'L0_ffn_Wk': 200.0,
     'L0_ffn_Wv': 200.0,
     'L0_ffn_Wo': 200.0,
     'L0_ffn_A': 200.0,
     'L0_ffn_B': 200.0}
    for name, (base, spread) in spreads.items():
        noise = np.random.default_rng([zlib.crc32(name.encode()), seed]).standard_normal(out[name].shape)
        drawn = base * np.exp(spread * noise) if base else spread * noise
        out[name] = jnp.asarray(drawn.astype(out[name].dtype))
    for name, factor in factors.items():
        out[name] = (out[name] * factor).astype(out[name].dtype)
    return out
```

```python
from contextlib import ExitStack

import numpy as np

import concourse.bass as bass
from concourse import mybir
from concourse.alu_op_type import AluOpType as ALU

F32 = mybir.dt.float32
F32R = mybir.dt.float32r
BF16 = mybir.dt.bfloat16
I32 = mybir.dt.int32
ACT = mybir.ActivationFunctionType

P = 128
BATCH, SEQ, D = 8, 512, 512
HEADS, HD = 16, 32
F = 2048
RANK = 16
ADAPTERS = 4
KC = D // P
TT = SEQ // P
GROUPS, GH = 4, 4
UNITS = 3 * GH
SCALE = float(HD) ** -0.5
NEG = -1.0e30
LN_EPS, RMS_EPS, MOD_SCALE = 1e-5, 1e-6, 0.1
RSQRT_MAGIC = float(0x5F3759DF)

PASSES = ((0, 0), (0, 1), (1, 0))

KEY_MAJOR = (((0, 0, 512),), ((1, 0, 384),), ((2, 0, 256), (3, 256, 128)))
QUERY_MAJOR = (((3, 0, 512),), ((2, 0, 384),), ((1, 0, 256), (0, 256, 128)))
WIDTH = (512, 384, 384)

COS, SIN, EYE, ROWMASK, COLMASK, COUNT = 0, 512, 1024, 1152, 1664, 1792
CONSTS = 1800


def at_least(eng, sem, value):
    if not isinstance(value, int) or value > 0:
        eng.wait_ge(sem, value)


def apart(eng, met, sem, value):
    if isinstance(value, int):
        at_least(eng, sem, value)
    else:
        eng.compute_val(value)
        eng.wait_ge(met, 1)
        eng.wait_ge(sem, value)


def batches(eng, body):
    body(0)
    with eng.Fori(1, BATCH - 1) as b:
        body(b)
    body(BATCH - 1)


def is_last(b):
    return isinstance(b, int) and b == BATCH - 1


class Attention:

    def __init__(self, nc, ctx, name, vd, ring):
        def sb(what, shape, dt=F32):
            return ctx.enter_context(nc.sbuf_tensor(f"{name}_{what}", shape, dt))

        def sem(what):
            return ctx.enter_context(nc.semaphore(f"{name}_{what}"))

        self.ring = ring
        self.vd = vd
        self.vcols = 2 * vd + 1
        self.sum_row = 2 * vd
        self.q_stack = [sb(f"q_stack{i}", [P, GH, SEQ], F32R) for i in range(2)]
        self.k_stack = [sb(f"k_stack{i}", [P, GH, SEQ], F32R) for i in range(2)]
        self.q_split = sb("q_split", [P, 2, SEQ], F32R)
        self.k_split = sb("k_split", [P, 2, SEQ], F32R)
        self.value = sb("value", [P, TT, HEADS, self.vcols], F32R)
        self.prob = sb("prob", [P, 2, SEQ])
        self.prob_hi = sb("prob_hi", [P, ring, SEQ], F32R)
        self.prob_lo = sb("prob_lo", [P, ring, SEQ], F32R)
        self.junk = sb("junk", [P, 2, SEQ], BF16)
        self.rowmax = sb("rowmax", [P, TT, GH])
        self.shift = sb("shift", [P, TT, 2 * GH], F32R)
        self.shift_row = sb("shift_row", [RANK, SEQ], F32R)
        self.pv_raw = sb("pv_raw", [P, GH, SEQ])

        self.scores_ps = ctx.enter_context(nc.psum_tensor(f"{name}_scores_ps", [P, 2, SEQ], F32))
        self.scores_t_ps = ctx.enter_context(nc.psum_tensor(f"{name}_scores_t_ps", [P, 2, SEQ], F32))
        self.pv_ps = ctx.enter_context(nc.psum_tensor(f"{name}_pv_ps", [P, SEQ], F32))

        self.ones_set = sem("ones_set")
        self.q_ready = sem("q_ready")
        self.k_ready = sem("k_ready")
        self.stacked = [sem(f"stacked{i}") for i in range(2)]
        self.score_ready = sem("score_ready")
        self.score_read = sem("score_read")
        self.shift_ready = sem("shift_ready")
        self.shift_turned = sem("shift_turned")
        self.shift_copied = sem("shift_copied")
        self.shifted = sem("shifted")
        self.score_t_ready = sem("score_t_ready")
        self.exp_done = sem("exp_done")
        self.lo_done = sem("lo_done")
        self.pv_done = sem("pv_done")
        self.pv_copied = sem("pv_copied")
        self.shift_hi = sem("shift_hi")
        self.value_ready = sem("value_ready")
        self.gathered = sem("gathered")




def group(b, g, ahead=0):
    return b + (g + ahead) // GROUPS, (g + ahead) % GROUPS


def number(b, g):
    return b * GROUPS + g


def uses(b, g):
    return b * (GROUPS // 2) + g // 2 + 1


def score_unit(pe, at, b, g, k):
    h, j = divmod(k, 3)
    n = number(b, g)
    if k == 0:
        pe.wait_ge(at.stacked[g % 2], uses(b, g) * 96)
    at_least(pe, at.score_read, n * UNITS + k - 1)
    q, key = at.q_stack[g % 2], at.k_stack[g % 2]
    for i, (qt, col, width) in enumerate(QUERY_MAJOR[j]):
        mm = pe.matmul(at.scores_ps[:, k % 2, col:col + width], q[0:96, h, qt * P:qt * P + P],
                       key[0:96, h, 0:(qt + 1) * P], start=(i == 0), stop=True, skip_group_check=True)
    mm.then_inc(at.score_ready, 1)


def score_max(dve, at, rowmask, b, g, k):
    h, j = divmod(k, 3)
    n = number(b, g)
    apart(dve, at.ones_set, at.score_ready, n * UNITS + k + 1)
    if k == 0:
        apart(dve, at.ones_set, at.shift_ready, n)
    apart(dve, at.ones_set, at.score_read, n * UNITS + k - 1)
    for qt, col, width in QUERY_MAJOR[j]:
        last = dve.tensor_tensor_reduce(at.junk[:, k % 2, col:col + width], at.scores_ps[:, k % 2, col:col + width],
                                        rowmask[:, SEQ - width:SEQ], 1.0, 4 * NEG, ALU.add, ALU.max,
                                        at.rowmax[:, qt, h:h + 1])
    last.then_inc(at.score_read, 1)


def shift_split(dve, at, b, g):
    n = number(b, g)
    dve.wait_ge(at.score_read, (n + 1) * UNITS)
    at_least(dve, at.shift_turned, n)
    dve.tensor_scalar(at.shift[:, :, 0:GH], at.rowmax[:, :, :], -1.0, None, ALU.mult).then_inc(at.shift_hi, 1)
    dve.wait_ge(at.shift_hi, n + 1)
    dve.scalar_tensor_tensor(out=at.shift[:, :, GH:2 * GH], in0=at.rowmax[:, :, :], scalar=-1.0,
                             in1=at.shift[:, :, 0:GH], op0=ALU.mult,
                             op1=ALU.subtract).then_inc(at.shift_ready, 1)


def shift_turn(pe, at, aux_ps, eye, b, g):
    n = number(b, g)
    pe.wait_ge(at.shift_ready, n + 1)
    at_least(pe, at.shift_copied, n)
    for qt in range(TT):
        mm = pe.transpose(aux_ps[0:2 * GH, qt * P:qt * P + P].bitcast(F32R), at.shift[:, qt, :], eye[:, :])
    mm.then_inc(at.shift_turned, 1)


def shift_copy(act, at, aux_ps, b, g):
    n = number(b, g)
    act.wait_ge(at.shift_turned, n + 1)
    at_least(act, at.shifted, n * 32)
    act.activation(at.shift_row[0:2 * GH, :], aux_ps[0:2 * GH, :].bitcast(F32R),
                   ACT.Copy).then_inc(at.shift_copied, 1)


def shift_send(sp, at, b, g):
    n = number(b, g)
    sp.wait_ge(at.shift_copied, n + 1)
    q = at.q_stack[g % 2]
    for r in range(2):
        sp.dma_start(q[96 + r:97 + r, :, :].bitcast(F32),
                     at.shift_row[r * GH:(r + 1) * GH, :].bitcast(F32)).then_inc(at.shifted, 16)


def stack_send(sp, at, b, g):
    n = number(b, g)
    q, key = at.q_stack[g % 2], at.k_stack[g % 2]
    apart(sp, at.ones_set, at.score_t_ready, (n - 1) * UNITS)
    apart(sp, at.ones_set, at.q_ready, n + 1)
    for r, part in enumerate((0, 0, 1)):
        sp.dma_start(q[32 * r:32 * r + 32, :, :].bitcast(F32),
                     at.q_split[:, part, :].bitcast(F32)).then_inc(at.stacked[g % 2], 16)
    sp.wait_ge(at.k_ready, n + 1)
    for r, part in enumerate((0, 1, 0)):
        sp.dma_start(key[32 * r:32 * r + 32, :, :].bitcast(F32),
                     at.k_split[:, part, :].bitcast(F32)).then_inc(at.stacked[g % 2], 16)


def score_t_unit(pe, at, eye_bf, colmask, b, g, k):
    h, j = divmod(k, 3)
    n = number(b, g)
    if k == 0:
        pe.wait_ge(at.shifted, n * 32 + 32)
    at_least(pe, at.exp_done, n * UNITS + k - 1)
    q, key = at.q_stack[g % 2], at.k_stack[g % 2]
    for i, (kt, col, width) in enumerate(KEY_MAJOR[j]):
        pe.matmul(at.scores_t_ps[:, k % 2, col:col + width], key[0:98, h, kt * P:kt * P + P],
                  q[0:98, h, kt * P:SEQ], start=(i == 0), stop=False, skip_group_check=True)
    for kt, col, width in KEY_MAJOR[j]:
        mm = pe.matmul(at.scores_t_ps[:, k % 2, col:col + P], eye_bf[:, :], colmask[:, :],
                       start=False, stop=True, skip_group_check=True)
    mm.then_inc(at.score_t_ready, 1)


def exp_unit(act, at, b, g, k):
    u, w = number(b, g) * UNITS + k, WIDTH[k % 3]
    act.wait_ge(at.score_t_ready, u + 1)
    at_least(act, at.lo_done, u - 1)
    act.activation(at.prob[:, k % 2, 0:w], at.scores_t_ps[:, k % 2, 0:w], ACT.Exp, scale=SCALE)
    at_least(act, at.pv_done, u + 1 - at.ring)
    act.activation(at.prob_hi[:, k % at.ring, 0:w], at.scores_t_ps[:, k % 2, 0:w], ACT.Exp,
                   scale=SCALE).then_inc(at.exp_done, 1)


def lo_unit(dve, at, b, g, k):
    u, w = number(b, g) * UNITS + k, WIDTH[k % 3]
    dve.wait_ge(at.exp_done, u + 1)
    dve.tensor_tensor(at.prob_lo[:, k % at.ring, 0:w], at.prob[:, k % 2, 0:w], at.prob_hi[:, k % at.ring, 0:w],
                      ALU.subtract).then_inc(at.lo_done, 1)


def pv_unit(pe, at, b, g, k):
    h, j = divmod(k, 3)
    n = number(b, g)
    pe.wait_ge(at.lo_done, n * UNITS + k + 1)
    if j == 0:
        at_least(pe, at.pv_copied, n * GH + h)
    if g == 0 and h == 0:
        pe.wait_ge(at.value_ready, b * TT + (1, 2, 4)[j])
    for kt, col, width in KEY_MAJOR[j]:
        for part, prob in enumerate((at.prob_hi, at.prob_lo)):
            mm = pe.matmul(at.pv_ps[0:at.vcols, kt * P:SEQ], at.value[:, kt, g * GH + h, :],
                           prob[:, k % at.ring, col:col + width], start=(kt == 0 and part == 0),
                           stop=(kt == TT - 1 and part == 1), skip_group_check=True)
    mm.then_inc(at.pv_done, 1)


def pv_copy(act, at, b, g, h):
    n = number(b, g)
    act.wait_ge(at.pv_done, (n * GH + h + 1) * 3)
    if h == 0:
        at_least(act, at.gathered, n * 48)
    act.activation(at.pv_raw[0:at.vcols, h, :], at.pv_ps[0:at.vcols, :], ACT.Copy).then_inc(at.pv_copied, 1)


QK_SLOTS = ((4, 7, 10), (0, 4, 8), (2, 5, 9), (0, 4, 8))


def share(count, slots, slot):
    return range(count * slot // slots, count * (slot + 1) // slots)


def attention_layer(nc, x_t, wq_t, wk_t, wv_t, a_qkv, b_qkv, starts, consts, sums_hbm, attn_hbm, ids):
    with ExitStack() as ctx:
        def sb(what, shape, dt=F32):
            return ctx.enter_context(nc.sbuf_tensor(f"a_{what}", shape, dt))

        def sem(what):
            return ctx.enter_context(nc.semaphore(f"a_{what}"))

        at = Attention(nc, ctx, "a", HD, 4)
        lin_ps = ctx.enter_context(nc.psum_tensor("a_lin_ps", [P, 2, SEQ], F32))
        aux_ps = ctx.enter_context(nc.psum_tensor("a_aux_ps", [P, SEQ], F32))

        w_split = [sb(f"w{n}_split", [P, 2, KC, D], F32R) for n in "qkv"]
        x_stage = sb("x_stage", [P, KC, SEQ])
        x_split = sb("x_split", [P, 2, KC, SEQ], F32R)
        a_stage = sb("a_stage", [P, KC, 3 * RANK])
        a_split = sb("a_split", [P, 2, KC, 3 * RANK], F32R)
        b_stage = sb("b_stage", [P, 3 * D * RANK // P])
        b_split = sb("b_split", [P, 2, 3 * D * RANK // P], F32R)
        b_stack = sb("b_stack", [3 * RANK, 3, D], F32R)
        low_split = sb("low_split", [3 * RANK, 2, SEQ], F32R)
        low_stack = sb("low_stack", [3 * RANK, 3, SEQ], F32R)
        rope_in = [sb(f"rope_in{i}", [P, SEQ]) for i in range(2)]
        rope_turned = [sb(f"rope_turned{i}", [P, SEQ]) for i in range(2)]
        rope_out = [sb(f"rope_out{i}", [P, SEQ]) for i in range(2)]
        cos_sin = sb("cos_sin", [P, 2, SEQ])
        rowmask = sb("rowmask", [P, SEQ])
        eye = sb("eye", [P, P], F32R)
        eye_bf = sb("eye_bf", [P, P], BF16)
        colmask = sb("colmask", [P, P], BF16)
        sum_hi = sb("sum_hi", [P, SEQ])
        sum_lo = sb("sum_lo", [P, SEQ])
        sums = sb("sums", [GH * TT, P])
        inverse = sb("inverse", [GH * TT, P])
        inverse_all = sb("inverse_all", [P, SEQ])
        starts_i = sb("starts_i", [1, ADAPTERS], I32)
        starts_f = sb("starts_f", [1, ADAPTERS])
        index = sb("index", [1, BATCH])
        count = sb("count", [1, BATCH])

        const_in = sem("const_in")
        const_ready = sem("const_ready")
        ids_step = sem("ids_step")
        w_in = [sem(f"w{n}_in") for n in "qkv"]
        w_hi = sem("w_hi")
        w_ready = sem("w_ready")
        x_in = sem("x_in")
        x_hi = sem("x_hi")
        x_ready = sem("x_ready")
        ab_in = sem("ab_in")
        ab_hi = sem("ab_hi")
        ab_ready = sem("ab_ready")
        b_stacked = sem("b_stacked")
        low_made = sem("low_made")
        low_hi = sem("low_hi")
        low_ready = sem("low_ready")
        low_stacked = sem("low_stacked")
        lin_ready = [sem(f"lin_ready{i}") for i in range(2)]
        lin_free = [sem(f"lin_free{i}") for i in range(2)]
        turned = [sem(f"turned{i}") for i in range(2)]
        roped = [sem(f"roped{i}") for i in range(2)]
        rope_hi = [sem(f"rope_hi{i}") for i in range(2)]
        value_hi = sem("value_hi")
        inverted = sem("inverted")
        inverse_out = sem("inverse_out")
        inverse_in = sem("inverse_in")
        merged = sem("merged")
        normalised = sem("normalised")
        attn_out = sem("attn_out")

        def qk_use(b, g):
            return b * 6 + (g if g < 2 else g + 2)

        def v_use(b, t):
            return b * 6 + 2 + t // 2

        square = rope_out[0][:, 0:2 * P].rearrange("p (a n) -> p a n", a=2)
        stage = (x_stage, at.pv_raw)

        block = ctx.enter_context(nc.Block())

        @block.sync
        def _(sp):
            sp.dma_start(starts_i[:, :], starts).then_inc(const_in, 16)
            sp.dma_start(index[:, :], consts[0:1, COUNT:COUNT + BATCH]).then_inc(const_in, 16)
            sp.dma_start(cos_sin[:, :, :], consts[:, COS:EYE].rearrange("p (a n) -> p a n", a=2)).then_inc(const_in, 16)
            sp.dma_start(square[:, 0, :], consts[:, EYE:EYE + P]).then_inc(const_in, 16)
            sp.dma_start(square[:, 1, :], consts[:, COLMASK:COLMASK + P]).then_inc(const_in, 16)
            sp.dma_start(rowmask[:, :], consts[:, ROWMASK:ROWMASK + SEQ]).then_inc(const_in, 16)
            for n, w in enumerate((wq_t, wk_t, wv_t)):
                if n == 2:
                    sp.wait_ge(w_ready, 1)
                sp.dma_start(stage[n % 2][:, :, :], w).then_inc(w_in[n], 16)
            sp.wait_ge(ids_step, 2 + ADAPTERS + 1)

            def load(b):
                if isinstance(b, int) and b == 0:
                    sp.wait_ge(w_ready, 3)
                else:
                    apart(sp, at.ones_set, x_ready, b * KC)
                    apart(sp, at.ones_set, ab_ready, b * 2)
                sp.dma_start(x_stage[:, :, :], x_t[:, :, bass.ds(b * SEQ, SEQ)]).then_inc(x_in, 16)
                i = sp.value_load(ids[0:1, bass.ds(b, 1)], min_val=0, max_val=ADAPTERS - 1)
                sp.dma_start(a_stage[:, :, :], a_qkv[bass.ds(i, 1)].rearrange("a p c r -> (a p) c r")).then_inc(ab_in, 16)
                sp.dma_start(b_stage[:, :], b_qkv[bass.ds(i, 1)].rearrange("a p n -> (a p) n")).then_inc(ab_in, 16)

            def send_b(b):
                apart(sp, at.ones_set, lin_ready[1], qk_use(b, 0))
                apart(sp, at.ones_set, ab_ready, b * 2 + 2)
                for r, part in enumerate((0, 1, 0)):
                    sp.dma_start(b_stack[RANK * r:RANK * (r + 1), :, :].bitcast(F32),
                                 b_split[:, part, :].bitcast(F32)).then_inc(b_stacked, 16)

            def send_low(b):
                sp.wait_ge(low_ready, b + 1)
                for r, part in enumerate((0, 0, 1)):
                    sp.dma_start(low_stack[RANK * r:RANK * (r + 1), :, :].bitcast(F32),
                                 low_split[:, part, :].bitcast(F32)).then_inc(low_stacked, 16)

            def gather(b, g):
                n = number(b, g)
                apart(sp, at.ones_set, at.pv_copied, (n + 1) * GH)
                apart(sp, at.ones_set, attn_out, n * 16)
                sp.dma_start(sum_hi[:, :], at.pv_raw[0:HD, :, :]).then_inc(at.gathered, 16)
                sp.dma_start(sum_lo[:, :], at.pv_raw[HD:2 * HD, :, :]).then_inc(at.gathered, 16)
                sp.dma_start(sums[:, :], at.pv_raw[2 * HD:2 * HD + 1, :, :]).then_inc(at.gathered, 16)

            def spread(b, g):
                n = number(b, g)
                sp.wait_ge(inverted, n + 1)
                sp.dma_start(sums_hbm.rearrange("h (c n) -> (h c) n", c=TT), inverse[:, :]).then_inc(inverse_out, 16)
                sp.wait_ge(inverse_out, n * 16 + 16)
                sp.dma_start(inverse_all[:, :], sums_hbm.rearrange("(o h) n -> o h n", o=1).broadcast_to(
                    [HD, GH, SEQ])).then_inc(inverse_in, 16)

            def store(b, g):
                n = number(b, g)
                sp.wait_ge(normalised, n + 1)
                sp.dma_start(attn_hbm[:, g, bass.ds(b * SEQ, SEQ)], sum_lo[:, :]).then_inc(attn_out, 16)

            def step(b, g):
                last = is_last(b)
                if g == 0 and not last:
                    load(b + 1)
                first = isinstance(b, int) and b == 0 and g == 0
                if not first:
                    gather(*group(b, g, -1))
                if g == 1 and not last:
                    send_b(b + 1)
                if g == 2 and not last:
                    send_low(b + 1)
                if not first:
                    spread(*group(b, g, -1))
                    store(*group(b, g, -1))
                if not (last and g == GROUPS - 1):
                    shift_send(sp, at, *group(b, g, 1))
                if not (last and g >= 2):
                    stack_send(sp, at, *group(b, g, 2))

            load(0)
            send_b(0)
            send_low(0)
            stack_send(sp, at, 0, 0)
            stack_send(sp, at, 0, 1)
            shift_send(sp, at, 0, 0)

            def body(b):
                for g in range(GROUPS):
                    step(b, g)

            batches(sp, body)
            gather(BATCH - 1, GROUPS - 1)
            spread(BATCH - 1, GROUPS - 1)
            store(BATCH - 1, GROUPS - 1)
            sp.wait_ge(attn_out, BATCH * GROUPS * 16)

        @block.gpsimd
        def _(pool):
            for i in range(2):
                pool.memset(at.k_stack[i][96:98, :, :].bitcast(F32), 1.0).then_inc(at.ones_set, 1)
                pool.wait_ge(at.ones_set, i + 1)
            pool.memset(at.value[:, :, :, 2 * HD:2 * HD + 1].bitcast(F32), 1.0).then_inc(at.ones_set, 1)
            pool.wait_ge(const_in, 96)

            def rope(b, g, i):
                n = number(b, g)
                pool.wait_ge(turned[i], n + 1)
                at_least(pool, at.k_ready if i else at.q_ready, n)
                pool.tensor_tensor(rope_out[i][:, :], rope_in[i][:, :], cos_sin[:, 0, :], ALU.mult).then_inc(roped[i], 1)
                pool.tensor_tensor(rope_turned[i][:, :], rope_turned[i][:, :], cos_sin[:, 1, :],
                                   ALU.mult).then_inc(roped[i], 1)
                pool.wait_ge(roped[i], n * 3 + 2)
                pool.tensor_tensor(rope_out[i][:, :], rope_out[i][:, :], rope_turned[i][:, :],
                                   ALU.add).then_inc(roped[i], 1)

            def merge(b, g):
                n = number(b, g)
                pool.wait_ge(at.gathered, n * 48 + 48)
                pool.tensor_tensor(sum_hi[:, :], sum_hi[:, :], sum_lo[:, :], ALU.add).then_inc(merged, 1)

            def step(b, g):
                if not (is_last(b) and g >= 2):
                    rope(*group(b, g, 2), 0)
                if not (isinstance(b, int) and b == 0 and g == 0):
                    merge(*group(b, g, -1))
                if not (is_last(b) and g >= 2):
                    rope(*group(b, g, 2), 1)

            for g in range(2):
                rope(0, g, 0)
                rope(0, g, 1)

            def body(b):
                for g in range(GROUPS):
                    step(b, g)

            batches(pool, body)
            merge(BATCH - 1, GROUPS - 1)

        @block.scalar
        def _(act):
            def weights(n):
                act.wait_ge(w_in[n], 16)
                act.activation(w_split[n][:, 0, :, :], stage[n % 2][:, :, :], ACT.Copy).then_inc(w_hi, 1)

            def x_chunk(b, c):
                if c == 0:
                    act.wait_ge(x_in, b * 16 + 16)
                    at_least(act, lin_ready[1], qk_use(b, 0))
                act.activation(x_split[:, 0, c, :], x_stage[:, c, :], ACT.Copy).then_inc(x_hi, 1)

            def adapter(b):
                act.wait_ge(ab_in, b * 32 + 32)
                act.activation(a_split[:, 0, :, :], a_stage[:, :, :], ACT.Copy).then_inc(ab_hi, 1)
                at_least(act, b_stacked, b * 48)
                act.activation(b_split[:, 0, :], b_stage[:, :], ACT.Copy).then_inc(ab_hi, 1)

            def low(b):
                act.wait_ge(low_made, b + 1)
                at_least(act, low_stacked, b * 48)
                act.activation(low_split[:, 0, :], aux_ps[0:3 * RANK, :], ACT.Copy).then_inc(low_hi, 1)

            def projected(b, g, i):
                act.wait_ge(lin_ready[i], qk_use(b, g) + 1)
                at_least(act, roped[i], number(b, g) * 3)
                act.activation(rope_in[i][:, :], lin_ps[:, i, :], ACT.Copy).then_inc(lin_free[i], 1)

            def rotated_hi(b, g, i):
                n = number(b, g)
                act.wait_ge(roped[i], n * 3 + 3)
                at_least(act, at.stacked[(g + 1) % 2], uses(*group(b, g, -1)) * 96)
                split = at.k_split if i else at.q_split
                act.activation(split[:, 0, :], rope_out[i][:, :], ACT.Copy).then_inc(rope_hi[i], 1)

            def value(b, t):
                act.wait_ge(lin_ready[t % 2], v_use(b, t) + 1)
                if t == 0:
                    at_least(act, at.pv_done, b * GROUPS * UNITS)
                act.activation(at.value[:, t, :, 0:HD], lin_ps[:, t % 2, :].rearrange("p (h d) -> p h d", d=HD),
                               ACT.Copy).then_inc(value_hi, 1)

            def step(b, g):
                last = is_last(b)
                first = isinstance(b, int) and b == 0 and g == 0
                q_from, k_from, k_to = QK_SLOTS[g]
                for slot in range(UNITS):
                    exp_unit(act, at, b, g, slot)
                    if slot == 0 and not first:
                        pv_copy(act, at, *group(b, g, -1), 2)
                    if slot == 3 and not first:
                        pv_copy(act, at, *group(b, g, -1), 3)
                    if slot == 6:
                        pv_copy(act, at, b, g, 0)
                    if slot == 9:
                        pv_copy(act, at, b, g, 1)
                    if g == 0 and 2 <= slot < 5:
                        for t in ((0, 1), (2,), (3,))[slot - 2]:
                            value(b, t)
                    if g == 0 and slot == 9 and not last:
                        adapter(b + 1)
                    if g == 1 and slot >= 8 and not last:
                        x_chunk(b + 1, slot - 8)
                    if g == 2 and slot == 2 and not last:
                        low(b + 1)
                    if not (last and g >= 2):
                        ahead = group(b, g, 2)
                        if slot == k_from:
                            projected(*ahead, 0)
                        if slot == k_from + 3:
                            rotated_hi(*ahead, 0)
                        if slot == k_to:
                            projected(*ahead, 1)
                        if slot == UNITS - 1:
                            rotated_hi(*ahead, 1)
                    if slot == UNITS - 1 and not (last and g == GROUPS - 1):
                        shift_copy(act, at, aux_ps, *group(b, g, 1))

            for n in range(3):
                weights(n)
            adapter(0)
            for c in range(KC):
                x_chunk(0, c)
            low(0)
            for g in range(2):
                for i in range(2):
                    projected(0, g, i)
                    rotated_hi(0, g, i)
            shift_copy(act, at, aux_ps, 0, 0)

            def body(b):
                for g in range(GROUPS):
                    step(b, g)

            batches(act, body)
            pv_copy(act, at, BATCH - 1, GROUPS - 1, 2)
            pv_copy(act, at, BATCH - 1, GROUPS - 1, 3)

        @block.vector
        def _(dve):
            dve.wait_ge(const_in, 96)
            dve.tensor_copy(starts_f[:, :], starts_i[:, :]).then_inc(ids_step, 1)
            dve.memset(count[:, :], -1.0).then_inc(ids_step, 1)
            for i in range(ADAPTERS):
                dve.wait_ge(ids_step, 2 + i)
                dve.scalar_tensor_tensor(out=count[:, :], in0=index[:, :], scalar=starts_f[0:1, i:i + 1],
                                         in1=count[:, :], op0=ALU.is_ge, op1=ALU.add).then_inc(ids_step, 1)
            dve.wait_ge(ids_step, 2 + ADAPTERS)
            dve.tensor_scalar(ids[:, :], count[:, :], 0.0, None, ALU.max).then_inc(ids_step, 1)
            dve.tensor_copy(eye[:, :], square[:, 0, :]).then_inc(const_ready, 1)
            dve.tensor_copy(eye_bf[:, :], square[:, 0, :]).then_inc(const_ready, 1)
            dve.tensor_copy(colmask[:, :], square[:, 1, :]).then_inc(const_ready, 1)

            def weights(n):
                dve.wait_ge(w_hi, n + 1)
                dve.tensor_tensor(w_split[n][:, 1, :, :], stage[n % 2][:, :, :], w_split[n][:, 0, :, :],
                                  ALU.subtract).then_inc(w_ready, 1)

            def x_chunk(b, c):
                dve.wait_ge(x_hi, b * KC + c + 1)
                dve.tensor_tensor(x_split[:, 1, c, :], x_stage[:, c, :], x_split[:, 0, c, :],
                                  ALU.subtract).then_inc(x_ready, 1)

            def adapter(b):
                dve.wait_ge(ab_hi, b * 2 + 2)
                dve.tensor_tensor(a_split[:, 1, :, :], a_stage[:, :, :], a_split[:, 0, :, :],
                                  ALU.subtract).then_inc(ab_ready, 1)
                dve.tensor_tensor(b_split[:, 1, :], b_stage[:, :], b_split[:, 0, :],
                                  ALU.subtract).then_inc(ab_ready, 1)

            def low(b):
                dve.wait_ge(low_hi, b + 1)
                dve.tensor_tensor(low_split[:, 1, :], aux_ps[0:3 * RANK, :], low_split[:, 0, :],
                                  ALU.subtract).then_inc(low_ready, 1)

            def exchange(b, g, i):
                apart(dve, at.ones_set, lin_free[i], number(b, g) + 1)
                apart(dve, at.ones_set, roped[i], number(b, g) * 3)
                dve.stream_shuffle(rope_turned[i][:, :], rope_in[i][:, :],
                                   [p ^ GH for p in range(32)]).then_inc(turned[i], 1)

            def rotated_lo(b, g, i):
                dve.wait_ge(rope_hi[i], number(b, g) + 1)
                split = at.k_split if i else at.q_split
                dve.tensor_tensor(split[:, 1, :], rope_out[i][:, :], split[:, 0, :],
                                  ALU.subtract).then_inc(at.k_ready if i else at.q_ready, 1)

            def value(b, t):
                dve.wait_ge(value_hi, b * TT + t + 1)
                dve.tensor_tensor(at.value[:, t, :, HD:2 * HD], lin_ps[:, t % 2, :].rearrange("p (h d) -> p h d", d=HD),
                                  at.value[:, t, :, 0:HD],
                                  ALU.subtract).then_inc(at.value_ready, 1)

            def invert(b, g):
                n = number(b, g)
                dve.wait_ge(at.gathered, n * 48 + 48)
                at_least(dve, inverse_out, n * 16)
                dve.reciprocal(inverse[:, :], sums[:, :]).then_inc(inverted, 1)

            def normalise(b, g):
                n = number(b, g)
                dve.wait_ge(merged, n + 1)
                dve.wait_ge(inverse_in, n * 16 + 16)
                dve.tensor_tensor(sum_lo[:, :], sum_hi[:, :], inverse_all[:, :], ALU.mult).then_inc(normalised, 1)

            def step(b, g):
                last = is_last(b)
                first = isinstance(b, int) and b == 0 and g == 0
                q_from, k_from, k_to = QK_SLOTS[g]
                for slot in range(UNITS):
                    lo_unit(dve, at, b, g, slot)
                    if 2 <= slot < 8 and not (last and g == GROUPS - 1):
                        score_max(dve, at, rowmask, *group(b, g, 1), 2 * slot - 4)
                        score_max(dve, at, rowmask, *group(b, g, 1), 2 * slot - 3)
                    if slot == 9 and not (last and g == GROUPS - 1):
                        shift_split(dve, at, *group(b, g, 1))
                    if slot == 6 and not first:
                        invert(*group(b, g, -1))
                    if slot == 10 and not first:
                        normalise(*group(b, g, -1))
                    if g == 0 and 2 <= slot < 5:
                        for t in ((0, 1), (2,), (3,))[slot - 2]:
                            value(b, t)
                    if g == 0 and slot == 9 and not last:
                        adapter(b + 1)
                    if g == 1 and slot >= 8 and not last:
                        x_chunk(b + 1, slot - 8)
                    if g == 2 and slot == 2 and not last:
                        low(b + 1)
                    if not (last and g >= 2):
                        ahead = group(b, g, 2)
                        if slot == k_from:
                            exchange(*ahead, 0)
                        if slot == k_from + 3:
                            rotated_lo(*ahead, 0)
                        if slot == k_to:
                            exchange(*ahead, 1)
                        if slot == UNITS - 1:
                            rotated_lo(*ahead, 1)

            for n in range(3):
                weights(n)
            adapter(0)
            for c in range(KC):
                x_chunk(0, c)
            low(0)
            for g in range(2):
                for i in range(2):
                    exchange(0, g, i)
                    rotated_lo(0, g, i)
            for k in range(UNITS):
                score_max(dve, at, rowmask, 0, 0, k)
            shift_split(dve, at, 0, 0)

            def body(b):
                for g in range(GROUPS):
                    step(b, g)

            batches(dve, body)
            invert(BATCH - 1, GROUPS - 1)
            normalise(BATCH - 1, GROUPS - 1)

        @block.tensor
        def _(pe):
            pe.wait_ge(const_ready, 3)
            pe.wait_ge(at.ones_set, 3)

            def low(b, items):
                for x in items:
                    c, (w, a) = x // 3, PASSES[x % 3]
                    if x == 0:
                        at_least(pe, at.shift_copied, b * GROUPS - 1)
                        pe.wait_ge(x_ready, (b + 1) * KC)
                        pe.wait_ge(ab_ready, (b + 1) * 2)
                    mm = pe.matmul(aux_ps[0:3 * RANK, :], a_split[:, w, c, :], x_split[:, a, c, :],
                                   start=(x == 0), stop=(x == 3 * KC - 1))
                    if x == 3 * KC - 1:
                        mm.then_inc(low_made, 1)

            def project(b, g, i, items):
                for x in items:
                    if x == 0:
                        if g == 2:
                            pe.wait_ge(at.value_ready, b * TT + 3 + i)
                        else:
                            at_least(pe, lin_free[i], number(b, g))
                    if x < 3 * KC:
                        c, (w, a) = x // 3, PASSES[x % 3]
                        pe.matmul(lin_ps[:, i, :], w_split[i][:, w, c, g * P:g * P + P], x_split[:, a, c, :],
                                  start=(x == 0), stop=False)
                    else:
                        pe.wait_ge(low_stacked, b * 48 + 48)
                        pe.wait_ge(b_stacked, b * 48 + 48)
                        pe.matmul(lin_ps[:, i, :], b_stack[:, i, g * P:g * P + P], low_stack[:, i, :],
                                  start=False, stop=True).then_inc(lin_ready[i], 1)

            def project_value(b, t):
                bank = t % 2
                if t < 2:
                    pe.wait_ge(lin_free[bank], b * GROUPS + 2)
                else:
                    pe.wait_ge(at.value_ready, b * TT + t - 1)
                for x in range(3 * KC):
                    c, (w, a) = x // 3, PASSES[x % 3]
                    pe.matmul(lin_ps[:, bank, :], x_split[:, a, c, t * P:t * P + P], w_split[2][:, w, c, :],
                              start=(x == 0), stop=False)
                pe.matmul(lin_ps[:, bank, :], low_stack[:, 2, t * P:t * P + P], b_stack[:, 2, :],
                          start=False, stop=True).then_inc(lin_ready[bank], 1)

            def step(b, g):
                last = is_last(b)
                first = isinstance(b, int) and b == 0 and g == 0
                q_from, k_from, k_to = QK_SLOTS[g]
                for slot in range(UNITS):
                    score_t_unit(pe, at, eye_bf, colmask, b, g, slot)
                    if 2 <= slot < 8 and not (last and g == GROUPS - 1):
                        score_unit(pe, at, *group(b, g, 1), 2 * slot - 4)
                        score_unit(pe, at, *group(b, g, 1), 2 * slot - 3)
                    if slot < 3 and not first:
                        pv_unit(pe, at, *group(b, g, -1), UNITS - 3 + slot)
                    if g == 0 and slot < TT:
                        project_value(b, slot)
                    if g == 2 and slot < 2 and not last:
                        low(b + 1, share(3 * KC, 2, slot))
                    if not (last and g >= 2):
                        ahead = group(b, g, 2)
                        if q_from <= slot < k_from:
                            project(*ahead, 0, share(3 * KC + 1, k_from - q_from, slot - q_from))
                        if k_from <= slot < k_to:
                            project(*ahead, 1, share(3 * KC + 1, k_to - k_from, slot - k_from))
                    if slot >= 3:
                        pv_unit(pe, at, b, g, slot - 3)
                    if slot == 10 and not (last and g == GROUPS - 1):
                        if g == 2 and not last:
                            pe.wait_ge(low_ready, b + 2)
                        shift_turn(pe, at, aux_ps, eye, *group(b, g, 1))

            pe.wait_ge(w_ready, 3)
            low(0, range(3 * KC))
            for g in range(2):
                for i in range(2):
                    project(0, g, i, range(3 * KC + 1))
            for k in range(UNITS):
                score_unit(pe, at, 0, 0, k)
            pe.wait_ge(low_ready, 1)
            shift_turn(pe, at, aux_ps, eye, 0, 0)

            def body(b):
                for g in range(GROUPS):
                    step(b, g)

            batches(pe, body)
            for k in range(UNITS - 3, UNITS):
                pv_unit(pe, at, BATCH - 1, GROUPS - 1, k)


QK_SLOTS_B = ((5, 8, 11), (6, 8, 11), (5, 8, 11), (0, 4, 8))


def rsqrt(dve, step, done, out, x, t):
    dve.tensor_scalar(t.bitcast(I32), x.bitcast(I32), 1, None, ALU.logical_shift_right).then_inc(step, 1)
    dve.wait_ge(step, done + 1)
    dve.tensor_scalar(out.bitcast(I32), t.bitcast(I32), -1.0, RSQRT_MAGIC, ALU.mult, ALU.add).then_inc(step, 1)
    for i in range(3):
        dve.wait_ge(step, done + 2 + 3 * i)
        dve.tensor_tensor(t, out, out, ALU.mult).then_inc(step, 1)
        dve.wait_ge(step, done + 3 + 3 * i)
        dve.scalar_tensor_tensor(out=t, in0=t, scalar=-0.5, in1=x, op0=ALU.mult, op1=ALU.mult).then_inc(step, 1)
        dve.wait_ge(step, done + 4 + 3 * i)
        dve.scalar_tensor_tensor(out=out, in0=t, scalar=1.5, in1=out, op0=ALU.add, op1=ALU.mult).then_inc(step, 1)


RSQRT_STEPS = 11


def gate_layer(nc, x, attn_hbm, wo_t, a_o, b_o, wq_t, wk_t, wv, wo, low_a, ln_w, selector, consts, ids, sums_hbm,
               x1_hbm, h_hbm, z_hbm):
    with ExitStack() as ctx:
        def sb(what, shape, dt=F32):
            return ctx.enter_context(nc.sbuf_tensor(f"b_{what}", shape, dt))

        def sem(what):
            return ctx.enter_context(nc.semaphore(f"b_{what}"))

        at = Attention(nc, ctx, "b", RANK, 3)
        lin_ps = ctx.enter_context(nc.psum_tensor("b_lin_ps", [P, 2, SEQ], F32))
        aux_ps = ctx.enter_context(nc.psum_tensor("b_aux_ps", [P, SEQ], F32))
        VW = HEADS * RANK

        wo_split = sb("wo_split", [P, 2, KC, D], F32R)
        qk_split = [sb(f"w{n}_split", [P, 2, KC, D], F32R) for n in "qk"]
        vw_split = sb("vw_split", [P, 2, KC, VW], F32R)
        low_a_split = sb("low_a_split", [P, 2, KC, RANK], F32R)
        wide = sb("wide", [P, KC, D])
        res = sb("res", [P, TT, D])
        attn_split = sb("attn_split", [P, 2, KC, SEQ], F32R)
        h_split = sb("h_split", [P, 2, KC, SEQ], F32R)
        h_turn = sb("h_turn", [P, 2, KC, P])
        a_stage = sb("a_stage", [P, KC, RANK])
        a_split = sb("a_split", [P, 2, KC, RANK], F32R)
        b_stage = sb("b_stage", [P, D * RANK // P])
        b_split = sb("b_split", [P, 2, D * RANK // P], F32R)
        b_stack = sb("b_stack", [3 * RANK, D], F32R)
        low_split = sb("low_split", [RANK, 2, SEQ], F32R)
        low_stack = sb("low_stack", [3 * RANK, SEQ], F32R)
        rowmask = sb("rowmask", [P, SEQ])
        square = h_turn[:, 0, 0:2, :]
        eye = sb("eye", [P, P], F32R)
        eye_bf = sb("eye_bf", [P, P], BF16)
        colmask = sb("colmask", [P, P], BF16)
        sel = sb("sel", [GH * RANK, RANK])
        lnw = sb("lnw", [P, 2, KC])
        a_full = at.prob[:, 0, 0:KC * RANK].rearrange("p (c r) -> p c r", c=KC)
        wo_a = at.prob[:, 1, 0:TT * GH * RANK].rearrange("p (t r) -> p t r", t=TT)
        stats = sb("stats", [P, TT, 6])
        mean_var = sb("mean_var", [P, TT, 2])
        squares = sb("squares", [P, 2, TT])
        inv_root = sb("inv_root", [P, 2, TT])
        newton = sb("newton", [P, 2, TT])
        sum_hi = sb("sum_hi", [GH * RANK, SEQ])
        sum_lo = sb("sum_lo", [GH * RANK, SEQ])
        sums = sb("sums", [GH * TT, P])
        inverse = sb("inverse", [GH * TT, P])
        out_sum = sb("out_sum", [GH * RANK, SEQ])
        h_low = sb("h_low", [RANK, SEQ])
        mod = at.shift_row[:, :].bitcast(F32)
        z_split = low_split

        const_in = sem("const_in")
        const_ready = sem("const_ready")
        stage_in = [sem(f"stage_in{i}") for i in range(3)]
        w_hi = sem("w_hi")
        w_ready = sem("w_ready")
        zeroed = sem("zeroed")
        wo_a_made = sem("wo_a_made")
        wo_a_copied = sem("wo_a_copied")
        vw_made = sem("vw_made")
        in_done = [sem(f"in_done{i}") for i in range(2)]
        attn_hi = sem("attn_hi")
        attn_ready = sem("attn_ready")
        ab_in = sem("ab_in")
        ab_hi = sem("ab_hi")
        ab_ready = sem("ab_ready")
        b_stacked = sem("b_stacked")
        low_made = sem("low_made")
        low_hi = sem("low_hi")
        low_ready = sem("low_ready")
        low_stacked = sem("low_stacked")
        o_made = sem("o_made")
        o_added = sem("o_added")
        stats_done = sem("stats_done")
        ln_step = sem("ln_step")
        x1_ready = sem("x1_ready")
        x1_out = sem("x1_out")
        h_ready = sem("h_ready")
        h_turned = sem("h_turned")
        h_copied = sem("h_copied")
        h_hi = sem("h_hi")
        h_split_ready = sem("h_split_ready")
        h_out = [sem(f"h_out{i}") for i in range(2)]
        qk_made = [sem(f"{n}_made") for n in "qk"]
        qk_hi = [sem(f"{n}_hi") for n in "qk"]
        v_made = sem("v_made")
        value_hi = sem("value_hi")
        inverted = sem("inverted")
        inverse_out = sem("inverse_out")
        inverse_in = sem("inverse_in")
        merged = sem("merged")
        normalised = sem("normalised")
        added = sem("added")
        mod_made = sem("mod_made")
        mod_done = sem("mod_done")
        h_low_made = sem("h_low_made")
        h_low_copied = sem("h_low_copied")
        z_made = sem("z_made")
        z_hi = sem("z_hi")
        z_ready = sem("z_ready")
        z_out = sem("z_out")

        LN_STEPS = TT + 4 + RSQRT_STEPS
        qk_ready = (at.q_ready, at.k_ready)
        stage = (wide, res, at.pv_raw)

        block = ctx.enter_context(nc.Block())

        @block.sync
        def _(sp):
            sp.dma_start(stage[0][:, :, :], wo).then_inc(stage_in[0], 16)
            sp.dma_start(a_full[:, :, :], low_a).then_inc(const_in, 16)
            sp.dma_start(square[:, 0, :], consts[:, EYE:EYE + P]).then_inc(const_in, 16)
            sp.dma_start(square[:, 1, :], consts[:, COLMASK:COLMASK + P]).then_inc(const_in, 16)
            sp.dma_start(rowmask[:, :], consts[:, ROWMASK:ROWMASK + SEQ]).then_inc(const_in, 16)
            sp.dma_start(lnw[:, :, :], ln_w).then_inc(const_in, 16)
            sp.dma_start(sel[:, :], selector).then_inc(const_in, 16)
            sp.dma_start(stage[1][:, :, :], wv).then_inc(stage_in[1], 16)
            sp.dma_start(stage[2][:, :, :], wo_t).then_inc(stage_in[2], 16)
            sp.wait_ge(wo_a_made, 1)
            sp.dma_start(stage[0][:, :, :], wq_t).then_inc(stage_in[0], 16)
            sp.wait_ge(vw_made, 2)
            sp.dma_start(stage[1][:, :, :], wk_t).then_inc(stage_in[1], 16)

            def load(b):
                if isinstance(b, int) and b == 0:
                    sp.wait_ge(w_ready, 4 * KC + KC)
                else:
                    apart(sp, at.ones_set, h_turned, b * TT)
                    apart(sp, at.ones_set, x1_out, b * 16)
                    apart(sp, at.ones_set, ab_ready, b * 2)
                    apart(sp, at.ones_set, h_ready, b * TT)
                sp.dma_start(wide[:, :, :], attn_hbm[:, :, bass.ds(b * SEQ, SEQ)]).then_inc(in_done[0], 16)
                sp.dma_start(res[:, :, :], x[bass.ds(b * SEQ, SEQ), :].rearrange("(t p) d -> p t d", p=P)).then_inc(
                    in_done[1], 16)
                i = sp.value_load(ids[0:1, bass.ds(b, 1)], min_val=0, max_val=ADAPTERS - 1)
                sp.dma_start(a_stage[:, :, :], a_o[bass.ds(i, 1)].rearrange("a p c r -> (a p) c r")).then_inc(ab_in, 16)
                sp.dma_start(b_stage[:, :], b_o[bass.ds(i, 1)].rearrange("a p n -> (a p) n")).then_inc(ab_in, 16)

            def send_b(b):
                apart(sp, at.ones_set, o_made, b * TT)
                apart(sp, at.ones_set, ab_ready, b * 2 + 2)
                for r, part in enumerate((0, 1, 0)):
                    sp.dma_start(b_stack[RANK * r:RANK * (r + 1), :].bitcast(F32),
                                 b_split[:, part, :].bitcast(F32)).then_inc(b_stacked, 16)

            def send_low(b):
                sp.wait_ge(low_ready, b + 1)
                for r, part in enumerate((0, 0, 1)):
                    sp.dma_start(low_stack[RANK * r:RANK * (r + 1), :].bitcast(F32),
                                 low_split[:, part, :].bitcast(F32)).then_inc(low_stacked, 16)

            def gather(b, g):
                n = number(b, g)
                apart(sp, at.ones_set, at.pv_copied, (n + 1) * GH)
                apart(sp, at.ones_set, added, n)
                sp.dma_start(sum_hi[:, :], at.pv_raw[0:RANK, :, :]).then_inc(at.gathered, 16)
                sp.dma_start(sum_lo[:, :], at.pv_raw[RANK:2 * RANK, :, :]).then_inc(at.gathered, 16)
                sp.dma_start(sums[:, :], at.pv_raw[2 * RANK:2 * RANK + 1, :, :]).then_inc(at.gathered, 16)

            def spread(b, g):
                n = number(b, g)
                sp.wait_ge(inverted, n + 1)
                sp.dma_start(sums_hbm.rearrange("h (c n) -> (h c) n", c=TT), inverse[:, :]).then_inc(inverse_out, 16)
                sp.wait_ge(inverse_out, n * 16 + 16)
                sp.wait_ge(merged, n + 1)
                sp.dma_start(sum_lo[:, :], sums_hbm.rearrange("(o h) n -> o h n", o=1).broadcast_to(
                    [RANK, GH, SEQ])).then_inc(inverse_in, 16)

            def store_x1(b):
                sp.wait_ge(x1_ready, b * TT + TT)
                sp.dma_start(x1_hbm[bass.ds(b * SEQ, SEQ), :].rearrange("(t p) d -> p t d", p=P),
                             res[:, :, :]).then_inc(x1_out, 16)

            def store_h(b, t):
                sp.wait_ge(h_copied, b * TT + t + 1)
                sp.dma_start(h_hbm[:, :, bass.ds(b * SEQ + t * P, P)], h_turn[:, t % 2, :, :]).then_inc(h_out[t % 2], 16)

            def store_z(b):
                sp.wait_ge(z_ready, b + 1)
                for part in range(2):
                    sp.dma_start(z_hbm[part, :, bass.ds(b * SEQ, SEQ)],
                                 z_split[:, part, :].bitcast(F32)).then_inc(z_out, 16)

            def step(b, g):
                last = is_last(b)
                zero = isinstance(b, int) and b == 0
                first = zero and g == 0
                if g == 0 and not last:
                    load(b + 1)
                if g == 2 and not last:
                    store_h(b + 1, 0)
                    store_h(b + 1, 1)
                if not first:
                    gather(*group(b, g, -1))
                if g == 0 and not last:
                    send_b(b + 1)
                if g == 2 and not last:
                    store_h(b + 1, 2)
                    store_h(b + 1, 3)
                if not first:
                    spread(*group(b, g, -1))
                if g == 0 and not last:
                    send_low(b + 1)
                if g == 1 and not zero:
                    store_z(b - 1)
                if g == 1 and not last:
                    store_x1(b + 1)
                if not (last and g == GROUPS - 1):
                    shift_send(sp, at, *group(b, g, 1))
                if not (last and g >= 2):
                    stack_send(sp, at, *group(b, g, 2))

            load(0)
            send_b(0)
            send_low(0)
            store_x1(0)
            for t in range(TT):
                store_h(0, t)
            stack_send(sp, at, 0, 0)
            stack_send(sp, at, 0, 1)
            shift_send(sp, at, 0, 0)

            def body(b):
                for g in range(GROUPS):
                    step(b, g)

            batches(sp, body)
            gather(BATCH - 1, GROUPS - 1)
            spread(BATCH - 1, GROUPS - 1)
            store_z(BATCH - 1)
            sp.wait_ge(z_out, BATCH * 32)
            sp.wait_ge(x1_out, BATCH * 16)
            for i in range(2):
                sp.wait_ge(h_out[i], BATCH * TT // 2 * 16)

        @block.gpsimd
        def _(pool):
            for i in range(2):
                pool.memset(at.k_stack[i][96:98, :, :].bitcast(F32), 1.0).then_inc(at.ones_set, 1)
                pool.wait_ge(at.ones_set, i + 1)
            pool.memset(at.value[:, :, :, 2 * RANK:2 * RANK + 1].bitcast(F32), 1.0).then_inc(at.ones_set, 1)
            pool.memset(wo_a[:, :, :], 0.0).then_inc(zeroed, 1)

            def merge(b, g):
                n = number(b, g)
                apart(pool, at.ones_set, at.gathered, n * 48 + 48)
                pool.tensor_tensor(sum_hi[:, :], sum_hi[:, :], sum_lo[:, :], ALU.add).then_inc(merged, 1)
                apart(pool, at.ones_set, normalised, n + 1)
                if g == 0:
                    apart(pool, at.ones_set, mod_made, b)
                    pool.tensor_copy(out_sum[:, :], sum_hi[:, :]).then_inc(added, 1)
                else:
                    apart(pool, at.ones_set, added, n)
                    pool.tensor_tensor(out_sum[:, :], out_sum[:, :], sum_hi[:, :], ALU.add).then_inc(added, 1)

            def body(b):
                for g in range(GROUPS):
                    if not (isinstance(b, int) and b == 0 and g == 0):
                        merge(*group(b, g, -1))

            batches(pool, body)
            merge(BATCH - 1, GROUPS - 1)

        @block.scalar
        def _(act):
            act.wait_ge(const_in, 96)
            act.wait_ge(stage_in[2], 16)
            for c in range(KC):
                act.activation(wo_split[:, 0, c, :], stage[2][:, c, :], ACT.Copy).then_inc(w_hi, 1)
            for c in range(KC):
                act.activation(low_a_split[:, 0, c, :], a_full[:, c, :], ACT.Copy,
                               scale=lnw[:, 1, c:c + 1]).then_inc(w_hi, 1)
            act.wait_ge(vw_made, 2)
            for c in range(KC):
                act.activation(vw_split[:, 0, c, :], lin_ps[:, c // 2, (c % 2) * VW:(c % 2 + 1) * VW], ACT.Copy,
                               scale=lnw[:, 0, c:c + 1]).then_inc(w_hi, 1)
            for n in range(2):
                act.wait_ge(stage_in[n], 32)
                for c in range(KC):
                    act.activation(qk_split[n][:, 0, c, :], stage[n][:, c, :], ACT.Copy,
                                   scale=lnw[:, 0, c:c + 1]).then_inc(w_hi, 1)

            def attn_chunk(b, c):
                if c == 0:
                    act.wait_ge(in_done[0], b * 16 + 16)
                    at_least(act, o_made, b * TT)
                act.activation(attn_split[:, 0, c, :], wide[:, c, :], ACT.Copy).then_inc(attn_hi, 1)

            def adapter(b):
                act.wait_ge(ab_in, b * 32 + 32)
                act.activation(a_split[:, 0, :, :], a_stage[:, :, :], ACT.Copy).then_inc(ab_hi, 1)
                at_least(act, b_stacked, b * 48)
                act.activation(b_split[:, 0, :], b_stage[:, :], ACT.Copy).then_inc(ab_hi, 1)

            def low(b):
                act.wait_ge(low_made, b + 1)
                at_least(act, z_out, (b - 2) * 32)
                act.activation(low_split[:, 0, :], aux_ps[0:RANK, :], ACT.Copy).then_inc(low_hi, 1)

            def h_tile(b, t):
                act.wait_ge(h_turned, b * TT + t + 1)
                at_least(act, h_out[t % 2], (b * 2 + t // 2) * 16)
                bank = lin_ps[:, t % 2, :].rearrange("p (c n) -> p c n", c=KC)
                act.activation(h_turn[:, t % 2, :, :], bank, ACT.Copy).then_inc(h_copied, 1)
                act.activation(h_split[:, 0, :, t * P:t * P + P], bank, ACT.Copy).then_inc(h_hi, 1)

            def projected(b, g, i):
                n = number(b, g)
                act.wait_ge(qk_made[i], n + 1)
                at_least(act, at.stacked[(g + 1) % 2], uses(*group(b, g, -1)) * 96)
                split = at.k_split if i else at.q_split
                act.activation(split[:, 0, :], lin_ps[:, i, :], ACT.Copy).then_inc(qk_hi[i], 1)

            def value(b, t):
                act.wait_ge(v_made, b * TT + t + 1)
                if t == 0:
                    at_least(act, at.pv_done, b * GROUPS * UNITS)
                act.activation(at.value[:, t, :, 0:RANK], lin_ps[:, t % 2, 0:VW].rearrange("p (h d) -> p h d", d=RANK),
                               ACT.Copy).then_inc(value_hi, 1)

            def tanh(b):
                act.wait_ge(mod_made, b + 1)
                act.wait_ge(at.shifted, min(number(b, 6), BATCH * GROUPS) * 32 if isinstance(b, int) else
                            b * GROUPS * 32 + 192)
                act.activation(mod[:, :], aux_ps[0:RANK, :], ACT.Tanh).then_inc(mod_done, 1)

            def z_part(b):
                act.wait_ge(z_made, b + 1)
                act.wait_ge(low_stacked, min(b + 3, BATCH) * 48 if isinstance(b, int) else b * 48 + 144)
                act.activation(z_split[:, 0, :], mod[:, :], ACT.Copy).then_inc(z_hi, 1)

            def h_times_a(b):
                act.wait_ge(h_low_made, b + 1)
                at_least(act, z_made, b)
                act.activation(h_low[:, :], aux_ps[0:RANK, :], ACT.Copy).then_inc(h_low_copied, 1)

            def step(b, g):
                last = is_last(b)
                zero = isinstance(b, int) and b == 0
                first = zero and g == 0
                q_from, k_from, k_to = QK_SLOTS_B[g]
                for slot in range(UNITS):
                    if slot == 0 and not first:
                        pv_copy(act, at, *group(b, g, -1), 2)
                    if slot == 3 and not first:
                        pv_copy(act, at, *group(b, g, -1), 3)
                    if slot == 6:
                        pv_copy(act, at, b, g, 0)
                    if slot == 9:
                        pv_copy(act, at, b, g, 1)
                    exp_unit(act, at, b, g, slot)
                    if g == 0 and 2 <= slot < 5:
                        for t in ((0, 1), (2,), (3,))[slot - 2]:
                            value(b, t)
                    if g == 0 and not last:
                        if 3 <= slot < 7:
                            attn_chunk(b + 1, slot - 3)
                        if slot == 6:
                            adapter(b + 1)
                        if slot == 9:
                            low(b + 1)
                    if g == 1 and not zero:
                        if slot == 3:
                            tanh(b - 1)
                        if slot == 5:
                            z_part(b - 1)
                    if g == 1 and slot == 9:
                        h_times_a(b)
                    if g == 2 and 1 <= slot < 5 and not last:
                        h_tile(b + 1, slot - 1)
                    if not (last and g >= 2):
                        if slot == k_from:
                            projected(*group(b, g, 2), 0)
                        if slot == k_to:
                            projected(*group(b, g, 2), 1)
                    if slot == UNITS - 1 and not (last and g == GROUPS - 1):
                        if g == 1 and not zero:
                            act.wait_ge(z_ready, b)
                        shift_copy(act, at, aux_ps, *group(b, g, 1))

            for c in range(KC):
                attn_chunk(0, c)
            adapter(0)
            low(0)
            for t in range(TT):
                h_tile(0, t)
            for g in range(2):
                for i in range(2):
                    projected(0, g, i)
            shift_copy(act, at, aux_ps, 0, 0)

            def body(b):
                for g in range(GROUPS):
                    step(b, g)

            batches(act, body)
            pv_copy(act, at, BATCH - 1, GROUPS - 1, 2)
            pv_copy(act, at, BATCH - 1, GROUPS - 1, 3)
            tanh(BATCH - 1)
            z_part(BATCH - 1)

        @block.vector
        def _(dve):
            dve.wait_ge(const_in, 96)
            dve.tensor_copy(eye[:, :], square[:, 0, :]).then_inc(const_ready, 1)
            dve.tensor_copy(eye_bf[:, :], square[:, 0, :]).then_inc(const_ready, 1)
            dve.tensor_copy(colmask[:, :], square[:, 1, :]).then_inc(const_ready, 1)

            dve.wait_ge(wo_a_made, 1)
            dve.wait_ge(zeroed, 1)
            for h in range(GH):
                rows = slice(h * HD, h * HD + HD)
                dve.tensor_copy(wo_a[rows, :, h * RANK:(h + 1) * RANK],
                                aux_ps[rows, 0:TT * RANK].rearrange("p (t r) -> p t r", t=TT)).then_inc(wo_a_copied, 1)
            for c in range(KC):
                dve.wait_ge(w_hi, c + 1)
                dve.tensor_tensor(wo_split[:, 1, c, :], stage[2][:, c, :], wo_split[:, 0, c, :],
                                  ALU.subtract).then_inc(w_ready, 1)
            for c in range(KC):
                dve.wait_ge(w_hi, KC + c + 1)
                dve.scalar_tensor_tensor(out=low_a_split[:, 1, c, :], in0=a_full[:, c, :], scalar=lnw[:, 1, c:c + 1],
                                         in1=low_a_split[:, 0, c, :], op0=ALU.mult,
                                         op1=ALU.subtract).then_inc(w_ready, 1)
            for c in range(KC):
                dve.wait_ge(w_hi, 2 * KC + c // 2 * 2 + 2)
                dve.scalar_tensor_tensor(out=vw_split[:, 1, c, :], in0=lin_ps[:, c // 2, (c % 2) * VW:(c % 2 + 1) * VW],
                                         scalar=lnw[:, 0, c:c + 1], in1=vw_split[:, 0, c, :], op0=ALU.mult,
                                         op1=ALU.subtract).then_inc(w_ready, 1)
            for n in range(2):
                for c in range(KC):
                    dve.wait_ge(w_hi, (3 + n) * KC + c + 1)
                    dve.scalar_tensor_tensor(out=qk_split[n][:, 1, c, :], in0=stage[n][:, c, :],
                                             scalar=lnw[:, 0, c:c + 1], in1=qk_split[n][:, 0, c, :], op0=ALU.mult,
                                             op1=ALU.subtract).then_inc(w_ready, 1)

            def attn_chunk(b, c):
                dve.wait_ge(attn_hi, b * KC + c + 1)
                dve.tensor_tensor(attn_split[:, 1, c, :], wide[:, c, :], attn_split[:, 0, c, :],
                                  ALU.subtract).then_inc(attn_ready, 1)

            def adapter(b):
                dve.wait_ge(ab_hi, b * 2 + 2)
                dve.tensor_tensor(a_split[:, 1, :, :], a_stage[:, :, :], a_split[:, 0, :, :],
                                  ALU.subtract).then_inc(ab_ready, 1)
                dve.tensor_tensor(b_split[:, 1, :], b_stage[:, :], b_split[:, 0, :],
                                  ALU.subtract).then_inc(ab_ready, 1)

            def low(b):
                dve.wait_ge(low_hi, b + 1)
                dve.tensor_tensor(low_split[:, 1, :], aux_ps[0:RANK, :], low_split[:, 0, :],
                                  ALU.subtract).then_inc(low_ready, 1)

            def add_residual(b, t):
                dve.wait_ge(o_made, b * TT + t + 1)
                dve.wait_ge(in_done[1], b * 16 + 16)
                dve.tensor_tensor(res[:, t, :], lin_ps[:, t % 2, :], res[:, t, :], ALU.add).then_inc(o_added, 1)
                dve.wait_ge(o_added, b * TT + t + 1)
                dve.bn_stats(stats[:, t, :], res[:, t, :]).then_inc(stats_done, 1)

            def norm_factors(b):
                done = b * LN_STEPS
                apart(dve, at.ones_set, stats_done, (b + 1) * TT)
                for t in range(TT):
                    dve.bn_aggr(mean_var[:, t, :], stats[:, t, :]).then_inc(ln_step, 1)
                dve.wait_ge(ln_step, done + TT)
                dve.tensor_scalar(squares[:, 0, :], mean_var[:, :, 1], LN_EPS, None, ALU.add).then_inc(ln_step, 1)
                dve.wait_ge(ln_step, done + TT + 1)
                dve.reciprocal(newton[:, 0, :], squares[:, 0, :]).then_inc(ln_step, 1)
                dve.wait_ge(ln_step, done + TT + 2)
                dve.tensor_tensor(newton[:, 1, :], newton[:, 0, :], mean_var[:, :, 1], ALU.mult).then_inc(ln_step, 1)
                dve.wait_ge(ln_step, done + TT + 3)
                dve.tensor_scalar(squares[:, 1, :], newton[:, 1, :], RMS_EPS, None, ALU.add).then_inc(ln_step, 1)
                dve.wait_ge(ln_step, done + TT + 4)
                rsqrt(dve, ln_step, done + TT + 4, inv_root[:, :, :], squares[:, :, :], newton[:, :, :])

            def normalise_tile(b, t):
                dve.wait_ge(ln_step, b * LN_STEPS + TT + 4 + RSQRT_STEPS)
                dve.tensor_scalar(res[:, t, :], res[:, t, :], mean_var[:, t, 0:1], inv_root[:, 0, t:t + 1],
                                  ALU.subtract, ALU.mult).then_inc(x1_ready, 1)
                if t == 0:
                    dve.wait_ge(attn_ready, (b + 1) * KC)
                dve.wait_ge(x1_ready, b * TT + t + 1)
                dve.tensor_scalar(wide[:, t, :], res[:, t, :], inv_root[:, 1, t:t + 1], None,
                                  ALU.mult).then_inc(h_ready, 1)

            def h_tile(b, t):
                dve.wait_ge(h_hi, b * TT + t + 1)
                dve.tensor_tensor(h_split[:, 1, :, t * P:t * P + P],
                                  lin_ps[:, t % 2, :].rearrange("p (c n) -> p c n", c=KC),
                                  h_split[:, 0, :, t * P:t * P + P], ALU.subtract).then_inc(h_split_ready, 1)

            def projected(b, g, i):
                dve.wait_ge(qk_hi[i], number(b, g) + 1)
                split = at.k_split if i else at.q_split
                dve.tensor_tensor(split[:, 1, :], lin_ps[:, i, :], split[:, 0, :],
                                  ALU.subtract).then_inc(qk_ready[i], 1)

            def value(b, t):
                dve.wait_ge(value_hi, b * TT + t + 1)
                dve.tensor_tensor(at.value[:, t, :, RANK:2 * RANK],
                                  lin_ps[:, t % 2, 0:VW].rearrange("p (h d) -> p h d", d=RANK),
                                  at.value[:, t, :, 0:RANK], ALU.subtract).then_inc(at.value_ready, 1)

            def invert(b, g):
                n = number(b, g)
                dve.wait_ge(at.gathered, n * 48 + 48)
                at_least(dve, inverse_out, n * 16)
                dve.reciprocal(inverse[:, :], sums[:, :]).then_inc(inverted, 1)

            def normalise(b, g):
                n = number(b, g)
                dve.wait_ge(merged, n + 1)
                dve.wait_ge(inverse_in, n * 16 + 16)
                dve.tensor_tensor(sum_hi[:, :], sum_hi[:, :], sum_lo[:, :], ALU.mult).then_inc(normalised, 1)

            def z_term(b):
                dve.wait_ge(mod_done, b + 1)
                dve.wait_ge(h_low_copied, b + 1)
                dve.scalar_tensor_tensor(out=mod[:, :], in0=mod[:, :], scalar=MOD_SCALE, in1=h_low[:, :],
                                         op0=ALU.mult, op1=ALU.mult).then_inc(z_made, 1)

            def z_part(b):
                dve.wait_ge(z_hi, b + 1)
                dve.tensor_tensor(z_split[:, 1, :], mod[:, :], z_split[:, 0, :], ALU.subtract).then_inc(z_ready, 1)

            def step(b, g):
                last = is_last(b)
                zero = isinstance(b, int) and b == 0
                first = zero and g == 0
                q_from, k_from, k_to = QK_SLOTS_B[g]
                for slot in range(UNITS):
                    lo_unit(dve, at, b, g, slot)
                    if 2 <= slot < 8 and not (last and g == GROUPS - 1):
                        score_max(dve, at, rowmask, *group(b, g, 1), 2 * slot - 4)
                        score_max(dve, at, rowmask, *group(b, g, 1), 2 * slot - 3)
                    if slot == 9 and not (last and g == GROUPS - 1):
                        shift_split(dve, at, *group(b, g, 1))
                    if slot == 6 and not first:
                        invert(*group(b, g, -1))
                    if slot == 10 and not first:
                        normalise(*group(b, g, -1))
                    if g == 0 and 2 <= slot < 5:
                        for t in ((0, 1), (2,), (3,))[slot - 2]:
                            value(b, t)
                    if g == 0 and not last:
                        if 3 <= slot < 7:
                            attn_chunk(b + 1, slot - 3)
                        if slot == 6:
                            adapter(b + 1)
                        if slot == 9:
                            low(b + 1)
                    if g == 1 and not zero:
                        if slot == 4:
                            z_term(b - 1)
                        if slot == 5:
                            z_part(b - 1)
                    if g == 1 and not last:
                        if slot in (2, 3, 5, 6):
                            add_residual(b + 1, (2, 3, 5, 6).index(slot))
                        if slot == 7:
                            norm_factors(b + 1)
                        if slot >= 8:
                            normalise_tile(b + 1, slot - 8)
                    if g == 2 and 1 <= slot < 5 and not last:
                        h_tile(b + 1, slot - 1)
                    if not (last and g >= 2):
                        if slot == k_from:
                            projected(*group(b, g, 2), 0)
                        if slot == k_to:
                            projected(*group(b, g, 2), 1)

            for c in range(KC):
                attn_chunk(0, c)
            adapter(0)
            low(0)
            for t in range(TT):
                add_residual(0, t)
            norm_factors(0)
            for t in range(TT):
                normalise_tile(0, t)
            for t in range(TT):
                h_tile(0, t)
            for g in range(2):
                for i in range(2):
                    projected(0, g, i)
            for k in range(UNITS):
                score_max(dve, at, rowmask, 0, 0, k)
            shift_split(dve, at, 0, 0)

            def body(b):
                for g in range(GROUPS):
                    step(b, g)

            batches(dve, body)
            invert(BATCH - 1, GROUPS - 1)
            normalise(BATCH - 1, GROUPS - 1)
            z_term(BATCH - 1)
            z_part(BATCH - 1)

        @block.tensor
        def _(pe):
            pe.wait_ge(const_in, 96)
            pe.wait_ge(stage_in[0], 16)
            for t in range(TT):
                for c in range(KC):
                    mm = pe.matmul(aux_ps[:, t * RANK:(t + 1) * RANK], stage[0][:, c, t * P:t * P + P], a_full[:, c, :],
                                   start=(t == 0 and c == 0), stop=(c == KC - 1), skip_group_check=True)
            mm.then_inc(wo_a_made, 1)
            pe.wait_ge(wo_a_copied, GH)
            pe.wait_ge(stage_in[1], 16)
            for c in range(KC):
                for t in range(TT):
                    mm = pe.matmul(lin_ps[:, c // 2, (c % 2) * VW + t * GH * RANK:(c % 2) * VW + (t + 1) * GH * RANK],
                                   stage[1][:, t, c * P:c * P + P], wo_a[:, t, :], start=(c % 2 == 0 and t == 0),
                                   stop=True, skip_group_check=True)
                if c % 2 == 1:
                    mm.then_inc(vw_made, 1)
            pe.wait_ge(const_ready, 3)
            pe.wait_ge(at.ones_set, 3)

            def low(b, items):
                for x in items:
                    c, (w, a) = x // 3, PASSES[x % 3]
                    if x == 0:
                        at_least(pe, at.shift_copied, b * GROUPS - 3 if not isinstance(b, int) else
                                 max(0, b * GROUPS - 3))
                        pe.wait_ge(attn_ready, (b + 1) * KC)
                        pe.wait_ge(ab_ready, (b + 1) * 2)
                    mm = pe.matmul(aux_ps[0:RANK, :], a_split[:, w, c, :], attn_split[:, a, c, :],
                                   start=(x == 0), stop=(x == 3 * KC - 1))
                    if x == 3 * KC - 1:
                        mm.then_inc(low_made, 1)

            def project_out(b, items):
                for x in items:
                    t, y = divmod(x, 3 * KC + 1)
                    bank = t % 2
                    if y == 0 and t < 2 and not (isinstance(b, int) and b == 0):
                        pe.wait_ge(qk_ready[bank], b * GROUPS - 1)
                    if y == 0 and t >= 2:
                        pe.wait_ge(o_added, b * TT + t - 1)
                    if y < 3 * KC:
                        c, (w, a) = y // 3, PASSES[y % 3]
                        pe.matmul(lin_ps[:, bank, :], attn_split[:, a, c, t * P:t * P + P], wo_split[:, w, c, :],
                                  start=(y == 0), stop=False)
                    else:
                        pe.wait_ge(low_stacked, b * 48 + 48)
                        pe.wait_ge(b_stacked, b * 48 + 48)
                        pe.matmul(lin_ps[:, bank, :], low_stack[:, t * P:t * P + P], b_stack[:, :],
                                  start=False, stop=True).then_inc(o_made, 1)

            def turn_h(b, t):
                bank = t % 2
                pe.wait_ge(h_ready, b * TT + t + 1)
                if t >= 2:
                    pe.wait_ge(h_split_ready, b * TT + t - 1)
                elif isinstance(b, int) and b == 0:
                    pe.wait_ge(o_added, 3 + t)
                else:
                    pe.wait_ge(qk_ready[bank], b * GROUPS)
                for c in range(KC):
                    mm = pe.transpose(lin_ps[:, bank, c * P:c * P + P], wide[:, t, c * P:c * P + P], eye[:, :].bitcast(F32))
                mm.then_inc(h_turned, 1)

            def project(b, g, i, items):
                for x in items:
                    if x == 0:
                        if g == 0:
                            pe.wait_ge(h_split_ready, (b + 1) * TT)
                        elif g == 2:
                            pe.wait_ge(at.value_ready, b * TT + 3 + i)
                        elif g == 3 and not is_last(b):
                            pe.wait_ge(o_added, (b + 1) * TT + 3 + i)
                        else:
                            pe.wait_ge(qk_ready[i], number(b, g))
                    c, (w, a) = x // 3, PASSES[x % 3]
                    mm = pe.matmul(lin_ps[:, i, :], qk_split[i][:, w, c, g * P:g * P + P], h_split[:, a, c, :],
                                   start=(x == 0), stop=(x == 3 * KC - 1))
                    if x == 3 * KC - 1:
                        mm.then_inc(qk_made[i], 1)

            def project_value(b, t):
                bank = t % 2
                if t < 2:
                    pe.wait_ge(qk_ready[bank], b * GROUPS + 2)
                else:
                    pe.wait_ge(at.value_ready, b * TT + t - 1)
                for x in range(3 * KC):
                    c, (w, a) = x // 3, PASSES[x % 3]
                    mm = pe.matmul(lin_ps[:, bank, 0:VW], h_split[:, a, c, t * P:t * P + P], vw_split[:, w, c, :],
                                   start=(x == 0), stop=(x == 3 * KC - 1))
                mm.then_inc(v_made, 1)

            def h_times_a(b):
                if isinstance(b, int) and b == 0:
                    pe.wait_ge(at.shift_copied, 2)
                else:
                    pe.wait_ge(mod_done, b)
                for x in range(3 * KC):
                    c, (w, a) = x // 3, PASSES[x % 3]
                    mm = pe.matmul(aux_ps[0:RANK, :], low_a_split[:, w, c, :], h_split[:, a, c, :],
                                   start=(x == 0), stop=(x == 3 * KC - 1))
                mm.then_inc(h_low_made, 1)

            def modulation(b):
                apart(pe, at.ones_set, added, (b + 1) * GROUPS)
                if not is_last(b):
                    apart(pe, at.ones_set, at.shift_copied, b * GROUPS + GROUPS + 2)
                pe.matmul(aux_ps[0:RANK, :], sel[:, :], out_sum[:, :], start=True, stop=True).then_inc(mod_made, 1)

            def step(b, g):
                last = is_last(b)
                zero = isinstance(b, int) and b == 0
                first = zero and g == 0
                q_from, k_from, k_to = QK_SLOTS_B[g]
                for slot in range(UNITS):
                    score_t_unit(pe, at, eye_bf, colmask, b, g, slot)
                    if 2 <= slot < 8 and not (last and g == GROUPS - 1):
                        score_unit(pe, at, *group(b, g, 1), 2 * slot - 4)
                        score_unit(pe, at, *group(b, g, 1), 2 * slot - 3)
                    if slot < 3 and not first:
                        pv_unit(pe, at, *group(b, g, -1), UNITS - 3 + slot)
                    if g == 0 and slot < TT:
                        project_value(b, slot)
                    if g == 0 and slot in (7, 8) and not last:
                        low(b + 1, share(3 * KC, 2, slot - 7))
                    if g == 1 and slot == 2 and not zero:
                        modulation(b - 1)
                    if g == 1 and slot < 6 and not last:
                        project_out(b + 1, share(TT * (3 * KC + 1), 6, slot))
                    if g == 1 and slot == 8:
                        h_times_a(b)
                    if g == 2 and slot < TT and not last:
                        turn_h(b + 1, slot)
                    if not (last and g >= 2):
                        ahead = group(b, g, 2)
                        if q_from <= slot < k_from:
                            project(*ahead, 0, share(3 * KC, k_from - q_from, slot - q_from))
                        if k_from <= slot < k_to:
                            project(*ahead, 1, share(3 * KC, k_to - k_from, slot - k_from))
                    if slot >= 3:
                        pv_unit(pe, at, b, g, slot - 3)
                    if slot == 10 and not (last and g == GROUPS - 1):
                        if g == 0 and not last:
                            pe.wait_ge(low_ready, b + 2)
                        if g == 1:
                            pe.wait_ge(h_low_copied, b + 1)
                        shift_turn(pe, at, aux_ps, eye, *group(b, g, 1))

            pe.wait_ge(w_ready, 5 * KC)
            low(0, range(3 * KC))
            project_out(0, range(TT * (3 * KC + 1)))
            for t in range(TT):
                turn_h(0, t)
            for g in range(2):
                for i in range(2):
                    project(0, g, i, range(3 * KC))
            for k in range(UNITS):
                score_unit(pe, at, 0, 0, k)
            pe.wait_ge(low_ready, 1)
            shift_turn(pe, at, aux_ps, eye, 0, 0)

            def body(b):
                for g in range(GROUPS):
                    step(b, g)

            batches(pe, body)
            for k in range(UNITS - 3, UNITS):
                pv_unit(pe, at, BATCH - 1, GROUPS - 1, k)
            modulation(BATCH - 1)


FT = F // 2 // P
W_COLS = 2 * KC * P + D


class Run:

    def __init__(self, n, pair, used):
        self.n, self.pair, self.used = n, pair, used

    def next(self):
        return Run(self.n + 1, 1 - self.pair, self.used + self.pair)

    def former(self):
        return Run(self.n - 1, 1 - self.pair, self.used + self.pair - 1)

    def is_(self, n):
        return isinstance(self.n, int) and self.n == n


def runs(eng, body):
    for second in range(2):
        first = second * BATCH
        body(Run(first, 0, first // 2), second)
        with eng.Fori(0, BATCH // 2 - 1) as i:
            body(Run(i * 2 + (first + 1), 1, i + first // 2), second)
            body(Run(i * 2 + (first + 2), 0, i + (first // 2 + 1)), second)
        body(Run(first + BATCH - 1, 1, (first + BATCH) // 2 - 1), second)


def mlp_layer(nc, mlp_w, low_b, ln_w, x1_hbm, h_hbm, z_hbm, out):
    with ExitStack() as ctx:
        def sb(what, shape, dt=F32):
            return ctx.enter_context(nc.sbuf_tensor(f"c_{what}", shape, dt))

        def sem(what):
            return ctx.enter_context(nc.semaphore(f"c_{what}"))

        gate_ps = ctx.enter_context(nc.psum_tensor("c_gate_ps", [P, 2, SEQ], F32))
        up_ps = ctx.enter_context(nc.psum_tensor("c_up_ps", [P, 2, SEQ], F32))
        down_ps = ctx.enter_context(nc.psum_tensor("c_down_ps", [P, TT, D], F32))

        w_split = sb("w_split", [P, 2, FT, W_COLS], F32R)
        w_stage = sb("w_stage", [P, 2, W_COLS])
        lnw = sb("lnw", [P, 2, KC])
        low_b_stage = sb("low_b_stage", [P, RANK * F // P])
        low_b_split = sb("low_b_split", [P, 2, RANK * F // P], F32R)
        low_b_stack = sb("low_b_stack", [3 * RANK, F], F32R)
        z_stack = [sb(f"z_stack{i}", [3 * RANK, SEQ], F32R) for i in range(2)]
        h_stage = sb("h_stage", [P, KC, SEQ])
        h_split = [sb(f"h_split{i}", [P, 2, KC, SEQ], F32R) for i in range(2)]
        res = [sb(f"res{i}", [P, TT, D]) for i in range(2)]
        gate = sb("gate", [P, 2, SEQ])
        product = sb("product", [P, 2, SEQ])
        product_split = sb("product_split", [P, 2, 2, SEQ], F32R)
        stats = sb("stats", [P, TT, 6])
        mean_var = sb("mean_var", [P, TT, 2])
        var_eps = sb("var_eps", [P, TT])
        inv_root = sb("inv_root", [P, TT])
        newton = sb("newton", [P, TT])

        const_in = sem("const_in")
        b_hi = sem("b_hi")
        b_ready = sem("b_ready")
        b_stacked = sem("b_stacked")
        w_in = [sem(f"w_in{i}") for i in range(2)]
        w_hi = sem("w_hi")
        w_ready = sem("w_ready")
        h_in = sem("h_in")
        h_hi = sem("h_hi")
        h_ready = sem("h_ready")
        z_in = [sem(f"z_in{i}") for i in range(2)]
        res_in = [sem(f"res_in{i}") for i in range(2)]
        res_out = [sem(f"res_out{i}") for i in range(2)]
        gate_made = sem("gate_made")
        up_made = sem("up_made")
        gate_done = sem("gate_done")
        product_done = sem("product_done")
        product_hi = sem("product_hi")
        product_ready = sem("product_ready")
        down_done = sem("down_done")
        res_added = sem("res_added")
        ln_step = sem("ln_step")
        normalised = sem("normalised")

        LN_STEPS = 2 * TT + 1 + RSQRT_STEPS
        RUNS = 2 * BATCH

        block = ctx.enter_context(nc.Block())

        @block.gpsimd
        def _(pool):
            for k in range(2 * FT):
                if k >= 2:
                    pool.wait_ge(w_ready, k - 1)
                pool.dma_start(w_stage[:, k % 2, :], mlp_w[k]).then_inc(w_in[k % 2], 16)

        @block.sync
        def _(sp):
            def load_h(run, rows):
                at_least(sp, h_ready, run.n * KC)
                sp.dma_start(h_stage[:, :, :], h_hbm[:, :, rows]).then_inc(h_in, 16)

            def load_z(run, rows):
                at_least(sp, gate_made, (run.n - 1) * FT)
                for r, part in enumerate((0, 0, 1)):
                    sp.dma_start(z_stack[run.pair][RANK * r:RANK * (r + 1), :].bitcast(F32),
                                 z_hbm[part, :, rows]).then_inc(z_in[run.pair], 16)

            def load_res(run, rows):
                at_least(sp, res_out[run.pair], run.used * 16)
                sp.dma_start(res[run.pair][:, :, :],
                             x1_hbm[rows, :].rearrange("(t p) d -> p t d", p=P)).then_inc(res_in[run.pair], 16)

            def store(run, rows, second):
                if second:
                    sp.wait_ge(normalised, (run.n - BATCH + 1) * TT)
                else:
                    sp.wait_ge(res_added, (run.n + 1) * TT)
                sp.dma_start((out if second else x1_hbm)[rows, :].rearrange("(t p) d -> p t d", p=P),
                             res[run.pair][:, :, :]).then_inc(res_out[run.pair], 16)

            def rows_of(n, second):
                return bass.ds((n - BATCH) * SEQ if second else n * SEQ, SEQ)

            def body(run, second):
                following = run.next()
                next_second = second or run.is_(BATCH - 1)
                if not run.is_(RUNS - 1):
                    load_h(following, rows_of(following.n, next_second))
                    load_z(following, rows_of(following.n, next_second))
                if not run.is_(0):
                    former = run.former()
                    former_second = second and not run.is_(BATCH)
                    store(former, rows_of(former.n, former_second), former_second)
                if not run.is_(RUNS - 1):
                    load_res(following, rows_of(following.n, next_second))

            start = Run(0, 0, 0)
            load_h(start, bass.ds(0, SEQ))
            sp.dma_start(lnw[:, :, :], ln_w).then_inc(const_in, 16)
            sp.dma_start(low_b_stage[:, :], low_b).then_inc(const_in, 16)
            load_z(start, bass.ds(0, SEQ))
            load_res(start, bass.ds(0, SEQ))
            sp.wait_ge(b_ready, 1)
            for r, part in enumerate((0, 1, 0)):
                sp.dma_start(low_b_stack[RANK * r:RANK * (r + 1), :].bitcast(F32),
                             low_b_split[:, part, :].bitcast(F32)).then_inc(b_stacked, 16)
            runs(sp, body)
            end = Run(RUNS - 1, 1, BATCH - 1)
            store(end, rows_of(end.n, True), True)
            for i in range(2):
                sp.wait_ge(res_out[i], BATCH * 16)

        def weight_splits(run, ft):
            if run.is_(0) and ft + 2 < FT:
                return (ft + 2,)
            if run.is_(BATCH - 1) and ft >= 2:
                return (FT + ft - 2,)
            if run.is_(BATCH) and ft < 2:
                return (2 * FT - 2 + ft,)
            return ()

        @block.scalar
        def _(act):
            def weights(k):
                act.wait_ge(w_in[k % 2], (k // 2 + 1) * 16)
                kt = k % FT
                if k >= FT:
                    act.wait_ge(down_done, ((BATCH - 1) * FT + kt + 1) * TT)
                for c in range(KC):
                    cols = slice(c * 2 * P, (c + 1) * 2 * P)
                    act.activation(w_split[:, 0, kt, cols], w_stage[:, k % 2, cols], ACT.Copy, scale=lnw[:, 1, c:c + 1])
                act.activation(w_split[:, 0, kt, 2 * KC * P:], w_stage[:, k % 2, 2 * KC * P:],
                               ACT.Copy).then_inc(w_hi, 1)

            def h_chunk(run, c):
                if c == 0:
                    act.wait_ge(h_in, run.n * 16 + 16)
                    at_least(act, up_made, (run.n - 1) * FT)
                act.activation(h_split[run.pair][:, 0, c, :], h_stage[:, c, :], ACT.Copy).then_inc(h_hi, 1)

            def body(run, second):
                for ft in range(FT):
                    p = run.n * FT + ft
                    bank = ft % 2
                    act.wait_ge(gate_made, p + 1)
                    at_least(act, product_done, p - 1)
                    act.activation(gate[:, bank, :], gate_ps[:, bank, :], ACT.Silu).then_inc(gate_done, 1)
                    act.wait_ge(product_done, p + 1)
                    at_least(act, down_done, (p - 1) * TT)
                    act.activation(product_split[:, bank, 0, :], product[:, bank, :], ACT.Copy).then_inc(product_hi, 1)
                    if 2 <= ft < 2 + KC and not run.is_(RUNS - 1):
                        h_chunk(run.next(), ft - 2)
                    for k in weight_splits(run, ft):
                        weights(k)

            start = Run(0, 0, 0)
            act.wait_ge(const_in, 32)
            weights(0)
            for c in range(KC):
                h_chunk(start, c)
            act.activation(low_b_split[:, 0, :], low_b_stage[:, :], ACT.Copy).then_inc(b_hi, 1)
            weights(1)
            runs(act, body)

        @block.vector
        def _(dve):
            def weights(k):
                dve.wait_ge(w_hi, k + 1)
                kt = k % FT
                for c in range(KC):
                    cols = slice(c * 2 * P, (c + 1) * 2 * P)
                    dve.scalar_tensor_tensor(out=w_split[:, 1, kt, cols], in0=w_stage[:, k % 2, cols],
                                             scalar=lnw[:, 1, c:c + 1], in1=w_split[:, 0, kt, cols], op0=ALU.mult,
                                             op1=ALU.subtract)
                dve.tensor_tensor(w_split[:, 1, kt, 2 * KC * P:], w_stage[:, k % 2, 2 * KC * P:],
                                  w_split[:, 0, kt, 2 * KC * P:], ALU.subtract).then_inc(w_ready, 1)

            def h_chunk(run, c):
                dve.wait_ge(h_hi, run.n * KC + c + 1)
                dve.tensor_tensor(h_split[run.pair][:, 1, c, :], h_stage[:, c, :], h_split[run.pair][:, 0, c, :],
                                  ALU.subtract).then_inc(h_ready, 1)

            def add(run, second):
                dve.wait_ge(res_in[run.pair], run.used * 16 + 16)
                for t in range(TT):
                    dve.wait_ge(down_done, ((run.n + 1) * FT - 1) * TT + t + 1)
                    dve.scalar_tensor_tensor(out=res[run.pair][:, t, :], in0=res[run.pair][:, t, :],
                                             scalar=1.0 if second else 2.0, in1=down_ps[:, t, :], op0=ALU.mult,
                                             op1=ALU.add).then_inc(res_added, 1)

            def norm_factors(run):
                m = run.n - BATCH
                done = m * LN_STEPS
                for t in range(TT):
                    dve.wait_ge(res_added, run.n * TT + t + 1)
                    dve.bn_stats(stats[:, t, :], res[run.pair][:, t, :]).then_inc(ln_step, 1)
                apart(dve, const_in, ln_step, done + TT)
                for t in range(TT):
                    dve.bn_aggr(mean_var[:, t, :], stats[:, t, :]).then_inc(ln_step, 1)
                dve.wait_ge(ln_step, done + 2 * TT)
                dve.tensor_scalar(var_eps[:, :], mean_var[:, :, 1], LN_EPS, None, ALU.add).then_inc(ln_step, 1)
                dve.wait_ge(ln_step, done + 2 * TT + 1)
                rsqrt(dve, ln_step, done + 2 * TT + 1, inv_root[:, :], var_eps[:, :], newton[:, :])

            def normalise(run):
                m = run.n - BATCH
                dve.wait_ge(ln_step, (m + 1) * LN_STEPS)
                for t in range(TT):
                    dve.tensor_scalar(res[run.pair][:, t, :], res[run.pair][:, t, :], mean_var[:, t, 0:1],
                                      inv_root[:, t:t + 1], ALU.subtract, ALU.mult).then_inc(normalised, 1)

            def body(run, second):
                former_second = second and not run.is_(BATCH)
                for ft in range(FT):
                    p = run.n * FT + ft
                    bank = ft % 2
                    if ft == 1 and not run.is_(0):
                        add(run.former(), former_second)
                    dve.wait_ge(gate_done, p + 1)
                    dve.wait_ge(up_made, p + 1)
                    dve.tensor_tensor(product[:, bank, :], up_ps[:, bank, :], gate[:, bank, :],
                                      ALU.mult).then_inc(product_done, 1)
                    dve.wait_ge(product_hi, p + 1)
                    dve.tensor_tensor(product_split[:, bank, 1, :], product[:, bank, :], product_split[:, bank, 0, :],
                                      ALU.subtract).then_inc(product_ready, 1)
                    if former_second and ft == 1:
                        norm_factors(run.former())
                    if former_second and ft == 2:
                        normalise(run.former())
                    if 2 <= ft < 2 + KC and not run.is_(RUNS - 1):
                        h_chunk(run.next(), ft - 2)
                    for k in weight_splits(run, ft):
                        weights(k)

            start = Run(0, 0, 0)
            dve.wait_ge(const_in, 32)
            weights(0)
            for c in range(KC):
                h_chunk(start, c)
            dve.wait_ge(b_hi, 1)
            dve.tensor_tensor(low_b_split[:, 1, :], low_b_stage[:, :], low_b_split[:, 0, :],
                              ALU.subtract).then_inc(b_ready, 1)
            weights(1)
            runs(dve, body)
            end = Run(RUNS - 1, 1, BATCH - 1)
            add(end, True)
            norm_factors(end)
            normalise(end)

        @block.tensor
        def _(pe):
            def down(p, kt, n):
                pe.wait_ge(product_ready, p + 1)
                for t in range(TT):
                    if kt == 0:
                        at_least(pe, res_added, (n - 1) * TT + t + 1)
                    for i, (w, a) in enumerate(PASSES):
                        mm = pe.matmul(down_ps[:, t, :], product_split[:, kt % 2, a, t * P:t * P + P],
                                       w_split[:, w, kt, 2 * KC * P:], start=(kt == 0 and i == 0),
                                       stop=(kt == FT - 1 and i == 2), skip_group_check=True)
                    mm.then_inc(down_done, 1)

            def body(run, second):
                for ft in range(FT):
                    p = run.n * FT + ft
                    bank = ft % 2
                    if ft == 0:
                        pe.wait_ge(h_ready, run.n * KC + KC)
                    if run.is_(0) or run.is_(BATCH):
                        pe.wait_ge(w_ready, second * FT + ft + 1)
                    at_least(pe, gate_done, p - 1)
                    for c in range(KC):
                        for w, a in PASSES:
                            pe.matmul(gate_ps[:, bank, :], w_split[:, w, ft, c * 2 * P:c * 2 * P + P],
                                      h_split[run.pair][:, a, c, :], start=(c == 0 and w == 0 and a == 0), stop=False)
                    if ft == 0:
                        pe.wait_ge(z_in[run.pair], run.used * 48 + 48)
                        if run.is_(0):
                            pe.wait_ge(b_stacked, 48)
                    k = second * FT + ft
                    pe.matmul(gate_ps[:, bank, :], low_b_stack[:, k * P:k * P + P], z_stack[run.pair][:, :],
                              start=False, stop=True).then_inc(gate_made, 1)
                    at_least(pe, product_done, p - 1)
                    for c in range(KC):
                        for w, a in PASSES:
                            mm = pe.matmul(up_ps[:, bank, :], w_split[:, w, ft, c * 2 * P + P:(c + 1) * 2 * P],
                                           h_split[run.pair][:, a, c, :], start=(c == 0 and w == 0 and a == 0),
                                           stop=(c == KC - 1 and (w, a) == PASSES[2]))
                    mm.then_inc(up_made, 1)
                    if ft > 0:
                        down(p - 1, ft - 1, run.n)
                    elif not run.is_(0):
                        down(p - 1, FT - 1, run.n - 1)

            runs(pe, body)
            down(RUNS * FT - 1, FT - 1, RUNS - 1)


def tables():
    inv_freq = np.float32(10000.0) ** (-np.arange(0, HD, 2, dtype=np.float32) / np.float32(HD))
    angle = np.arange(SEQ, dtype=np.float32)[None, :] * inv_freq[:, None].astype(np.float32)
    dim = np.arange(P) // GH
    out = np.zeros((P, CONSTS), np.float32)
    out[:, COS:COS + SEQ] = np.cos(angle)[dim // 2]
    out[:, SIN:SIN + SEQ] = np.sin(angle)[dim // 2] * np.where(dim % 2 == 0, -1.0, 1.0)[:, None]
    out[:, EYE:EYE + P] = np.eye(P)
    out[:, ROWMASK + SEQ - P:ROWMASK + SEQ] = np.triu(np.full((P, P), NEG), 1)
    out[:, COLMASK:COLMASK + P] = np.tril(np.full((P, P), NEG), -1)
    out[:, COUNT:COUNT + 8] = np.arange(8)
    return out


def chunked(w):
    return w.reshape(-1, P, w.shape[1]).transpose(1, 0, 2)


def by_dimension(w):
    return w.reshape(GROUPS, GH, -1, w.shape[1]).transpose(0, 2, 1, 3).reshape(w.shape)


def layout(**t):
    a = {k: np.asarray(v) for k, v in t.items()}
    one = {k[len("L0_attn_"):]: v for k, v in a.items() if k.startswith("L0_attn_")}
    two = {k[len("L0_ffn_"):]: v for k, v in a.items() if k.startswith("L0_ffn_")}
    b_q, b_k = (np.stack([by_dimension(m) for m in one[n]]) for n in ("Bq", "Bk"))
    out = {
        "x_t": chunked(one["x"].reshape(-1, D).T),
        "wq_t": chunked(by_dimension(one["Wq"]).T),
        "wk_t": chunked(by_dimension(one["Wk"]).T),
        "wv_t": chunked(one["Wv"].T),
        "a_qkv": np.stack([one["Aq"], one["Ak"], one["Av"]], 2).transpose(0, 3, 1, 2).reshape(
            ADAPTERS, KC, P, 3 * RANK).transpose(0, 2, 1, 3),
        "b_qkv": np.stack([b_q, b_k, one["Bv"]], 1).transpose(0, 3, 1, 2).reshape(ADAPTERS, P, -1),
        "starts": one["lora_start_indices"].reshape(1, -1),
        "x": one["x"].reshape(-1, D),
        "wo_t": chunked(by_dimension(one["Wo"].T)),
        "a_o": np.stack([chunked(by_dimension(m.T)) for m in one["Ao"]]),
        "b_o": one["Bo"].transpose(0, 2, 1).reshape(ADAPTERS, P, -1),
        "wq2_t": chunked(by_dimension(two["Wq"]).T),
        "wk2_t": chunked(by_dimension(two["Wk"]).T),
        "wv2": chunked(two["Wv"]),
        "wo2": chunked(two["Wo"]),
        "low_a": chunked(two["A"]),
        "mlp_w": np.concatenate([np.stack([chunked(two[n].T).reshape(P, KC, F // P, P) for n in (
            "W_in_base", "W_up_base")], 3).transpose(2, 0, 1, 3, 4).reshape(F // P, P, -1),
            two["W_down"].T.reshape(F // P, P, D)], 2),
        "low_b": two["B"].reshape(P, -1),
        "ln_w": np.stack([two["ln1_w"].reshape(KC, P).T, two["ln2_w"].reshape(KC, P).T], 1),
        "selector": np.repeat(np.eye(RANK, dtype=np.float32), GH, 0),
        "consts": tables(),
    }
    return {k: np.ascontiguousarray(v) for k, v in out.items()}


def build(nc, t, out):
    def scratch(name, shape):
        return nc.dram_tensor(name, shape, F32, kind="Internal").ap()

    sums = scratch("softmax_sums", [GH, SEQ])
    attn = scratch("attention_t", [P, KC, BATCH * SEQ])
    x1 = scratch("x1", [BATCH * SEQ, D])
    h = scratch("h_t", [P, KC, BATCH * SEQ])
    z = scratch("z", [2, RANK, BATCH * SEQ])
    with nc.sbuf_tensor("adapter_ids", [1, BATCH], I32) as ids:
        attention_layer(nc, t["x_t"], t["wq_t"], t["wk_t"], t["wv_t"], t["a_qkv"], t["b_qkv"], t["starts"],
                        t["consts"], sums, attn, ids)
        gate_layer(nc, t["x"], attn, t["wo_t"], t["a_o"], t["b_o"], t["wq2_t"], t["wk2_t"], t["wv2"], t["wo2"],
                   t["low_a"], t["ln_w"], t["selector"], t["consts"], ids, sums, x1, h, z)
        mlp_layer(nc, t["mlp_w"], t["low_b"], t["ln_w"], x1, h, z, out)


def kernel(**inputs):
    import concourse.bacc as bacc
    from concourse.bass_utils import run_bass_kernel_spmd

    arrays = {f"in_{k}": v for k, v in layout(**inputs).items()}
    nc = bacc.Bacc("TRN2", target_bir_lowering=False, num_devices=1)
    t = {k[len("in_"):]: nc.dram_tensor(k, v.shape, mybir.dt.from_np(v.dtype), kind="ExternalInput").ap()
         for k, v in arrays.items()}
    out = nc.dram_tensor("out_0_dram", [BATCH * SEQ, D], F32, kind="ExternalOutput").ap()
    build(nc, t, out)
    r = run_bass_kernel_spmd(nc, [arrays], core_ids=[0])
    return r.results[0]["out_0_dram"].reshape(BATCH, SEQ, D)
```

```python
from contextlib import ExitStack

import numpy as np

import concourse.bass as bass
from concourse import mybir
from concourse.alu_op_type import AluOpType as ALU

F32 = mybir.dt.float32
F32R = mybir.dt.float32r
BF16 = mybir.dt.bfloat16
I32 = mybir.dt.int32
ACT = mybir.ActivationFunctionType

P = 128
BATCH, SEQ, D = 8, 512, 512
HEADS, HD = 16, 32
F = 2048
RANK = 16
ADAPTERS = 4
KC = D // P
TT = SEQ // P
GROUPS, GH = 4, 4
UNITS = 3 * GH
SCALE = float(HD) ** -0.5
NEG = -1.0e30
LN_EPS, RMS_EPS, MOD_SCALE = 1e-5, 1e-6, 0.1
RSQRT_MAGIC = float(0x5F3759DF)

PASSES = ((0, 0), (0, 1), (1, 0))

KEY_MAJOR = (((0, 0, 512),), ((1, 0, 384),), ((2, 0, 256), (3, 256, 128)))
QUERY_MAJOR = (((3, 0, 512),), ((2, 0, 384),), ((1, 0, 256), (0, 256, 128)))
WIDTH = (512, 384, 384)

COS, SIN, EYE, ROWMASK, COLMASK, COUNT = 0, 512, 1024, 1152, 1664, 1792
CONSTS = 1800


def at_least(eng, sem, value):
    if not isinstance(value, int) or value > 0:
        eng.wait_ge(sem, value)


def apart(eng, met, sem, value):
    if isinstance(value, int):
        at_least(eng, sem, value)
    else:
        eng.compute_val(value)
        eng.wait_ge(met, 1)
        eng.wait_ge(sem, value)


def batches(eng, body):
    body(0)
    with eng.Fori(1, BATCH - 1) as b:
        body(b)
    body(BATCH - 1)


def is_last(b):
    return isinstance(b, int) and b == BATCH - 1


class Attention:

    def __init__(self, nc, ctx, name, vd, ring):
        def sb(what, shape, dt=F32):
            return ctx.enter_context(nc.sbuf_tensor(f"{name}_{what}", shape, dt))

        def sem(what):
            return ctx.enter_context(nc.semaphore(f"{name}_{what}"))

        self.ring = ring
        self.vd = vd
        self.vcols = 2 * vd + 1
        self.sum_row = 2 * vd
        self.q_stack = [sb(f"q_stack{i}", [P, GH, SEQ], F32R) for i in range(2)]
        self.k_stack = [sb(f"k_stack{i}", [P, GH, SEQ], F32R) for i in range(2)]
        self.q_split = sb("q_split", [P, 2, SEQ], F32R)
        self.k_split = sb("k_split", [P, 2, SEQ], F32R)
        self.value = sb("value", [P, TT, HEADS, self.vcols], F32R)
        self.prob = sb("prob", [P, 2, SEQ])
        self.prob_hi = sb("prob_hi", [P, ring, SEQ], F32R)
        self.prob_lo = sb("prob_lo", [P, ring, SEQ], F32R)
        self.junk = sb("junk", [P, 2, SEQ], BF16)
        self.rowmax = sb("rowmax", [P, TT, GH])
        self.shift = sb("shift", [P, TT, 2 * GH], F32R)
        self.shift_row = sb("shift_row", [RANK, SEQ], F32R)
        self.pv_raw = sb("pv_raw", [P, GH, SEQ])

        self.scores_ps = ctx.enter_context(nc.psum_tensor(f"{name}_scores_ps", [P, 2, SEQ], F32))
        self.scores_t_ps = ctx.enter_context(nc.psum_tensor(f"{name}_scores_t_ps", [P, 2, SEQ], F32))
        self.pv_ps = ctx.enter_context(nc.psum_tensor(f"{name}_pv_ps", [P, 2, SEQ], F32))

        self.ones_set = sem("ones_set")
        self.q_ready = sem("q_ready")
        self.k_ready = sem("k_ready")
        self.stacked = [sem(f"stacked{i}") for i in range(2)]
        self.score_ready = sem("score_ready")
        self.score_read = sem("score_read")
        self.shift_ready = sem("shift_ready")
        self.shift_turned = sem("shift_turned")
        self.shift_copied = sem("shift_copied")
        self.shifted = sem("shifted")
        self.score_t_ready = sem("score_t_ready")
        self.exp_done = sem("exp_done")
        self.lo_done = sem("lo_done")
        self.pv_done = sem("pv_done")
        self.pv_copied = sem("pv_copied")
        self.shift_hi = sem("shift_hi")
        self.value_ready = sem("value_ready")
        self.gathered = sem("gathered")




def group(b, g, ahead=0):
    return b + (g + ahead) // GROUPS, (g + ahead) % GROUPS


def number(b, g):
    return b * GROUPS + g


def score_unit(pe, at, b, g, k):
    h, j = divmod(k, 3)
    n = number(b, g)
    if k % (UNITS // 2) == 0:
        pe.wait_ge(at.stacked[h // 2], n * 96 + 96)
    if k == 0:
        at_least(pe, at.shift_copied, n)
    at_least(pe, at.score_read, n * UNITS + k - 1)
    q, key = at.q_stack[g % 2], at.k_stack[g % 2]
    for i, (qt, col, width) in enumerate(QUERY_MAJOR[j]):
        mm = pe.matmul(at.scores_ps[:, k % 2, col:col + width], q[0:96, h, qt * P:qt * P + P],
                       key[0:96, h, 0:(qt + 1) * P], start=(i == 0), stop=True, skip_group_check=True)
    mm.then_inc(at.score_ready, 1)


def score_max(dve, at, rowmask, b, g, k):
    h, j = divmod(k, 3)
    n = number(b, g)
    apart(dve, at.ones_set, at.score_ready, n * UNITS + k + 1)
    if k == 0:
        apart(dve, at.ones_set, at.shift_ready, n)
    apart(dve, at.ones_set, at.score_read, n * UNITS + k - 1)
    for qt, col, width in QUERY_MAJOR[j]:
        last = dve.tensor_tensor_reduce(at.junk[:, k % 2, col:col + width], at.scores_ps[:, k % 2, col:col + width],
                                        rowmask[:, SEQ - width:SEQ], 1.0, 4 * NEG, ALU.add, ALU.max,
                                        at.rowmax[:, qt, h:h + 1])
    last.then_inc(at.score_read, 1)


def shift_split(dve, at, b, g):
    n = number(b, g)
    dve.wait_ge(at.score_read, (n + 1) * UNITS)
    at_least(dve, at.shift_turned, n)
    dve.tensor_scalar(at.shift[:, :, 0:GH], at.rowmax[:, :, :], -1.0, None, ALU.mult).then_inc(at.shift_hi, 1)
    dve.wait_ge(at.shift_hi, n + 1)
    dve.scalar_tensor_tensor(out=at.shift[:, :, GH:2 * GH], in0=at.rowmax[:, :, :], scalar=-1.0,
                             in1=at.shift[:, :, 0:GH], op0=ALU.mult,
                             op1=ALU.subtract).then_inc(at.shift_ready, 1)


def shift_turn(pe, at, eye, b, g):
    n = number(b, g)
    pe.wait_ge(at.shift_ready, n + 1)
    for qt in range(TT):
        mm = pe.transpose(at.scores_ps[0:2 * GH, 0, qt * P:qt * P + P].bitcast(F32R), at.shift[:, qt, :], eye[:, :])
    mm.then_inc(at.shift_turned, 1)


def shift_copy(act, at, b, g):
    n = number(b, g)
    act.wait_ge(at.shift_turned, n + 1)
    at_least(act, at.shifted, n * 16)
    act.activation(at.shift_row[0:2 * GH, :], at.scores_ps[0:2 * GH, 0, :].bitcast(F32R),
                   ACT.Copy).then_inc(at.shift_copied, 1)


def shift_send(act, at, b, g):
    n = number(b, g)
    act.wait_ge(at.shift_copied, n + 1)
    act.dma_start(at.q_stack[g % 2][96:98, :, :].bitcast(F32),
                  at.shift_row[0:2 * GH, :].bitcast(F32)).then_inc(at.shifted, 16)


def stack_send(sp, at, b, g, pair):
    n = number(b, g)
    heads, rows = slice(2 * pair, 2 * pair + 2), slice(2 * HD * pair, 2 * HD * (pair + 1))
    q, key = at.q_stack[g % 2], at.k_stack[g % 2]
    apart(sp, at.ones_set, at.score_t_ready, (n - 2) * UNITS + UNITS // 2 * (pair + 1))
    apart(sp, at.ones_set, at.q_ready, n + 1)
    for r, part in enumerate((0, 0, 1)):
        sp.dma_start(q[32 * r:32 * r + 32, heads, :].bitcast(F32),
                     at.q_split[rows, part, :].bitcast(F32)).then_inc(at.stacked[pair], 16)
    apart(sp, at.ones_set, at.k_ready, n + 1)
    for r, part in enumerate((0, 1, 0)):
        sp.dma_start(key[32 * r:32 * r + 32, heads, :].bitcast(F32),
                     at.k_split[rows, part, :].bitcast(F32)).then_inc(at.stacked[pair], 16)


def score_t_unit(pe, at, eye_bf, colmask, b, g, k):
    h, j = divmod(k, 3)
    n = number(b, g)
    if k == 0:
        pe.wait_ge(at.shifted, n * 16 + 16)
    at_least(pe, at.exp_done, n * UNITS + k - 1)
    q, key = at.q_stack[g % 2], at.k_stack[g % 2]
    for i, (kt, col, width) in enumerate(KEY_MAJOR[j]):
        pe.matmul(at.scores_t_ps[:, k % 2, col:col + width], key[0:98, h, kt * P:kt * P + P],
                  q[0:98, h, kt * P:SEQ], start=(i == 0), stop=False, skip_group_check=True)
    for kt, col, width in KEY_MAJOR[j]:
        mm = pe.matmul(at.scores_t_ps[:, k % 2, col:col + P], eye_bf[:, :], colmask[:, :],
                       start=False, stop=True, skip_group_check=True)
    mm.then_inc(at.score_t_ready, 1)


def exp_unit(act, at, b, g, k):
    u, w = number(b, g) * UNITS + k, WIDTH[k % 3]
    act.wait_ge(at.score_t_ready, u + 1)
    at_least(act, at.lo_done, u - 1)
    act.activation(at.prob[:, k % 2, 0:w], at.scores_t_ps[:, k % 2, 0:w], ACT.Exp, scale=SCALE)
    at_least(act, at.pv_done, u + 1 - at.ring)
    act.activation(at.prob_hi[:, k % at.ring, 0:w], at.scores_t_ps[:, k % 2, 0:w], ACT.Exp,
                   scale=SCALE).then_inc(at.exp_done, 1)


def lo_unit(dve, at, b, g, k):
    u, w = number(b, g) * UNITS + k, WIDTH[k % 3]
    dve.wait_ge(at.exp_done, u + 1)
    dve.tensor_tensor(at.prob_lo[:, k % at.ring, 0:w], at.prob[:, k % 2, 0:w], at.prob_hi[:, k % at.ring, 0:w],
                      ALU.subtract).then_inc(at.lo_done, 1)


def pv_unit(pe, at, b, g, k):
    h, j = divmod(k, 3)
    n = number(b, g)
    pe.wait_ge(at.lo_done, n * UNITS + k + 1)
    if j == 0:
        at_least(pe, at.pv_copied, n * GH + h - 1)
    if g == 0 and h == 0:
        pe.wait_ge(at.value_ready, b * TT + (1, 2, 4)[j])
    for kt, col, width in KEY_MAJOR[j]:
        for part, prob in enumerate((at.prob_hi, at.prob_lo)):
            mm = pe.matmul(at.pv_ps[0:at.vcols, h % 2, kt * P:SEQ], at.value[:, kt, g * GH + h, :],
                           prob[:, k % at.ring, col:col + width], start=(kt == 0 and part == 0),
                           stop=(kt == TT - 1 and part == 1), skip_group_check=True)
    mm.then_inc(at.pv_done, 1)


def pv_copy(act, at, b, g, h):
    n = number(b, g)
    act.wait_ge(at.pv_done, (n * GH + h + 1) * 3)
    if h == 0:
        at_least(act, at.gathered, n * 48)
    act.activation(at.pv_raw[0:at.vcols, h, :], at.pv_ps[0:at.vcols, h % 2, :], ACT.Copy).then_inc(at.pv_copied, 1)


PROJECTIONS = (((4, 7), (9, 12)), ((7, 9), (9, 12)), ((5, 8), (9, 12)), ((5, 8), (9, 12)))
AHEAD = 3
ROTATED = (4, 5)


def exists(b, g, ahead):
    return not (is_last(b) and g + ahead >= GROUPS)


def leaving(b, g, slot):
    for i, (start, stop) in enumerate(PROJECTIONS[g]):
        if stop == slot and exists(b, g, AHEAD):
            yield *group(b, g, AHEAD), i
    if slot == 0 and not (isinstance(b, int) and b == 0 and g == 0) and exists(b, g, AHEAD - 1):
        for i, (start, stop) in enumerate(PROJECTIONS[g - 1]):
            if stop == UNITS:
                yield *group(b, g, AHEAD - 1), i


def splitting(b, g, slot):
    if slot in ROTATED and exists(b, g, AHEAD - 1):
        yield *group(b, g, AHEAD - 1), ROTATED.index(slot)


SCORE_SLOTS = range(1, 8)


def share(count, slots, slot):
    return range(count * slot // slots, count * (slot + 1) // slots)


def behind(b, g, slot):
    return (b, g, slot - 1) if slot > 0 else (*group(b, g, -1), UNITS - 1)


def score_share(slot):
    return share(UNITS, len(SCORE_SLOTS), slot - SCORE_SLOTS[0]) if slot in SCORE_SLOTS else ()


def attention_layer(nc, x_t, wq_t, wk_t, wv_t, a_qkv, b_qkv, starts, consts, sums_hbm, attn_hbm, ids):
    with ExitStack() as ctx:
        def sb(what, shape, dt=F32):
            return ctx.enter_context(nc.sbuf_tensor(f"a_{what}", shape, dt))

        def sem(what):
            return ctx.enter_context(nc.semaphore(f"a_{what}"))

        at = Attention(nc, ctx, "a", HD, 4)
        lin_ps = ctx.enter_context(nc.psum_tensor("a_lin_ps", [P, 2, SEQ], F32))

        w_split = [sb(f"w{n}_split", [P, 2, KC, D], F32R) for n in "qkv"]
        x_stage = sb("x_stage", [P, KC, SEQ])
        x_split = sb("x_split", [P, 2, KC, SEQ], F32R)
        a_stage = sb("a_stage", [P, KC, 3 * RANK])
        a_split = sb("a_split", [P, 2, KC, 3 * RANK], F32R)
        b_stage = sb("b_stage", [P, 3 * D * RANK // P])
        b_split = sb("b_split", [P, 2, 3 * D * RANK // P], F32R)
        b_stack = sb("b_stack", [3 * RANK, 3, D], F32R)
        low_split = sb("low_split", [3 * RANK, 2, SEQ], F32R)
        low_stack = sb("low_stack", [3 * RANK, 3, SEQ], F32R)
        rope_in = [sb(f"rope_in{i}", [P, SEQ]) for i in range(2)]
        rope_turned = [sb(f"rope_turned{i}", [P, SEQ]) for i in range(2)]
        rope_out = [sb(f"rope_out{i}", [P, SEQ]) for i in range(2)]
        cos_sin = sb("cos_sin", [P, 2, SEQ])
        rowmask = sb("rowmask", [P, SEQ])
        eye = sb("eye", [P, P], F32R)
        eye_bf = sb("eye_bf", [P, P], BF16)
        colmask = sb("colmask", [P, P], BF16)
        sum_hi = sb("sum_hi", [P, SEQ])
        sum_lo = sb("sum_lo", [P, SEQ])
        sums = sb("sums", [GH * TT, P])
        inverse = sb("inverse", [GH * TT, P])
        inverse_all = sb("inverse_all", [P, SEQ])
        starts_i = sb("starts_i", [1, ADAPTERS], I32)
        starts_f = sb("starts_f", [1, ADAPTERS])
        index = sb("index", [1, BATCH])
        count = sb("count", [1, BATCH])

        const_in = sem("const_in")
        const_ready = sem("const_ready")
        ids_step = sem("ids_step")
        w_in = [sem(f"w{n}_in") for n in "qkv"]
        w_hi = sem("w_hi")
        w_ready = sem("w_ready")
        x_in = sem("x_in")
        x_hi = sem("x_hi")
        x_ready = sem("x_ready")
        ab_in = sem("ab_in")
        ab_hi = sem("ab_hi")
        ab_ready = sem("ab_ready")
        b_stacked = sem("b_stacked")
        low_made = sem("low_made")
        low_hi = sem("low_hi")
        low_ready = sem("low_ready")
        low_stacked = sem("low_stacked")
        lin_ready = [sem(f"lin_ready{i}") for i in range(2)]
        lin_free = [sem(f"lin_free{i}") for i in range(2)]
        turned = [sem(f"turned{i}") for i in range(2)]
        roped = [sem(f"roped{i}") for i in range(2)]
        rope_hi = [sem(f"rope_hi{i}") for i in range(2)]
        value_hi = sem("value_hi")
        inverted = sem("inverted")
        inverse_out = sem("inverse_out")
        inverse_in = sem("inverse_in")
        merged = sem("merged")
        normalised = sem("normalised")
        attn_out = sem("attn_out")

        def qk_use(b, g):
            return b * 6 + (g if g < 3 else 5)

        def v_use(b, t):
            return b * 6 + 3 + t // 2

        square = rope_out[0][:, 0:2 * P].rearrange("p (a n) -> p a n", a=2)
        stage = (x_stage, at.pv_raw)

        block = ctx.enter_context(nc.Block())

        @block.sync
        def _(sp):
            sp.dma_start(starts_i[:, :], starts).then_inc(const_in, 16)
            sp.dma_start(index[:, :], consts[0:1, COUNT:COUNT + BATCH]).then_inc(const_in, 16)
            sp.dma_start(cos_sin[:, :, :], consts[:, COS:EYE].rearrange("p (a n) -> p a n", a=2)).then_inc(const_in, 16)
            sp.dma_start(square[:, 0, :], consts[:, EYE:EYE + P]).then_inc(const_in, 16)
            sp.dma_start(square[:, 1, :], consts[:, COLMASK:COLMASK + P]).then_inc(const_in, 16)
            sp.dma_start(rowmask[:, :], consts[:, ROWMASK:ROWMASK + SEQ]).then_inc(const_in, 16)
            for n, w in enumerate((wq_t, wk_t, wv_t)):
                if n == 2:
                    sp.wait_ge(w_ready, 1)
                sp.dma_start(stage[n % 2][:, :, :], w).then_inc(w_in[n], 16)
            sp.wait_ge(ids_step, 2 + ADAPTERS + 1)

            def load(b):
                if isinstance(b, int) and b == 0:
                    sp.wait_ge(w_ready, 3)
                else:
                    apart(sp, at.ones_set, x_ready, b * KC)
                    apart(sp, at.ones_set, ab_ready, b * 2)
                sp.dma_start(x_stage[:, :, :], x_t[:, :, bass.ds(b * SEQ, SEQ)]).then_inc(x_in, 16)
                i = sp.value_load(ids[0:1, bass.ds(b, 1)], min_val=0, max_val=ADAPTERS - 1)
                sp.dma_start(a_stage[:, :, :], a_qkv[bass.ds(i, 1)].rearrange("a p c r -> (a p) c r")).then_inc(ab_in, 16)
                sp.dma_start(b_stage[:, :], b_qkv[bass.ds(i, 1)].rearrange("a p n -> (a p) n")).then_inc(ab_in, 16)

            def send_b(b):
                apart(sp, at.ones_set, lin_ready[1], qk_use(b, 0))
                apart(sp, at.ones_set, ab_ready, b * 2 + 2)
                for r, part in enumerate((0, 1, 0)):
                    sp.dma_start(b_stack[RANK * r:RANK * (r + 1), :, :].bitcast(F32),
                                 b_split[:, part, :].bitcast(F32)).then_inc(b_stacked, 16)

            def send_low(b):
                sp.wait_ge(low_ready, b + 1)
                for r, part in enumerate((0, 0, 1)):
                    sp.dma_start(low_stack[RANK * r:RANK * (r + 1), :, :].bitcast(F32),
                                 low_split[:, part, :].bitcast(F32)).then_inc(low_stacked, 16)

            def gather(b, g):
                n = number(b, g)
                apart(sp, at.ones_set, at.pv_copied, (n + 1) * GH)
                apart(sp, at.ones_set, attn_out, n * 16)
                sp.dma_start(sum_hi[:, :], at.pv_raw[0:HD, :, :]).then_inc(at.gathered, 16)
                sp.dma_start(sum_lo[:, :], at.pv_raw[HD:2 * HD, :, :]).then_inc(at.gathered, 16)
                sp.dma_start(sums[:, :], at.pv_raw[2 * HD:2 * HD + 1, :, :]).then_inc(at.gathered, 16)

            def spread(b, g):
                n = number(b, g)
                sp.wait_ge(inverted, n + 1)
                sp.dma_start(sums_hbm.rearrange("h (c n) -> (h c) n", c=TT), inverse[:, :]).then_inc(inverse_out, 16)
                sp.wait_ge(inverse_out, n * 16 + 16)
                sp.dma_start(inverse_all[:, :], sums_hbm.rearrange("(o h) n -> o h n", o=1).broadcast_to(
                    [HD, GH, SEQ])).then_inc(inverse_in, 16)

            def store(b, g):
                n = number(b, g)
                sp.wait_ge(normalised, n + 1)
                sp.dma_start(attn_hbm[:, g, bass.ds(b * SEQ, SEQ)], sum_lo[:, :]).then_inc(attn_out, 16)

            def step(b, g):
                last = is_last(b)
                if g == 0 and not last:
                    load(b + 1)
                first = isinstance(b, int) and b == 0 and g == 0
                if not first:
                    gather(*group(b, g, -1))
                if g == 1 and not last:
                    send_b(b + 1)
                    send_low(b + 1)
                if not first:
                    spread(*group(b, g, -1))
                if not (last and g >= 2):
                    stack_send(sp, at, *group(b, g, 2), 0)
                if not first:
                    store(*group(b, g, -1))
                if not (last and g >= 2):
                    stack_send(sp, at, *group(b, g, 2), 1)

            load(0)
            send_b(0)
            send_low(0)
            for pair in range(2):
                stack_send(sp, at, 0, 0, pair)
            for pair in range(2):
                stack_send(sp, at, 0, 1, pair)

            def body(b):
                for g in range(GROUPS):
                    step(b, g)

            batches(sp, body)
            gather(BATCH - 1, GROUPS - 1)
            spread(BATCH - 1, GROUPS - 1)
            store(BATCH - 1, GROUPS - 1)
            sp.wait_ge(attn_out, BATCH * GROUPS * 16)

        @block.gpsimd
        def _(pool):
            for i in range(2):
                pool.memset(at.k_stack[i][96:98, :, :].bitcast(F32), 1.0).then_inc(at.ones_set, 1)
                pool.wait_ge(at.ones_set, i + 1)
            pool.memset(at.value[:, :, :, 2 * HD:2 * HD + 1].bitcast(F32), 1.0).then_inc(at.ones_set, 1)
            pool.wait_ge(const_in, 96)

            def rope(b, g, i):
                n = number(b, g)
                pool.wait_ge(turned[i], n + 1)
                at_least(pool, at.k_ready if i else at.q_ready, n)
                pool.tensor_tensor(rope_out[i][:, :], rope_in[i][:, :], cos_sin[:, 0, :], ALU.mult).then_inc(roped[i], 1)
                pool.tensor_tensor(rope_turned[i][:, :], rope_turned[i][:, :], cos_sin[:, 1, :],
                                   ALU.mult).then_inc(roped[i], 1)
                pool.wait_ge(roped[i], n * 3 + 2)
                pool.tensor_tensor(rope_out[i][:, :], rope_out[i][:, :], rope_turned[i][:, :],
                                   ALU.add).then_inc(roped[i], 1)

            def merge(b, g):
                n = number(b, g)
                pool.wait_ge(at.gathered, n * 48 + 48)
                pool.tensor_tensor(sum_hi[:, :], sum_hi[:, :], sum_lo[:, :], ALU.add).then_inc(merged, 1)

            def step(b, g):
                tiles = [t for slot in range(UNITS) for t in leaving(b, g, slot)]
                for t in tiles[:1]:
                    rope(*t)
                if not (isinstance(b, int) and b == 0 and g == 0):
                    merge(*group(b, g, -1))
                for t in tiles[1:]:
                    rope(*t)

            for g in range(3):
                rope(0, g, 0)
                rope(0, g, 1)

            def body(b):
                for g in range(GROUPS):
                    step(b, g)

            batches(pool, body)
            merge(BATCH - 1, GROUPS - 1)

        @block.scalar
        def _(act):
            def weights(n):
                act.wait_ge(w_in[n], 16)
                act.activation(w_split[n][:, 0, :, :], stage[n % 2][:, :, :], ACT.Copy).then_inc(w_hi, 1)

            def x_chunk(b, c):
                if c == 0:
                    act.wait_ge(x_in, b * 16 + 16)
                    at_least(act, lin_ready[1], qk_use(b, 0))
                act.activation(x_split[:, 0, c, :], x_stage[:, c, :], ACT.Copy).then_inc(x_hi, 1)

            def adapter(b):
                act.wait_ge(ab_in, b * 32 + 32)
                act.activation(a_split[:, 0, :, :], a_stage[:, :, :], ACT.Copy).then_inc(ab_hi, 1)
                at_least(act, b_stacked, b * 48)
                act.activation(b_split[:, 0, :], b_stage[:, :], ACT.Copy).then_inc(ab_hi, 1)

            def low(b):
                act.wait_ge(low_made, b + 1)
                at_least(act, low_stacked, b * 48)
                act.activation(low_split[:, 0, :], lin_ps[0:3 * RANK, 1, :], ACT.Copy).then_inc(low_hi, 1)

            def projected(b, g, i):
                act.wait_ge(lin_ready[i], qk_use(b, g) + 1)
                at_least(act, roped[i], number(b, g) * 3)
                act.activation(rope_in[i][:, :], lin_ps[:, i, :], ACT.Copy).then_inc(lin_free[i], 1)

            def rotated_hi(b, g, i):
                n = number(b, g)
                act.wait_ge(roped[i], n * 3 + 3)
                for pair in range(2):
                    at_least(act, at.stacked[pair], n * 96)
                split = at.k_split if i else at.q_split
                act.activation(split[:, 0, :], rope_out[i][:, :], ACT.Copy).then_inc(rope_hi[i], 1)

            def value(b, t):
                act.wait_ge(lin_ready[t % 2], v_use(b, t) + 1)
                if t == 0:
                    at_least(act, at.pv_done, b * GROUPS * UNITS)
                act.activation(at.value[:, t, :, 0:HD], lin_ps[:, t % 2, :].rearrange("p (h d) -> p h d", d=HD),
                               ACT.Copy).then_inc(value_hi, 1)

            def step(b, g):
                last = is_last(b)
                first = isinstance(b, int) and b == 0 and g == 0
                for slot in range(UNITS):
                    if slot == 2 and not first:
                        pv_copy(act, at, *group(b, g, -1), 3)
                    if slot in (5, 8, 11):
                        pv_copy(act, at, b, g, (slot - 5) // 3)
                    exp_unit(act, at, b, g, slot)
                    if slot == 9 and not (last and g == GROUPS - 1):
                        shift_copy(act, at, *group(b, g, 1))
                        shift_send(act, at, *group(b, g, 1))
                    if g == 0 and 1 <= slot <= TT:
                        value(b, slot - 1)
                    if g == 0 and slot == 9 and not last:
                        adapter(b + 1)
                    if g == 1 and slot < 2 and not last:
                        for c in range(2):
                            x_chunk(b + 1, slot * 2 + c)
                    if g == 1 and slot == 5 and not last:
                        low(b + 1)
                    for tile in leaving(b, g, slot):
                        projected(*tile)
                    for tile in splitting(b, g, slot):
                        rotated_hi(*tile)

            for n in range(3):
                weights(n)
            adapter(0)
            for c in range(KC):
                x_chunk(0, c)
            low(0)
            for g in range(2):
                for i in range(2):
                    projected(0, g, i)
                    rotated_hi(0, g, i)
            for i in range(2):
                projected(0, 2, i)
            shift_copy(act, at, 0, 0)
            shift_send(act, at, 0, 0)

            def body(b):
                for g in range(GROUPS):
                    step(b, g)

            batches(act, body)
            pv_copy(act, at, BATCH - 1, GROUPS - 1, 3)

        @block.vector
        def _(dve):
            dve.wait_ge(const_in, 96)
            dve.tensor_copy(starts_f[:, :], starts_i[:, :]).then_inc(ids_step, 1)
            dve.memset(count[:, :], -1.0).then_inc(ids_step, 1)
            for i in range(ADAPTERS):
                dve.wait_ge(ids_step, 2 + i)
                dve.scalar_tensor_tensor(out=count[:, :], in0=index[:, :], scalar=starts_f[0:1, i:i + 1],
                                         in1=count[:, :], op0=ALU.is_ge, op1=ALU.add).then_inc(ids_step, 1)
            dve.wait_ge(ids_step, 2 + ADAPTERS)
            dve.tensor_scalar(ids[:, :], count[:, :], 0.0, None, ALU.max).then_inc(ids_step, 1)
            dve.tensor_copy(eye[:, :], square[:, 0, :]).then_inc(const_ready, 1)
            dve.tensor_copy(eye_bf[:, :], square[:, 0, :]).then_inc(const_ready, 1)
            dve.tensor_copy(colmask[:, :], square[:, 1, :]).then_inc(const_ready, 1)

            def weights(n):
                dve.wait_ge(w_hi, n + 1)
                dve.tensor_tensor(w_split[n][:, 1, :, :], stage[n % 2][:, :, :], w_split[n][:, 0, :, :],
                                  ALU.subtract).then_inc(w_ready, 1)

            def x_chunk(b, c):
                dve.wait_ge(x_hi, b * KC + c + 1)
                dve.tensor_tensor(x_split[:, 1, c, :], x_stage[:, c, :], x_split[:, 0, c, :],
                                  ALU.subtract).then_inc(x_ready, 1)

            def adapter(b):
                dve.wait_ge(ab_hi, b * 2 + 2)
                dve.tensor_tensor(a_split[:, 1, :, :], a_stage[:, :, :], a_split[:, 0, :, :],
                                  ALU.subtract).then_inc(ab_ready, 1)
                dve.tensor_tensor(b_split[:, 1, :], b_stage[:, :], b_split[:, 0, :],
                                  ALU.subtract).then_inc(ab_ready, 1)

            def low(b):
                dve.wait_ge(low_hi, b + 1)
                dve.tensor_tensor(low_split[:, 1, :], lin_ps[0:3 * RANK, 1, :], low_split[:, 0, :],
                                  ALU.subtract).then_inc(low_ready, 1)

            def exchange(b, g, i):
                apart(dve, at.ones_set, lin_free[i], number(b, g) + 1)
                apart(dve, at.ones_set, roped[i], number(b, g) * 3)
                dve.stream_shuffle(rope_turned[i][:, :], rope_in[i][:, :],
                                   [p ^ 2 for p in range(32)]).then_inc(turned[i], 1)

            def rotated_lo(b, g, i):
                dve.wait_ge(rope_hi[i], number(b, g) + 1)
                split = at.k_split if i else at.q_split
                dve.tensor_tensor(split[:, 1, :], rope_out[i][:, :], split[:, 0, :],
                                  ALU.subtract).then_inc(at.k_ready if i else at.q_ready, 1)

            def value(b, t):
                dve.wait_ge(value_hi, b * TT + t + 1)
                dve.tensor_tensor(at.value[:, t, :, HD:2 * HD], lin_ps[:, t % 2, :].rearrange("p (h d) -> p h d", d=HD),
                                  at.value[:, t, :, 0:HD],
                                  ALU.subtract).then_inc(at.value_ready, 1)

            def invert(b, g):
                n = number(b, g)
                dve.wait_ge(at.gathered, n * 48 + 48)
                at_least(dve, inverse_out, n * 16)
                dve.reciprocal(inverse[:, :], sums[:, :]).then_inc(inverted, 1)

            def normalise(b, g):
                n = number(b, g)
                dve.wait_ge(merged, n + 1)
                dve.wait_ge(inverse_in, n * 16 + 16)
                dve.tensor_tensor(sum_lo[:, :], sum_hi[:, :], inverse_all[:, :], ALU.mult).then_inc(normalised, 1)

            def step(b, g):
                last = is_last(b)
                first = isinstance(b, int) and b == 0 and g == 0
                for slot in range(UNITS):
                    if slot > 0:
                        lo_unit(dve, at, b, g, slot - 1)
                    elif not first:
                        lo_unit(dve, at, *group(b, g, -1), UNITS - 1)
                    if not (last and g == GROUPS - 1):
                        for k in score_share(slot):
                            score_max(dve, at, rowmask, *group(b, g, 1), k)
                        if slot == SCORE_SLOTS[-1]:
                            shift_split(dve, at, *group(b, g, 1))
                    if slot == 6 and not first:
                        invert(*group(b, g, -1))
                    if slot == 10 and not first:
                        normalise(*group(b, g, -1))
                    if g == 0 and 1 <= slot <= TT:
                        value(b, slot - 1)
                    if g == 0 and slot == 10 and not last:
                        adapter(b + 1)
                    if g == 1 and 1 <= slot < 3 and not last:
                        for c in range(2):
                            x_chunk(b + 1, (slot - 1) * 2 + c)
                    if g == 1 and slot == 6 and not last:
                        low(b + 1)
                    if not (first and slot == 0):
                        for tile in leaving(*behind(b, g, slot)):
                            exchange(*tile)
                        for tile in splitting(*behind(b, g, slot)):
                            rotated_lo(*tile)

            for n in range(3):
                weights(n)
            adapter(0)
            for c in range(KC):
                x_chunk(0, c)
            low(0)
            for g in range(2):
                for i in range(2):
                    exchange(0, g, i)
                    rotated_lo(0, g, i)
            for i in range(2):
                exchange(0, 2, i)
            for k in range(UNITS):
                score_max(dve, at, rowmask, 0, 0, k)
            shift_split(dve, at, 0, 0)

            def body(b):
                for g in range(GROUPS):
                    step(b, g)

            batches(dve, body)
            lo_unit(dve, at, BATCH - 1, GROUPS - 1, UNITS - 1)
            invert(BATCH - 1, GROUPS - 1)
            normalise(BATCH - 1, GROUPS - 1)

        @block.tensor
        def _(pe):
            pe.wait_ge(const_ready, 3)
            pe.wait_ge(at.ones_set, 3)

            def low(b, items):
                for x in items:
                    c, (w, a) = x // 3, PASSES[x % 3]
                    if x == 0:
                        at_least(pe, lin_free[1], b * GROUPS)
                        pe.wait_ge(x_ready, (b + 1) * KC)
                        pe.wait_ge(ab_ready, (b + 1) * 2)
                    mm = pe.matmul(lin_ps[0:3 * RANK, 1, :], a_split[:, w, c, :], x_split[:, a, c, :],
                                   start=(x == 0), stop=(x == 3 * KC - 1))
                    if x == 3 * KC - 1:
                        mm.then_inc(low_made, 1)

            def project(b, g, i, items):
                for x in items:
                    if x == 0:
                        if g == 3:
                            pe.wait_ge(at.value_ready, b * TT + 3 + i)
                        elif g == 0 and i == 1:
                            pe.wait_ge(low_ready, b + 1)
                        else:
                            at_least(pe, lin_free[i], number(b, g))
                    if x < 3 * KC:
                        c, (w, a) = x // 3, PASSES[x % 3]
                        pe.matmul(lin_ps[:, i, :], w_split[i][:, w, c, g * P:g * P + P], x_split[:, a, c, :],
                                  start=(x == 0), stop=False)
                    else:
                        pe.wait_ge(low_stacked, b * 48 + 48)
                        pe.wait_ge(b_stacked, b * 48 + 48)
                        pe.matmul(lin_ps[:, i, :], b_stack[:, i, g * P:g * P + P], low_stack[:, i, :],
                                  start=False, stop=True).then_inc(lin_ready[i], 1)

            def project_value(b, t):
                bank = t % 2
                if t < 2:
                    pe.wait_ge(lin_free[bank], b * GROUPS + 3)
                else:
                    pe.wait_ge(at.value_ready, b * TT + t - 1)
                for x in range(3 * KC):
                    c, (w, a) = x // 3, PASSES[x % 3]
                    pe.matmul(lin_ps[:, bank, :], x_split[:, a, c, t * P:t * P + P], w_split[2][:, w, c, :],
                              start=(x == 0), stop=False)
                pe.matmul(lin_ps[:, bank, :], low_stack[:, 2, t * P:t * P + P], b_stack[:, 2, :],
                          start=False, stop=True).then_inc(lin_ready[bank], 1)

            def step(b, g):
                last = is_last(b)
                first = isinstance(b, int) and b == 0 and g == 0
                for slot in range(UNITS):
                    score_t_unit(pe, at, eye_bf, colmask, b, g, slot)
                    if slot == 9 and not (last and g == GROUPS - 1):
                        shift_turn(pe, at, eye, *group(b, g, 1))
                    if not (last and g == GROUPS - 1):
                        for k in score_share(slot):
                            score_unit(pe, at, *group(b, g, 1), k)
                    if slot < 2 and not first:
                        pv_unit(pe, at, *group(b, g, -1), UNITS - 2 + slot)
                    if g == 0 and slot < TT:
                        project_value(b, slot)
                    if g == 1 and 3 <= slot < 5 and not last:
                        low(b + 1, share(3 * KC, 2, slot - 3))
                    for i, (start, stop) in enumerate(PROJECTIONS[g]):
                        if start <= slot < stop and exists(b, g, AHEAD):
                            project(*group(b, g, AHEAD), i, share(3 * KC + 1, stop - start, slot - start))
                    if slot >= 2:
                        pv_unit(pe, at, b, g, slot - 2)

            pe.wait_ge(w_ready, 3)
            low(0, range(3 * KC))
            for g in range(3):
                for i in range(2):
                    project(0, g, i, range(3 * KC + 1))
            for k in range(UNITS):
                score_unit(pe, at, 0, 0, k)
            shift_turn(pe, at, eye, 0, 0)

            def body(b):
                for g in range(GROUPS):
                    step(b, g)

            batches(pe, body)
            for k in range(UNITS - 2, UNITS):
                pv_unit(pe, at, BATCH - 1, GROUPS - 1, k)


QK_SLOTS_B = ((4, 6, 8), (5, 7, 9), (5, 7, 9), (0, 4, 8))


def rsqrt(dve, step, done, out, x, t):
    dve.tensor_scalar(t.bitcast(I32), x.bitcast(I32), 1, None, ALU.logical_shift_right).then_inc(step, 1)
    dve.wait_ge(step, done + 1)
    dve.tensor_scalar(out.bitcast(I32), t.bitcast(I32), -1.0, RSQRT_MAGIC, ALU.mult, ALU.add).then_inc(step, 1)
    for i in range(3):
        dve.wait_ge(step, done + 2 + 3 * i)
        dve.tensor_tensor(t, out, out, ALU.mult).then_inc(step, 1)
        dve.wait_ge(step, done + 3 + 3 * i)
        dve.scalar_tensor_tensor(out=t, in0=t, scalar=-0.5, in1=x, op0=ALU.mult, op1=ALU.mult).then_inc(step, 1)
        dve.wait_ge(step, done + 4 + 3 * i)
        dve.scalar_tensor_tensor(out=out, in0=t, scalar=1.5, in1=out, op0=ALU.add, op1=ALU.mult).then_inc(step, 1)


RSQRT_STEPS = 11


def gate_layer(nc, x, attn_hbm, wo_t, a_o, b_o, wq_t, wk_t, wv, wo, low_a, ln_w, selector, consts, ids, sums_hbm,
               x1_hbm, h_hbm, z_hbm):
    with ExitStack() as ctx:
        def sb(what, shape, dt=F32):
            return ctx.enter_context(nc.sbuf_tensor(f"b_{what}", shape, dt))

        def sem(what):
            return ctx.enter_context(nc.semaphore(f"b_{what}"))

        at = Attention(nc, ctx, "b", RANK, 3)
        lin_ps = ctx.enter_context(nc.psum_tensor("b_lin_ps", [P, 2, SEQ], F32))
        VW = HEADS * RANK

        wo_split = sb("wo_split", [P, 2, KC, D], F32R)
        qk_split = [sb(f"w{n}_split", [P, 2, KC, D], F32R) for n in "qk"]
        vw_split = sb("vw_split", [P, 2, KC, VW], F32R)
        low_a_split = sb("low_a_split", [P, 2, KC, RANK], F32R)
        wide = sb("wide", [P, KC, D])
        res = sb("res", [P, TT, D])
        attn_split = sb("attn_split", [P, 2, KC, SEQ], F32R)
        h_split = sb("h_split", [P, 2, KC, SEQ], F32R)
        h_turn = sb("h_turn", [P, 2, KC, P])
        a_stage = sb("a_stage", [P, KC, RANK])
        a_split = sb("a_split", [P, 2, KC, RANK], F32R)
        b_stage = sb("b_stage", [P, D * RANK // P])
        b_split = sb("b_split", [P, 2, D * RANK // P], F32R)
        b_stack = sb("b_stack", [3 * RANK, D], F32R)
        low_split = sb("low_split", [RANK, 2, SEQ], F32R)
        low_stack = sb("low_stack", [3 * RANK, SEQ], F32R)
        rowmask = sb("rowmask", [P, SEQ])
        square = h_turn[:, 0, 0:2, :]
        eye = sb("eye", [P, P], F32R)
        eye_bf = sb("eye_bf", [P, P], BF16)
        colmask = sb("colmask", [P, P], BF16)
        sel = sb("sel", [GH * RANK, RANK])
        lnw = sb("lnw", [P, 2, KC])
        a_full = at.prob[:, 0, 0:KC * RANK].rearrange("p (c r) -> p c r", c=KC)
        wo_a = at.prob[:, 1, 0:TT * GH * RANK].rearrange("p (t r) -> p t r", t=TT)
        stats = sb("stats", [P, TT, 6])
        mean_var = sb("mean_var", [P, TT, 2])
        squares = sb("squares", [P, 2, TT])
        inv_root = sb("inv_root", [P, 2, TT])
        newton = sb("newton", [P, 2, TT])
        sum_hi = sb("sum_hi", [GH * RANK, SEQ])
        sum_lo = sb("sum_lo", [GH * RANK, SEQ])
        sums = sb("sums", [GH * TT, P])
        inverse = sb("inverse", [GH * TT, P])
        out_sum = sb("out_sum", [GH * RANK, SEQ])
        h_low = sb("h_low", [RANK, SEQ])
        mod = at.shift_row[:, :].bitcast(F32)
        z_split = low_split

        const_in = sem("const_in")
        const_ready = sem("const_ready")
        stage_in = [sem(f"stage_in{i}") for i in range(3)]
        w_hi = sem("w_hi")
        w_ready = sem("w_ready")
        zeroed = sem("zeroed")
        wo_a_made = sem("wo_a_made")
        wo_a_copied = sem("wo_a_copied")
        vw_made = sem("vw_made")
        in_done = [sem(f"in_done{i}") for i in range(2)]
        attn_hi = sem("attn_hi")
        attn_ready = sem("attn_ready")
        ab_in = sem("ab_in")
        ab_hi = sem("ab_hi")
        ab_ready = sem("ab_ready")
        b_stacked = sem("b_stacked")
        low_made = sem("low_made")
        low_hi = sem("low_hi")
        low_ready = sem("low_ready")
        low_stacked = sem("low_stacked")
        o_made = sem("o_made")
        o_added = sem("o_added")
        stats_done = sem("stats_done")
        ln_step = sem("ln_step")
        x1_ready = sem("x1_ready")
        x1_out = sem("x1_out")
        h_ready = sem("h_ready")
        h_turned = sem("h_turned")
        h_copied = sem("h_copied")
        h_hi = sem("h_hi")
        h_split_ready = sem("h_split_ready")
        h_out = [sem(f"h_out{i}") for i in range(2)]
        qk_made = [sem(f"{n}_made") for n in "qk"]
        qk_hi = [sem(f"{n}_hi") for n in "qk"]
        v_made = sem("v_made")
        value_hi = sem("value_hi")
        inverted = sem("inverted")
        inverse_out = sem("inverse_out")
        inverse_in = sem("inverse_in")
        merged = sem("merged")
        normalised = sem("normalised")
        added = sem("added")
        mod_made = sem("mod_made")
        mod_done = sem("mod_done")
        h_low_made = sem("h_low_made")
        h_low_copied = sem("h_low_copied")
        z_made = sem("z_made")
        z_hi = sem("z_hi")
        z_ready = sem("z_ready")
        z_out = sem("z_out")

        LN_STEPS = TT + 4 + RSQRT_STEPS
        qk_ready = (at.q_ready, at.k_ready)
        stage = (wide, res, at.pv_raw)

        block = ctx.enter_context(nc.Block())

        @block.sync
        def _(sp):
            sp.dma_start(stage[0][:, :, :], wo).then_inc(stage_in[0], 16)
            sp.dma_start(a_full[:, :, :], low_a).then_inc(const_in, 16)
            sp.dma_start(square[:, 0, :], consts[:, EYE:EYE + P]).then_inc(const_in, 16)
            sp.dma_start(square[:, 1, :], consts[:, COLMASK:COLMASK + P]).then_inc(const_in, 16)
            sp.dma_start(rowmask[:, :], consts[:, ROWMASK:ROWMASK + SEQ]).then_inc(const_in, 16)
            sp.dma_start(lnw[:, :, :], ln_w).then_inc(const_in, 16)
            sp.dma_start(sel[:, :], selector).then_inc(const_in, 16)
            sp.dma_start(stage[1][:, :, :], wv).then_inc(stage_in[1], 16)
            sp.dma_start(stage[2][:, :, :], wo_t).then_inc(stage_in[2], 16)
            sp.wait_ge(wo_a_made, 1)
            sp.dma_start(stage[0][:, :, :], wq_t).then_inc(stage_in[0], 16)
            sp.wait_ge(vw_made, 2)
            sp.dma_start(stage[1][:, :, :], wk_t).then_inc(stage_in[1], 16)

            def load(b):
                if isinstance(b, int) and b == 0:
                    sp.wait_ge(w_ready, 4 * KC + KC)
                else:
                    apart(sp, at.ones_set, h_turned, b * TT)
                    apart(sp, at.ones_set, ab_ready, b * 2)
                sp.dma_start(wide[:, :, :], attn_hbm[:, :, bass.ds(b * SEQ, SEQ)]).then_inc(in_done[0], 16)
                i = sp.value_load(ids[0:1, bass.ds(b, 1)], min_val=0, max_val=ADAPTERS - 1)
                sp.dma_start(a_stage[:, :, :], a_o[bass.ds(i, 1)].rearrange("a p c r -> (a p) c r")).then_inc(ab_in, 16)
                sp.dma_start(b_stage[:, :], b_o[bass.ds(i, 1)].rearrange("a p n -> (a p) n")).then_inc(ab_in, 16)

            def load_x(b):
                if not (isinstance(b, int) and b == 0):
                    apart(sp, at.ones_set, x1_out, b * 16)
                    apart(sp, at.ones_set, h_ready, b * TT)
                sp.dma_start(res[:, :, :], x[bass.ds(b * SEQ, SEQ), :].rearrange("(t p) d -> p t d", p=P)).then_inc(
                    in_done[1], 16)

            def send_b(b):
                apart(sp, at.ones_set, o_made, b * TT)
                apart(sp, at.ones_set, ab_ready, b * 2 + 2)
                for r, part in enumerate((0, 1, 0)):
                    sp.dma_start(b_stack[RANK * r:RANK * (r + 1), :].bitcast(F32),
                                 b_split[:, part, :].bitcast(F32)).then_inc(b_stacked, 16)

            def send_low(b):
                sp.wait_ge(low_ready, b + 1)
                for r, part in enumerate((0, 0, 1)):
                    sp.dma_start(low_stack[RANK * r:RANK * (r + 1), :].bitcast(F32),
                                 low_split[:, part, :].bitcast(F32)).then_inc(low_stacked, 16)

            def gather(b, g):
                n = number(b, g)
                apart(sp, at.ones_set, at.pv_copied, (n + 1) * GH)
                apart(sp, at.ones_set, added, n)
                sp.dma_start(sum_hi[:, :], at.pv_raw[0:RANK, :, :]).then_inc(at.gathered, 16)
                sp.dma_start(sum_lo[:, :], at.pv_raw[RANK:2 * RANK, :, :]).then_inc(at.gathered, 16)
                sp.dma_start(sums[:, :], at.pv_raw[2 * RANK:2 * RANK + 1, :, :]).then_inc(at.gathered, 16)

            def spread(b, g):
                n = number(b, g)
                sp.wait_ge(inverted, n + 1)
                sp.dma_start(sums_hbm.rearrange("h (c n) -> (h c) n", c=TT), inverse[:, :]).then_inc(inverse_out, 16)
                sp.wait_ge(inverse_out, n * 16 + 16)
                sp.wait_ge(merged, n + 1)
                sp.dma_start(sum_lo[:, :], sums_hbm.rearrange("(o h) n -> o h n", o=1).broadcast_to(
                    [RANK, GH, SEQ])).then_inc(inverse_in, 16)

            def store_x1(b):
                sp.wait_ge(x1_ready, b * TT + TT)
                sp.dma_start(x1_hbm[bass.ds(b * SEQ, SEQ), :].rearrange("(t p) d -> p t d", p=P),
                             res[:, :, :]).then_inc(x1_out, 16)

            def store_h(b, t):
                sp.wait_ge(h_copied, b * TT + t + 1)
                sp.dma_start(h_hbm[:, :, bass.ds(b * SEQ + t * P, P)], h_turn[:, t % 2, :, :]).then_inc(h_out[t % 2], 16)

            def store_z(b):
                sp.wait_ge(z_ready, b + 1)
                for part in range(2):
                    sp.dma_start(z_hbm[part, :, bass.ds(b * SEQ, SEQ)],
                                 z_split[:, part, :].bitcast(F32)).then_inc(z_out, 16)

            def step(b, g):
                last = is_last(b)
                zero = isinstance(b, int) and b == 0
                first = zero and g == 0
                if g == 0 and not last:
                    load(b + 1)
                if g == 2 and not last:
                    store_h(b + 1, 0)
                    store_h(b + 1, 1)
                if not first:
                    gather(*group(b, g, -1))
                if g == 2 and not last:
                    store_h(b + 1, 2)
                    store_h(b + 1, 3)
                if not first:
                    spread(*group(b, g, -1))
                if not (last and g >= 2):
                    stack_send(sp, at, *group(b, g, 2), 0)
                if g == 0 and not last:
                    send_b(b + 1)
                    send_low(b + 1)
                    load_x(b + 1)
                if g == 1 and not zero:
                    store_z(b - 1)
                if g == 2 and not last:
                    store_x1(b + 1)
                if not (last and g >= 2):
                    stack_send(sp, at, *group(b, g, 2), 1)

            load(0)
            load_x(0)
            send_b(0)
            send_low(0)
            store_x1(0)
            for t in range(TT):
                store_h(0, t)
            for pair in range(2):
                stack_send(sp, at, 0, 0, pair)
            for pair in range(2):
                stack_send(sp, at, 0, 1, pair)

            def body(b):
                for g in range(GROUPS):
                    step(b, g)

            batches(sp, body)
            gather(BATCH - 1, GROUPS - 1)
            spread(BATCH - 1, GROUPS - 1)
            store_z(BATCH - 1)
            sp.wait_ge(z_out, BATCH * 32)
            sp.wait_ge(x1_out, BATCH * 16)
            for i in range(2):
                sp.wait_ge(h_out[i], BATCH * TT // 2 * 16)

        @block.gpsimd
        def _(pool):
            for i in range(2):
                pool.memset(at.k_stack[i][96:98, :, :].bitcast(F32), 1.0).then_inc(at.ones_set, 1)
                pool.wait_ge(at.ones_set, i + 1)
            pool.memset(at.value[:, :, :, 2 * RANK:2 * RANK + 1].bitcast(F32), 1.0).then_inc(at.ones_set, 1)
            pool.memset(wo_a[:, :, :], 0.0).then_inc(zeroed, 1)

            def merge(b, g):
                n = number(b, g)
                apart(pool, at.ones_set, at.gathered, n * 48 + 48)
                pool.tensor_tensor(sum_hi[:, :], sum_hi[:, :], sum_lo[:, :], ALU.add).then_inc(merged, 1)
                pool.wait_ge(merged, n + 1)
                pool.wait_ge(inverse_in, n * 16 + 16)
                pool.tensor_tensor(sum_hi[:, :], sum_hi[:, :], sum_lo[:, :], ALU.mult).then_inc(normalised, 1)
                apart(pool, at.ones_set, normalised, n + 1)
                if g == 0:
                    apart(pool, at.ones_set, mod_made, b)
                    pool.tensor_copy(out_sum[:, :], sum_hi[:, :]).then_inc(added, 1)
                else:
                    apart(pool, at.ones_set, added, n)
                    pool.tensor_tensor(out_sum[:, :], out_sum[:, :], sum_hi[:, :], ALU.add).then_inc(added, 1)

            def body(b):
                for g in range(GROUPS):
                    if not (isinstance(b, int) and b == 0 and g == 0):
                        merge(*group(b, g, -1))

            batches(pool, body)
            merge(BATCH - 1, GROUPS - 1)

        @block.scalar
        def _(act):
            act.wait_ge(const_in, 96)
            act.wait_ge(stage_in[2], 16)
            for c in range(KC):
                act.activation(wo_split[:, 0, c, :], stage[2][:, c, :], ACT.Copy).then_inc(w_hi, 1)
            for c in range(KC):
                act.activation(low_a_split[:, 0, c, :], a_full[:, c, :], ACT.Copy,
                               scale=lnw[:, 1, c:c + 1]).then_inc(w_hi, 1)
            act.wait_ge(vw_made, 2)
            for c in range(KC):
                act.activation(vw_split[:, 0, c, :], lin_ps[:, c // 2, (c % 2) * VW:(c % 2 + 1) * VW], ACT.Copy,
                               scale=lnw[:, 0, c:c + 1]).then_inc(w_hi, 1)
            for n in range(2):
                act.wait_ge(stage_in[n], 32)
                for c in range(KC):
                    act.activation(qk_split[n][:, 0, c, :], stage[n][:, c, :], ACT.Copy,
                                   scale=lnw[:, 0, c:c + 1]).then_inc(w_hi, 1)

            def attn_chunk(b, c):
                if c == 0:
                    act.wait_ge(in_done[0], b * 16 + 16)
                    at_least(act, o_made, b * TT)
                act.activation(attn_split[:, 0, c, :], wide[:, c, :], ACT.Copy).then_inc(attn_hi, 1)

            def adapter(b):
                act.wait_ge(ab_in, b * 32 + 32)
                act.activation(a_split[:, 0, :, :], a_stage[:, :, :], ACT.Copy).then_inc(ab_hi, 1)
                at_least(act, b_stacked, b * 48)
                act.activation(b_split[:, 0, :], b_stage[:, :], ACT.Copy).then_inc(ab_hi, 1)

            def low(b):
                act.wait_ge(low_made, b + 1)
                act.activation(low_split[:, 0, :], at.scores_ps[0:RANK, 1, :], ACT.Copy).then_inc(low_hi, 1)

            def h_tile(b, t):
                act.wait_ge(h_turned, b * TT + t + 1)
                at_least(act, h_out[t % 2], (b * 2 + t // 2) * 16)
                bank = lin_ps[:, t % 2, :].rearrange("p (c n) -> p c n", c=KC)
                act.activation(h_turn[:, t % 2, :, :], bank, ACT.Copy).then_inc(h_copied, 1)
                act.activation(h_split[:, 0, :, t * P:t * P + P], bank, ACT.Copy).then_inc(h_hi, 1)

            def projected(b, g, i):
                n = number(b, g)
                act.wait_ge(qk_made[i], n + 1)
                for pair in range(2):
                    at_least(act, at.stacked[pair], n * 96)
                split = at.k_split if i else at.q_split
                act.activation(split[:, 0, :], lin_ps[:, i, :], ACT.Copy).then_inc(qk_hi[i], 1)

            def value(b, t):
                act.wait_ge(v_made, b * TT + t + 1)
                if t == 0:
                    at_least(act, at.pv_done, b * GROUPS * UNITS)
                act.activation(at.value[:, t, :, 0:RANK], lin_ps[:, t % 2, 0:VW].rearrange("p (h d) -> p h d", d=RANK),
                               ACT.Copy).then_inc(value_hi, 1)

            def tanh(b):
                act.wait_ge(mod_made, b + 1)
                act.wait_ge(at.shifted, min(number(b, 6), BATCH * GROUPS) * 16 if isinstance(b, int) else
                            b * GROUPS * 16 + 96)
                act.activation(mod[:, :], at.scores_ps[0:RANK, 1, :], ACT.Tanh).then_inc(mod_done, 1)

            def z_part(b):
                act.wait_ge(z_made, b + 1)
                act.wait_ge(low_stacked, min(b + 3, BATCH) * 48 if isinstance(b, int) else b * 48 + 144)
                act.activation(z_split[:, 0, :], mod[:, :], ACT.Copy).then_inc(z_hi, 1)

            def h_times_a(b):
                act.wait_ge(h_low_made, b + 1)
                at_least(act, z_made, b)
                act.activation(h_low[:, :], at.scores_ps[0:RANK, 1, :], ACT.Copy).then_inc(h_low_copied, 1)

            def step(b, g):
                last = is_last(b)
                zero = isinstance(b, int) and b == 0
                first = zero and g == 0
                q_from, k_from, k_to = QK_SLOTS_B[g]
                for slot in range(UNITS):
                    if slot == 2 and not first:
                        pv_copy(act, at, *group(b, g, -1), 3)
                    if slot in (5, 8, 11):
                        pv_copy(act, at, b, g, (slot - 5) // 3)
                    exp_unit(act, at, b, g, slot)
                    if slot == 9 and not (last and g == GROUPS - 1):
                        if g == 1 and not zero:
                            act.wait_ge(z_ready, b)
                        shift_copy(act, at, *group(b, g, 1))
                        shift_send(act, at, *group(b, g, 1))
                    if g == 0 and 1 <= slot <= TT:
                        value(b, slot - 1)
                    if g == 0 and not last:
                        if 3 <= slot < 7:
                            attn_chunk(b + 1, slot - 3)
                        if slot == 6:
                            adapter(b + 1)
                        if slot == 10:
                            low(b + 1)
                    if g == 1 and not zero:
                        if slot == 1:
                            tanh(b - 1)
                        if slot == 4:
                            z_part(b - 1)
                    if g == 1 and slot == 11:
                        h_times_a(b)
                    if g == 2 and 1 <= slot < 5 and not last:
                        h_tile(b + 1, slot - 1)
                    if g == 3 and slot == 8 and not zero and not last:
                        act.wait_ge(z_out, b * 32)
                    if not (last and g >= 2):
                        if slot == k_from:
                            projected(*group(b, g, 2), 0)
                        if slot == k_to:
                            projected(*group(b, g, 2), 1)

            for c in range(KC):
                attn_chunk(0, c)
            adapter(0)
            low(0)
            for t in range(TT):
                h_tile(0, t)
            for g in range(2):
                for i in range(2):
                    projected(0, g, i)
            shift_copy(act, at, 0, 0)
            shift_send(act, at, 0, 0)

            def body(b):
                for g in range(GROUPS):
                    step(b, g)

            batches(act, body)
            pv_copy(act, at, BATCH - 1, GROUPS - 1, 3)
            tanh(BATCH - 1)
            z_part(BATCH - 1)

        @block.vector
        def _(dve):
            dve.wait_ge(const_in, 96)
            dve.tensor_copy(eye[:, :], square[:, 0, :]).then_inc(const_ready, 1)
            dve.tensor_copy(eye_bf[:, :], square[:, 0, :]).then_inc(const_ready, 1)
            dve.tensor_copy(colmask[:, :], square[:, 1, :]).then_inc(const_ready, 1)

            dve.wait_ge(wo_a_made, 1)
            dve.wait_ge(zeroed, 1)
            for h in range(GH):
                rows = slice(h * HD, h * HD + HD)
                dve.tensor_copy(wo_a[rows, :, h * RANK:(h + 1) * RANK],
                                at.scores_ps[rows, 1, 0:TT * RANK].rearrange("p (t r) -> p t r", t=TT)).then_inc(wo_a_copied, 1)
            for c in range(KC):
                dve.wait_ge(w_hi, c + 1)
                dve.tensor_tensor(wo_split[:, 1, c, :], stage[2][:, c, :], wo_split[:, 0, c, :],
                                  ALU.subtract).then_inc(w_ready, 1)
            for c in range(KC):
                dve.wait_ge(w_hi, KC + c + 1)
                dve.scalar_tensor_tensor(out=low_a_split[:, 1, c, :], in0=a_full[:, c, :], scalar=lnw[:, 1, c:c + 1],
                                         in1=low_a_split[:, 0, c, :], op0=ALU.mult,
                                         op1=ALU.subtract).then_inc(w_ready, 1)
            for c in range(KC):
                dve.wait_ge(w_hi, 2 * KC + c // 2 * 2 + 2)
                dve.scalar_tensor_tensor(out=vw_split[:, 1, c, :], in0=lin_ps[:, c // 2, (c % 2) * VW:(c % 2 + 1) * VW],
                                         scalar=lnw[:, 0, c:c + 1], in1=vw_split[:, 0, c, :], op0=ALU.mult,
                                         op1=ALU.subtract).then_inc(w_ready, 1)
            for n in range(2):
                for c in range(KC):
                    dve.wait_ge(w_hi, (3 + n) * KC + c + 1)
                    dve.scalar_tensor_tensor(out=qk_split[n][:, 1, c, :], in0=stage[n][:, c, :],
                                             scalar=lnw[:, 0, c:c + 1], in1=qk_split[n][:, 0, c, :], op0=ALU.mult,
                                             op1=ALU.subtract).then_inc(w_ready, 1)

            def attn_chunk(b, c):
                dve.wait_ge(attn_hi, b * KC + c + 1)
                dve.tensor_tensor(attn_split[:, 1, c, :], wide[:, c, :], attn_split[:, 0, c, :],
                                  ALU.subtract).then_inc(attn_ready, 1)

            def adapter(b):
                dve.wait_ge(ab_hi, b * 2 + 2)
                dve.tensor_tensor(a_split[:, 1, :, :], a_stage[:, :, :], a_split[:, 0, :, :],
                                  ALU.subtract).then_inc(ab_ready, 1)
                dve.tensor_tensor(b_split[:, 1, :], b_stage[:, :], b_split[:, 0, :],
                                  ALU.subtract).then_inc(ab_ready, 1)

            def low(b):
                dve.wait_ge(low_hi, b + 1)
                dve.tensor_tensor(low_split[:, 1, :], at.scores_ps[0:RANK, 1, :], low_split[:, 0, :],
                                  ALU.subtract).then_inc(low_ready, 1)

            def add_residual(b, t):
                dve.wait_ge(o_made, b * TT + t + 1)
                dve.wait_ge(in_done[1], b * 16 + 16)
                dve.tensor_tensor(res[:, t, :], lin_ps[:, t % 2, :], res[:, t, :], ALU.add).then_inc(o_added, 1)
                dve.wait_ge(o_added, b * TT + t + 1)
                dve.bn_stats(stats[:, t, :], res[:, t, :]).then_inc(stats_done, 1)

            def norm_factors(b):
                done = b * LN_STEPS
                apart(dve, at.ones_set, stats_done, (b + 1) * TT)
                for t in range(TT):
                    dve.bn_aggr(mean_var[:, t, :], stats[:, t, :]).then_inc(ln_step, 1)
                dve.wait_ge(ln_step, done + TT)
                dve.tensor_scalar(squares[:, 0, :], mean_var[:, :, 1], LN_EPS, None, ALU.add).then_inc(ln_step, 1)
                dve.wait_ge(ln_step, done + TT + 1)
                dve.reciprocal(newton[:, 0, :], squares[:, 0, :]).then_inc(ln_step, 1)
                dve.wait_ge(ln_step, done + TT + 2)
                dve.tensor_tensor(newton[:, 1, :], newton[:, 0, :], mean_var[:, :, 1], ALU.mult).then_inc(ln_step, 1)
                dve.wait_ge(ln_step, done + TT + 3)
                dve.tensor_scalar(squares[:, 1, :], newton[:, 1, :], RMS_EPS, None, ALU.add).then_inc(ln_step, 1)
                dve.wait_ge(ln_step, done + TT + 4)
                rsqrt(dve, ln_step, done + TT + 4, inv_root[:, :, :], squares[:, :, :], newton[:, :, :])

            def normalise_tile(b, t):
                dve.wait_ge(ln_step, b * LN_STEPS + TT + 4 + RSQRT_STEPS)
                dve.tensor_scalar(res[:, t, :], res[:, t, :], mean_var[:, t, 0:1], inv_root[:, 0, t:t + 1],
                                  ALU.subtract, ALU.mult).then_inc(x1_ready, 1)
                if t == 0:
                    dve.wait_ge(attn_ready, (b + 1) * KC)
                dve.wait_ge(x1_ready, b * TT + t + 1)
                dve.tensor_scalar(wide[:, t, :], res[:, t, :], inv_root[:, 1, t:t + 1], None,
                                  ALU.mult).then_inc(h_ready, 1)

            def h_tile(b, t):
                dve.wait_ge(h_hi, b * TT + t + 1)
                dve.tensor_tensor(h_split[:, 1, :, t * P:t * P + P],
                                  lin_ps[:, t % 2, :].rearrange("p (c n) -> p c n", c=KC),
                                  h_split[:, 0, :, t * P:t * P + P], ALU.subtract).then_inc(h_split_ready, 1)

            def projected(b, g, i):
                dve.wait_ge(qk_hi[i], number(b, g) + 1)
                split = at.k_split if i else at.q_split
                dve.tensor_tensor(split[:, 1, :], lin_ps[:, i, :], split[:, 0, :],
                                  ALU.subtract).then_inc(qk_ready[i], 1)

            def value(b, t):
                dve.wait_ge(value_hi, b * TT + t + 1)
                dve.tensor_tensor(at.value[:, t, :, RANK:2 * RANK],
                                  lin_ps[:, t % 2, 0:VW].rearrange("p (h d) -> p h d", d=RANK),
                                  at.value[:, t, :, 0:RANK], ALU.subtract).then_inc(at.value_ready, 1)

            def invert(b, g):
                n = number(b, g)
                dve.wait_ge(at.gathered, n * 48 + 48)
                at_least(dve, inverse_out, n * 16)
                dve.reciprocal(inverse[:, :], sums[:, :]).then_inc(inverted, 1)

            def z_term(b):
                dve.wait_ge(mod_done, b + 1)
                dve.wait_ge(h_low_copied, b + 1)
                dve.scalar_tensor_tensor(out=mod[:, :], in0=mod[:, :], scalar=MOD_SCALE, in1=h_low[:, :],
                                         op0=ALU.mult, op1=ALU.mult).then_inc(z_made, 1)

            def z_part(b):
                dve.wait_ge(z_hi, b + 1)
                dve.tensor_tensor(z_split[:, 1, :], mod[:, :], z_split[:, 0, :], ALU.subtract).then_inc(z_ready, 1)

            def step(b, g):
                last = is_last(b)
                zero = isinstance(b, int) and b == 0
                first = zero and g == 0
                q_from, k_from, k_to = QK_SLOTS_B[g]
                for slot in range(UNITS):
                    if slot > 0:
                        lo_unit(dve, at, b, g, slot - 1)
                    elif not first:
                        lo_unit(dve, at, *group(b, g, -1), UNITS - 1)
                    if not (last and g == GROUPS - 1):
                        for k in score_share(slot):
                            score_max(dve, at, rowmask, *group(b, g, 1), k)
                        if slot == SCORE_SLOTS[-1]:
                            shift_split(dve, at, *group(b, g, 1))
                    if slot == 5 and not first:
                        invert(*group(b, g, -1))
                    if g == 0 and 1 <= slot <= TT:
                        value(b, slot - 1)
                    if g == 0 and not last:
                        if 4 <= slot < 8:
                            attn_chunk(b + 1, slot - 4)
                        if slot == 7:
                            adapter(b + 1)
                        if slot == 11:
                            low(b + 1)
                    if g == 1 and not zero:
                        if slot == 3:
                            z_term(b - 1)
                        if slot == 5:
                            z_part(b - 1)
                    if g == 1 and not last:
                        if slot in (2, 3, 5, 6):
                            add_residual(b + 1, (2, 3, 5, 6).index(slot))
                        if slot == 7:
                            norm_factors(b + 1)
                        if slot >= 8:
                            normalise_tile(b + 1, slot - 8)
                    if g == 2 and 1 <= slot < 5 and not last:
                        h_tile(b + 1, slot - 1)
                    if not (last and g >= 2):
                        if slot == k_from + 1:
                            projected(*group(b, g, 2), 0)
                        if slot == k_to + 1:
                            projected(*group(b, g, 2), 1)

            for c in range(KC):
                attn_chunk(0, c)
            adapter(0)
            low(0)
            for t in range(TT):
                add_residual(0, t)
            norm_factors(0)
            for t in range(TT):
                normalise_tile(0, t)
            for t in range(TT):
                h_tile(0, t)
            for g in range(2):
                for i in range(2):
                    projected(0, g, i)
            for k in range(UNITS):
                score_max(dve, at, rowmask, 0, 0, k)
            shift_split(dve, at, 0, 0)

            def body(b):
                for g in range(GROUPS):
                    step(b, g)

            batches(dve, body)
            lo_unit(dve, at, BATCH - 1, GROUPS - 1, UNITS - 1)
            invert(BATCH - 1, GROUPS - 1)
            z_term(BATCH - 1)
            z_part(BATCH - 1)

        @block.tensor
        def _(pe):
            pe.wait_ge(const_in, 96)
            pe.wait_ge(stage_in[0], 16)
            for t in range(TT):
                for c in range(KC):
                    mm = pe.matmul(at.scores_ps[:, 1, t * RANK:(t + 1) * RANK], stage[0][:, c, t * P:t * P + P], a_full[:, c, :],
                                   start=(t == 0 and c == 0), stop=(c == KC - 1), skip_group_check=True)
            mm.then_inc(wo_a_made, 1)
            pe.wait_ge(wo_a_copied, GH)
            pe.wait_ge(stage_in[1], 16)
            for c in range(KC):
                for t in range(TT):
                    mm = pe.matmul(lin_ps[:, c // 2, (c % 2) * VW + t * GH * RANK:(c % 2) * VW + (t + 1) * GH * RANK],
                                   stage[1][:, t, c * P:c * P + P], wo_a[:, t, :], start=(c % 2 == 0 and t == 0),
                                   stop=True, skip_group_check=True)
                if c % 2 == 1:
                    mm.then_inc(vw_made, 1)
            pe.wait_ge(const_ready, 3)
            pe.wait_ge(at.ones_set, 3)

            def low(b, items):
                for x in items:
                    c, (w, a) = x // 3, PASSES[x % 3]
                    if x == 0:
                        at_least(pe, at.score_read, ((b - 1) * GROUPS + 2) * UNITS)
                        pe.wait_ge(attn_ready, (b + 1) * KC)
                        pe.wait_ge(ab_ready, (b + 1) * 2)
                    mm = pe.matmul(at.scores_ps[0:RANK, 1, :], a_split[:, w, c, :], attn_split[:, a, c, :],
                                   start=(x == 0), stop=(x == 3 * KC - 1))
                    if x == 3 * KC - 1:
                        mm.then_inc(low_made, 1)

            def project_out(b, items):
                for x in items:
                    t, y = divmod(x, 3 * KC + 1)
                    bank = t % 2
                    if y == 0 and t < 2 and not (isinstance(b, int) and b == 0):
                        pe.wait_ge(qk_ready[bank], b * GROUPS - 1)
                    if y == 0 and t >= 2:
                        pe.wait_ge(o_added, b * TT + t - 1)
                    if y < 3 * KC:
                        c, (w, a) = y // 3, PASSES[y % 3]
                        pe.matmul(lin_ps[:, bank, :], attn_split[:, a, c, t * P:t * P + P], wo_split[:, w, c, :],
                                  start=(y == 0), stop=False)
                    else:
                        pe.wait_ge(low_stacked, b * 48 + 48)
                        pe.wait_ge(b_stacked, b * 48 + 48)
                        pe.matmul(lin_ps[:, bank, :], low_stack[:, t * P:t * P + P], b_stack[:, :],
                                  start=False, stop=True).then_inc(o_made, 1)

            def turn_h(b, t):
                bank = t % 2
                pe.wait_ge(h_ready, b * TT + t + 1)
                if t >= 2:
                    pe.wait_ge(h_split_ready, b * TT + t - 1)
                elif isinstance(b, int) and b == 0:
                    pe.wait_ge(o_added, 3 + t)
                else:
                    pe.wait_ge(qk_ready[bank], b * GROUPS)
                for c in range(KC):
                    mm = pe.transpose(lin_ps[:, bank, c * P:c * P + P], wide[:, t, c * P:c * P + P], eye[:, :].bitcast(F32))
                mm.then_inc(h_turned, 1)

            def project(b, g, i, items):
                for x in items:
                    if x == 0:
                        if g == 0:
                            pe.wait_ge(h_split_ready, (b + 1) * TT)
                        elif g == 2:
                            pe.wait_ge(at.value_ready, b * TT + 3 + i)
                        elif g == 3 and not is_last(b):
                            pe.wait_ge(o_added, (b + 1) * TT + 3 + i)
                        else:
                            pe.wait_ge(qk_ready[i], number(b, g))
                    c, (w, a) = x // 3, PASSES[x % 3]
                    mm = pe.matmul(lin_ps[:, i, :], qk_split[i][:, w, c, g * P:g * P + P], h_split[:, a, c, :],
                                   start=(x == 0), stop=(x == 3 * KC - 1))
                    if x == 3 * KC - 1:
                        mm.then_inc(qk_made[i], 1)

            def project_value(b, t):
                bank = t % 2
                if t < 2:
                    pe.wait_ge(qk_ready[bank], b * GROUPS + 2)
                else:
                    pe.wait_ge(at.value_ready, b * TT + t - 1)
                for x in range(3 * KC):
                    c, (w, a) = x // 3, PASSES[x % 3]
                    mm = pe.matmul(lin_ps[:, bank, 0:VW], h_split[:, a, c, t * P:t * P + P], vw_split[:, w, c, :],
                                   start=(x == 0), stop=(x == 3 * KC - 1))
                mm.then_inc(v_made, 1)

            def h_times_a(b):
                pe.wait_ge(at.score_read, (b * GROUPS + 3) * UNITS)
                for x in range(3 * KC):
                    c, (w, a) = x // 3, PASSES[x % 3]
                    mm = pe.matmul(at.scores_ps[0:RANK, 1, :], low_a_split[:, w, c, :], h_split[:, a, c, :],
                                   start=(x == 0), stop=(x == 3 * KC - 1))
                mm.then_inc(h_low_made, 1)

            def modulation(b):
                apart(pe, at.ones_set, added, (b + 1) * GROUPS)
                apart(pe, at.ones_set, low_ready, min(b + 3, BATCH) if isinstance(b, int) else b + 3)
                pe.matmul(at.scores_ps[0:RANK, 1, :], sel[:, :], out_sum[:, :], start=True, stop=True).then_inc(mod_made, 1)

            def step(b, g):
                last = is_last(b)
                zero = isinstance(b, int) and b == 0
                first = zero and g == 0
                q_from, k_from, k_to = QK_SLOTS_B[g]
                for slot in range(UNITS):
                    score_t_unit(pe, at, eye_bf, colmask, b, g, slot)
                    if slot == 9 and not (last and g == GROUPS - 1):
                        shift_turn(pe, at, eye, *group(b, g, 1))
                    if slot == 2 and g == 1:
                        if zero:
                            pe.wait_ge(low_ready, 2)
                        else:
                            pe.wait_ge(mod_done, b)
                    if slot == 2 and g == 2:
                        pe.wait_ge(h_low_copied, b + 1)
                    if not (last and g == GROUPS - 1):
                        for k in score_share(slot):
                            score_unit(pe, at, *group(b, g, 1), k)
                    if slot < 2 and not first:
                        pv_unit(pe, at, *group(b, g, -1), UNITS - 2 + slot)
                    if g == 0 and slot < TT:
                        project_value(b, slot)
                    if g == 0 and slot in (8, 9) and not last:
                        low(b + 1, share(3 * KC, 2, slot - 8))
                    if g == 1 and slot == 1 and not zero:
                        modulation(b - 1)
                    if g == 1 and 1 <= slot < 7 and not last:
                        project_out(b + 1, share(TT * (3 * KC + 1), 6, slot - 1))
                    if g == 2 and slot < TT and not last:
                        turn_h(b + 1, slot)
                    if not (last and g >= 2):
                        ahead = group(b, g, 2)
                        if q_from <= slot < k_from:
                            project(*ahead, 0, share(3 * KC, k_from - q_from, slot - q_from))
                        if k_from <= slot < k_to:
                            project(*ahead, 1, share(3 * KC, k_to - k_from, slot - k_from))
                    if slot >= 2:
                        pv_unit(pe, at, b, g, slot - 2)
                    if g == 1 and slot == 10:
                        h_times_a(b)

            pe.wait_ge(w_ready, 5 * KC)
            low(0, range(3 * KC))
            project_out(0, range(TT * (3 * KC + 1)))
            for t in range(TT):
                turn_h(0, t)
            for g in range(2):
                for i in range(2):
                    project(0, g, i, range(3 * KC))
            for k in range(UNITS):
                score_unit(pe, at, 0, 0, k)
            shift_turn(pe, at, eye, 0, 0)

            def body(b):
                for g in range(GROUPS):
                    step(b, g)

            batches(pe, body)
            for k in range(UNITS - 2, UNITS):
                pv_unit(pe, at, BATCH - 1, GROUPS - 1, k)
            modulation(BATCH - 1)


FT = F // 2 // P
W_COLS = 2 * KC * P + D


class Run:

    def __init__(self, n, pair, used):
        self.n, self.pair, self.used = n, pair, used

    def next(self):
        return Run(self.n + 1, 1 - self.pair, self.used + self.pair)

    def former(self):
        return Run(self.n - 1, 1 - self.pair, self.used + self.pair - 1)

    def is_(self, n):
        return isinstance(self.n, int) and self.n == n


def runs(eng, body):
    for second in range(2):
        first = second * BATCH
        body(Run(first, 0, first // 2), second)
        with eng.Fori(0, BATCH // 2 - 1) as i:
            body(Run(i * 2 + (first + 1), 1, i + first // 2), second)
            body(Run(i * 2 + (first + 2), 0, i + (first // 2 + 1)), second)
        body(Run(first + BATCH - 1, 1, (first + BATCH) // 2 - 1), second)


def mlp_layer(nc, mlp_w, low_b, ln_w, x1_hbm, h_hbm, z_hbm, out):
    with ExitStack() as ctx:
        def sb(what, shape, dt=F32):
            return ctx.enter_context(nc.sbuf_tensor(f"c_{what}", shape, dt))

        def sem(what):
            return ctx.enter_context(nc.semaphore(f"c_{what}"))

        gate_ps = ctx.enter_context(nc.psum_tensor("c_gate_ps", [P, 2, SEQ], F32))
        up_ps = ctx.enter_context(nc.psum_tensor("c_up_ps", [P, 2, SEQ], F32))
        down_ps = ctx.enter_context(nc.psum_tensor("c_down_ps", [P, TT, D], F32))

        w_split = sb("w_split", [P, 2, FT, W_COLS], F32R)
        w_stage = sb("w_stage", [P, 2, W_COLS])
        lnw = sb("lnw", [P, 2, KC])
        low_b_stage = sb("low_b_stage", [P, RANK * F // P])
        low_b_split = sb("low_b_split", [P, 2, RANK * F // P], F32R)
        low_b_stack = sb("low_b_stack", [3 * RANK, F], F32R)
        z_stack = [sb(f"z_stack{i}", [3 * RANK, SEQ], F32R) for i in range(2)]
        h_stage = sb("h_stage", [P, KC, SEQ])
        h_split = [sb(f"h_split{i}", [P, 2, KC, SEQ], F32R) for i in range(2)]
        res = [sb(f"res{i}", [P, TT, D]) for i in range(2)]
        gate = sb("gate", [P, 2, SEQ])
        product = sb("product", [P, 2, SEQ])
        product_split = sb("product_split", [P, 2, 2, SEQ], F32R)
        stats = sb("stats", [P, TT, 6])
        mean_var = sb("mean_var", [P, TT, 2])
        var_eps = sb("var_eps", [P, TT])
        inv_root = sb("inv_root", [P, TT])
        newton = sb("newton", [P, TT])

        const_in = sem("const_in")
        b_hi = sem("b_hi")
        b_ready = sem("b_ready")
        b_stacked = sem("b_stacked")
        w_in = [sem(f"w_in{i}") for i in range(2)]
        w_hi = sem("w_hi")
        w_ready = sem("w_ready")
        h_in = sem("h_in")
        h_hi = sem("h_hi")
        h_ready = sem("h_ready")
        z_in = [sem(f"z_in{i}") for i in range(2)]
        res_in = [sem(f"res_in{i}") for i in range(2)]
        res_out = [sem(f"res_out{i}") for i in range(2)]
        gate_made = sem("gate_made")
        up_made = sem("up_made")
        gate_done = sem("gate_done")
        product_done = sem("product_done")
        product_hi = sem("product_hi")
        product_ready = sem("product_ready")
        down_done = sem("down_done")
        res_added = sem("res_added")
        ln_step = sem("ln_step")
        normalised = sem("normalised")

        LN_STEPS = 2 * TT + 1 + RSQRT_STEPS
        RUNS = 2 * BATCH

        block = ctx.enter_context(nc.Block())

        @block.gpsimd
        def _(pool):
            for k in range(2 * FT):
                if k >= 2:
                    pool.wait_ge(w_ready, k - 1)
                pool.dma_start(w_stage[:, k % 2, :], mlp_w[k]).then_inc(w_in[k % 2], 16)

        @block.sync
        def _(sp):
            def load_h(run, rows):
                at_least(sp, h_ready, run.n * KC)
                sp.dma_start(h_stage[:, :, :], h_hbm[:, :, rows]).then_inc(h_in, 16)

            def load_z(run, rows):
                at_least(sp, gate_made, (run.n - 1) * FT)
                for r, part in enumerate((0, 0, 1)):
                    sp.dma_start(z_stack[run.pair][RANK * r:RANK * (r + 1), :].bitcast(F32),
                                 z_hbm[part, :, rows]).then_inc(z_in[run.pair], 16)

            def load_res(run, rows):
                at_least(sp, res_out[run.pair], run.used * 16)
                sp.dma_start(res[run.pair][:, :, :],
                             x1_hbm[rows, :].rearrange("(t p) d -> p t d", p=P)).then_inc(res_in[run.pair], 16)

            def store(run, rows, second):
                if second:
                    sp.wait_ge(normalised, (run.n - BATCH + 1) * TT)
                else:
                    sp.wait_ge(res_added, (run.n + 1) * TT)
                sp.dma_start((out if second else x1_hbm)[rows, :].rearrange("(t p) d -> p t d", p=P),
                             res[run.pair][:, :, :]).then_inc(res_out[run.pair], 16)

            def rows_of(n, second):
                return bass.ds((n - BATCH) * SEQ if second else n * SEQ, SEQ)

            def body(run, second):
                following = run.next()
                next_second = second or run.is_(BATCH - 1)
                if not run.is_(RUNS - 1):
                    load_h(following, rows_of(following.n, next_second))
                    load_z(following, rows_of(following.n, next_second))
                if not run.is_(0):
                    former = run.former()
                    former_second = second and not run.is_(BATCH)
                    store(former, rows_of(former.n, former_second), former_second)
                if not run.is_(RUNS - 1):
                    load_res(following, rows_of(following.n, next_second))

            start = Run(0, 0, 0)
            load_h(start, bass.ds(0, SEQ))
            sp.dma_start(lnw[:, :, :], ln_w).then_inc(const_in, 16)
            sp.dma_start(low_b_stage[:, :], low_b).then_inc(const_in, 16)
            load_z(start, bass.ds(0, SEQ))
            load_res(start, bass.ds(0, SEQ))
            sp.wait_ge(b_ready, 1)
            for r, part in enumerate((0, 1, 0)):
                sp.dma_start(low_b_stack[RANK * r:RANK * (r + 1), :].bitcast(F32),
                             low_b_split[:, part, :].bitcast(F32)).then_inc(b_stacked, 16)
            runs(sp, body)
            end = Run(RUNS - 1, 1, BATCH - 1)
            store(end, rows_of(end.n, True), True)
            for i in range(2):
                sp.wait_ge(res_out[i], BATCH * 16)

        def weight_splits(run, ft):
            if run.is_(0) and ft + 2 < FT:
                return (ft + 2,)
            if run.is_(BATCH - 1) and ft >= 2:
                return (FT + ft - 2,)
            if run.is_(BATCH) and ft < 2:
                return (2 * FT - 2 + ft,)
            return ()

        @block.scalar
        def _(act):
            def weights(k):
                act.wait_ge(w_in[k % 2], (k // 2 + 1) * 16)
                kt = k % FT
                if k >= FT:
                    act.wait_ge(down_done, ((BATCH - 1) * FT + kt + 1) * TT)
                for c in range(KC):
                    cols = slice(c * 2 * P, (c + 1) * 2 * P)
                    act.activation(w_split[:, 0, kt, cols], w_stage[:, k % 2, cols], ACT.Copy, scale=lnw[:, 1, c:c + 1])
                act.activation(w_split[:, 0, kt, 2 * KC * P:], w_stage[:, k % 2, 2 * KC * P:],
                               ACT.Copy).then_inc(w_hi, 1)

            def h_chunk(run, c):
                if c == 0:
                    act.wait_ge(h_in, run.n * 16 + 16)
                    at_least(act, up_made, (run.n - 1) * FT)
                act.activation(h_split[run.pair][:, 0, c, :], h_stage[:, c, :], ACT.Copy).then_inc(h_hi, 1)

            def body(run, second):
                for ft in range(FT):
                    p = run.n * FT + ft
                    bank = ft % 2
                    act.wait_ge(gate_made, p + 1)
                    at_least(act, product_done, p - 1)
                    act.activation(gate[:, bank, :], gate_ps[:, bank, :], ACT.Silu).then_inc(gate_done, 1)
                    act.wait_ge(product_done, p + 1)
                    at_least(act, down_done, (p - 1) * TT)
                    act.activation(product_split[:, bank, 0, :], product[:, bank, :], ACT.Copy).then_inc(product_hi, 1)
                    if 2 <= ft < 2 + KC and not run.is_(RUNS - 1):
                        h_chunk(run.next(), ft - 2)
                    for k in weight_splits(run, ft):
                        weights(k)

            start = Run(0, 0, 0)
            act.wait_ge(const_in, 32)
            weights(0)
            for c in range(KC):
                h_chunk(start, c)
            act.activation(low_b_split[:, 0, :], low_b_stage[:, :], ACT.Copy).then_inc(b_hi, 1)
            weights(1)
            runs(act, body)

        @block.vector
        def _(dve):
            def weights(k):
                dve.wait_ge(w_hi, k + 1)
                kt = k % FT
                for c in range(KC):
                    cols = slice(c * 2 * P, (c + 1) * 2 * P)
                    dve.scalar_tensor_tensor(out=w_split[:, 1, kt, cols], in0=w_stage[:, k % 2, cols],
                                             scalar=lnw[:, 1, c:c + 1], in1=w_split[:, 0, kt, cols], op0=ALU.mult,
                                             op1=ALU.subtract)
                dve.tensor_tensor(w_split[:, 1, kt, 2 * KC * P:], w_stage[:, k % 2, 2 * KC * P:],
                                  w_split[:, 0, kt, 2 * KC * P:], ALU.subtract).then_inc(w_ready, 1)

            def h_chunk(run, c):
                dve.wait_ge(h_hi, run.n * KC + c + 1)
                dve.tensor_tensor(h_split[run.pair][:, 1, c, :], h_stage[:, c, :], h_split[run.pair][:, 0, c, :],
                                  ALU.subtract).then_inc(h_ready, 1)

            def add(run, second):
                dve.wait_ge(res_in[run.pair], run.used * 16 + 16)
                for t in range(TT):
                    dve.wait_ge(down_done, ((run.n + 1) * FT - 1) * TT + t + 1)
                    dve.scalar_tensor_tensor(out=res[run.pair][:, t, :], in0=res[run.pair][:, t, :],
                                             scalar=1.0 if second else 2.0, in1=down_ps[:, t, :], op0=ALU.mult,
                                             op1=ALU.add).then_inc(res_added, 1)

            def norm_factors(run):
                m = run.n - BATCH
                done = m * LN_STEPS
                for t in range(TT):
                    dve.wait_ge(res_added, run.n * TT + t + 1)
                    dve.bn_stats(stats[:, t, :], res[run.pair][:, t, :]).then_inc(ln_step, 1)
                apart(dve, const_in, ln_step, done + TT)
                for t in range(TT):
                    dve.bn_aggr(mean_var[:, t, :], stats[:, t, :]).then_inc(ln_step, 1)
                dve.wait_ge(ln_step, done + 2 * TT)
                dve.tensor_scalar(var_eps[:, :], mean_var[:, :, 1], LN_EPS, None, ALU.add).then_inc(ln_step, 1)
                dve.wait_ge(ln_step, done + 2 * TT + 1)
                rsqrt(dve, ln_step, done + 2 * TT + 1, inv_root[:, :], var_eps[:, :], newton[:, :])

            def normalise(run):
                m = run.n - BATCH
                dve.wait_ge(ln_step, (m + 1) * LN_STEPS)
                for t in range(TT):
                    dve.tensor_scalar(res[run.pair][:, t, :], res[run.pair][:, t, :], mean_var[:, t, 0:1],
                                      inv_root[:, t:t + 1], ALU.subtract, ALU.mult).then_inc(normalised, 1)

            def body(run, second):
                former_second = second and not run.is_(BATCH)
                for ft in range(FT):
                    p = run.n * FT + ft
                    bank = ft % 2
                    if ft == 1 and not run.is_(0):
                        add(run.former(), former_second)
                    dve.wait_ge(gate_done, p + 1)
                    dve.wait_ge(up_made, p + 1)
                    dve.tensor_tensor(product[:, bank, :], up_ps[:, bank, :], gate[:, bank, :],
                                      ALU.mult).then_inc(product_done, 1)
                    dve.wait_ge(product_hi, p + 1)
                    dve.tensor_tensor(product_split[:, bank, 1, :], product[:, bank, :], product_split[:, bank, 0, :],
                                      ALU.subtract).then_inc(product_ready, 1)
                    if former_second and ft == 1:
                        norm_factors(run.former())
                    if former_second and ft == 2:
                        normalise(run.former())
                    if 2 <= ft < 2 + KC and not run.is_(RUNS - 1):
                        h_chunk(run.next(), ft - 2)
                    for k in weight_splits(run, ft):
                        weights(k)

            start = Run(0, 0, 0)
            dve.wait_ge(const_in, 32)
            weights(0)
            for c in range(KC):
                h_chunk(start, c)
            dve.wait_ge(b_hi, 1)
            dve.tensor_tensor(low_b_split[:, 1, :], low_b_stage[:, :], low_b_split[:, 0, :],
                              ALU.subtract).then_inc(b_ready, 1)
            weights(1)
            runs(dve, body)
            end = Run(RUNS - 1, 1, BATCH - 1)
            add(end, True)
            norm_factors(end)
            normalise(end)

        @block.tensor
        def _(pe):
            def down(p, kt, n):
                pe.wait_ge(product_ready, p + 1)
                for t in range(TT):
                    if kt == 0:
                        at_least(pe, res_added, (n - 1) * TT + t + 1)
                    for i, (w, a) in enumerate(PASSES):
                        mm = pe.matmul(down_ps[:, t, :], product_split[:, kt % 2, a, t * P:t * P + P],
                                       w_split[:, w, kt, 2 * KC * P:], start=(kt == 0 and i == 0),
                                       stop=(kt == FT - 1 and i == 2), skip_group_check=True)
                    mm.then_inc(down_done, 1)

            def body(run, second):
                for ft in range(FT):
                    p = run.n * FT + ft
                    bank = ft % 2
                    if ft == 0:
                        pe.wait_ge(h_ready, run.n * KC + KC)
                    if run.is_(0) or run.is_(BATCH):
                        pe.wait_ge(w_ready, second * FT + ft + 1)
                    at_least(pe, gate_done, p - 1)
                    for c in range(KC):
                        for w, a in PASSES:
                            pe.matmul(gate_ps[:, bank, :], w_split[:, w, ft, c * 2 * P:c * 2 * P + P],
                                      h_split[run.pair][:, a, c, :], start=(c == 0 and w == 0 and a == 0), stop=False)
                    if ft == 0:
                        pe.wait_ge(z_in[run.pair], run.used * 48 + 48)
                        if run.is_(0):
                            pe.wait_ge(b_stacked, 48)
                    k = second * FT + ft
                    pe.matmul(gate_ps[:, bank, :], low_b_stack[:, k * P:k * P + P], z_stack[run.pair][:, :],
                              start=False, stop=True).then_inc(gate_made, 1)
                    at_least(pe, product_done, p - 1)
                    for c in range(KC):
                        for w, a in PASSES:
                            mm = pe.matmul(up_ps[:, bank, :], w_split[:, w, ft, c * 2 * P + P:(c + 1) * 2 * P],
                                           h_split[run.pair][:, a, c, :], start=(c == 0 and w == 0 and a == 0),
                                           stop=(c == KC - 1 and (w, a) == PASSES[2]))
                    mm.then_inc(up_made, 1)
                    if ft > 0:
                        down(p - 1, ft - 1, run.n)
                    elif not run.is_(0):
                        down(p - 1, FT - 1, run.n - 1)

            runs(pe, body)
            down(RUNS * FT - 1, FT - 1, RUNS - 1)


def tables():
    inv_freq = np.float32(10000.0) ** (-np.arange(0, HD, 2, dtype=np.float32) / np.float32(HD))
    angle = np.arange(SEQ, dtype=np.float32)[None, :] * inv_freq[:, None].astype(np.float32)
    dim = np.arange(P) % (2 * HD) // 2
    out = np.zeros((P, CONSTS), np.float32)
    out[:, COS:COS + SEQ] = np.cos(angle)[dim // 2]
    out[:, SIN:SIN + SEQ] = np.sin(angle)[dim // 2] * np.where(dim % 2 == 0, -1.0, 1.0)[:, None]
    out[:, EYE:EYE + P] = np.eye(P)
    out[:, ROWMASK + SEQ - P:ROWMASK + SEQ] = np.triu(np.full((P, P), NEG), 1)
    out[:, COLMASK:COLMASK + P] = np.tril(np.full((P, P), NEG), -1)
    out[:, COUNT:COUNT + 8] = np.arange(8)
    return out


def chunked(w):
    return w.reshape(-1, P, w.shape[1]).transpose(1, 0, 2)


def by_dimension(w):
    return w.reshape(GROUPS, GH, -1, w.shape[1]).transpose(0, 2, 1, 3).reshape(w.shape)


def by_pair(w):
    return w.reshape(HEADS // 2, 2, -1, w.shape[1]).transpose(0, 2, 1, 3).reshape(w.shape)


def layout(**t):
    a = {k: np.asarray(v) for k, v in t.items()}
    one = {k[len("L0_attn_"):]: v for k, v in a.items() if k.startswith("L0_attn_")}
    two = {k[len("L0_ffn_"):]: v for k, v in a.items() if k.startswith("L0_ffn_")}
    b_q, b_k = (np.stack([by_pair(m) for m in one[n]]) for n in ("Bq", "Bk"))
    out = {
        "x_t": chunked(one["x"].reshape(-1, D).T),
        "wq_t": chunked(by_pair(one["Wq"]).T),
        "wk_t": chunked(by_pair(one["Wk"]).T),
        "wv_t": chunked(one["Wv"].T),
        "a_qkv": np.stack([one["Aq"], one["Ak"], one["Av"]], 2).transpose(0, 3, 1, 2).reshape(
            ADAPTERS, KC, P, 3 * RANK).transpose(0, 2, 1, 3),
        "b_qkv": np.stack([b_q, b_k, one["Bv"]], 1).transpose(0, 3, 1, 2).reshape(ADAPTERS, P, -1),
        "starts": one["lora_start_indices"].reshape(1, -1),
        "x": one["x"].reshape(-1, D),
        "wo_t": chunked(by_dimension(one["Wo"].T)),
        "a_o": np.stack([chunked(by_dimension(m.T)) for m in one["Ao"]]),
        "b_o": one["Bo"].transpose(0, 2, 1).reshape(ADAPTERS, P, -1),
        "wq2_t": chunked(by_pair(two["Wq"]).T),
        "wk2_t": chunked(by_pair(two["Wk"]).T),
        "wv2": chunked(two["Wv"]),
        "wo2": chunked(two["Wo"]),
        "low_a": chunked(two["A"]),
        "mlp_w": np.concatenate([np.stack([chunked(two[n].T).reshape(P, KC, F // P, P) for n in (
            "W_in_base", "W_up_base")], 3).transpose(2, 0, 1, 3, 4).reshape(F // P, P, -1),
            two["W_down"].T.reshape(F // P, P, D)], 2),
        "low_b": two["B"].reshape(P, -1),
        "ln_w": np.stack([two["ln1_w"].reshape(KC, P).T, two["ln2_w"].reshape(KC, P).T], 1),
        "selector": np.repeat(np.eye(RANK, dtype=np.float32), GH, 0),
        "consts": tables(),
    }
    return {k: np.ascontiguousarray(v) for k, v in out.items()}


def build(nc, t, out):
    def scratch(name, shape):
        return nc.dram_tensor(name, shape, F32, kind="Internal").ap()

    sums = scratch("softmax_sums", [GH, SEQ])
    attn = scratch("attention_t", [P, KC, BATCH * SEQ])
    x1 = scratch("x1", [BATCH * SEQ, D])
    h = scratch("h_t", [P, KC, BATCH * SEQ])
    z = scratch("z", [2, RANK, BATCH * SEQ])
    with nc.sbuf_tensor("adapter_ids", [1, BATCH], I32) as ids:
        attention_layer(nc, t["x_t"], t["wq_t"], t["wk_t"], t["wv_t"], t["a_qkv"], t["b_qkv"], t["starts"],
                        t["consts"], sums, attn, ids)
        gate_layer(nc, t["x"], attn, t["wo_t"], t["a_o"], t["b_o"], t["wq2_t"], t["wk2_t"], t["wv2"], t["wo2"],
                   t["low_a"], t["ln_w"], t["selector"], t["consts"], ids, sums, x1, h, z)
        mlp_layer(nc, t["mlp_w"], t["low_b"], t["ln_w"], x1, h, z, out)


def kernel(**inputs):
    import concourse.bacc as bacc
    from concourse.bass_utils import run_bass_kernel_spmd

    arrays = {f"in_{k}": v for k, v in layout(**inputs).items()}
    nc = bacc.Bacc("TRN2", target_bir_lowering=False, num_devices=1)
    t = {k[len("in_"):]: nc.dram_tensor(k, v.shape, mybir.dt.from_np(v.dtype), kind="ExternalInput").ap()
         for k, v in arrays.items()}
    out = nc.dram_tensor("out_0_dram", [BATCH * SEQ, D], F32, kind="ExternalOutput").ap()
    build(nc, t, out)
    r = run_bass_kernel_spmd(nc, [arrays], core_ids=[0])
    return r.results[0]["out_0_dram"].reshape(BATCH, SEQ, D)
```

```python
from contextlib import ExitStack

import numpy as np

import concourse.bass as bass
from concourse import mybir
from concourse.alu_op_type import AluOpType as ALU

F32 = mybir.dt.float32
F32R = mybir.dt.float32r
BF16 = mybir.dt.bfloat16
I32 = mybir.dt.int32
ACT = mybir.ActivationFunctionType

P = 128
BATCH, SEQ, D = 8, 512, 512
HEADS, HD = 16, 32
F = 2048
RANK = 16
ADAPTERS = 4
KC = D // P
TT = SEQ // P
GROUPS, GH = 4, 4
UNITS = 3 * GH
SCALE = float(HD) ** -0.5
NEG = -1.0e30
LN_EPS, RMS_EPS, MOD_SCALE = 1e-5, 1e-6, 0.1
RSQRT_MAGIC = float(0x5F3759DF)

PASSES = ((0, 0), (0, 1), (1, 0))
HI_FIRST = ((0, 0), (1, 0), (0, 1))

KEY_MAJOR = (((0, 0, 512),), ((1, 0, 384),), ((2, 0, 256), (3, 256, 128)))
QUERY_MAJOR = (((3, 0, 512),), ((2, 0, 384),), ((1, 0, 256), (0, 256, 128)))
WIDTH = (512, 384, 384)

COS, SIN, EYE, ROWMASK, COLMASK, COUNT = 0, 512, 1024, 1152, 1664, 1792
CONSTS = 1800


def at_least(eng, sem, value):
    if not isinstance(value, int) or value > 0:
        eng.wait_ge(sem, value)


def apart(eng, met, sem, value):
    if isinstance(value, int):
        at_least(eng, sem, value)
    else:
        eng.compute_val(value)
        eng.wait_ge(met, 1)
        eng.wait_ge(sem, value)


def batches(eng, body, ahead=1):
    body(0)
    with eng.Fori(1, BATCH - ahead) as b:
        body(b)
    for b in range(BATCH - ahead, BATCH):
        body(b)


def has(b, ahead):
    return not isinstance(b, int) or b + ahead < BATCH


def is_last(b):
    return not has(b, 1)


class Shared:

    def __init__(self, nc, ctx):
        def sb(what, shape, dt=F32):
            return ctx.enter_context(nc.sbuf_tensor(what, shape, dt))

        self.ids = sb("adapter_ids", [1, BATCH], I32)
        self.w_split = [sb(f"w{n}_split", [P, 2, KC, D], F32R) for n in range(3)]
        self.stage = sb("stage", [P, KC, SEQ])
        self.x_split = sb("x_split", [P, 2, KC, SEQ], F32R)
        self.rowmask = sb("rowmask", [P, SEQ])
        self.eye = sb("eye", [P, P], F32R)
        self.eye_bf = sb("eye_bf", [P, P], BF16)
        self.colmask = sb("colmask", [P, P], BF16)
        self.lnw = sb("lnw", [P, 2, KC])


class Attention:

    def __init__(self, nc, ctx, name, vd, ring, value_steps):
        def sb(what, shape, dt=F32):
            return ctx.enter_context(nc.sbuf_tensor(f"{name}_{what}", shape, dt))

        def sem(what):
            return ctx.enter_context(nc.semaphore(f"{name}_{what}"))

        self.ring = ring
        self.value_steps = value_steps
        self.vd = vd
        self.vcols = 2 * vd + 1
        self.sum_row = 2 * vd
        self.q_stack = [sb(f"q_stack{i}", [P, GH, SEQ], F32R) for i in range(2)]
        self.k_stack = [sb(f"k_stack{i}", [P, GH, SEQ], F32R) for i in range(2)]
        self.q_split = sb("q_split", [P, 2, SEQ], F32R)
        self.k_split = sb("k_split", [P, 2, SEQ], F32R)
        self.value = sb("value", [P, TT, HEADS, self.vcols], F32R)
        self.prob = sb("prob", [P, 2, SEQ])
        self.prob_hi = sb("prob_hi", [P, ring, SEQ], F32R)
        self.prob_lo = sb("prob_lo", [P, ring, SEQ], F32R)
        self.junk = sb("junk", [P, 2, SEQ], BF16)
        self.rowmax = sb("rowmax", [P, TT, GH])
        self.shift = sb("shift", [P, TT, 2 * GH], F32R)
        self.shift_row = sb("shift_row", [RANK, SEQ], F32R)
        self.pv_raw = sb("pv_raw", [P, GH, SEQ])

        self.scores_ps = ctx.enter_context(nc.psum_tensor(f"{name}_scores_ps", [P, 2, SEQ], F32))
        self.scores_t_ps = ctx.enter_context(nc.psum_tensor(f"{name}_scores_t_ps", [P, 2, SEQ], F32))
        self.pv_ps = ctx.enter_context(nc.psum_tensor(f"{name}_pv_ps", [P, 2, SEQ], F32))

        self.ones_set = sem("ones_set")
        self.q_ready = sem("q_ready")
        self.k_ready = sem("k_ready")
        self.stacked = [sem(f"stacked{i}") for i in range(2)]
        self.score_ready = sem("score_ready")
        self.score_read = sem("score_read")
        self.shift_ready = sem("shift_ready")
        self.shift_turned = sem("shift_turned")
        self.shift_copied = sem("shift_copied")
        self.shifted = sem("shifted")
        self.score_t_ready = sem("score_t_ready")
        self.exp_done = sem("exp_done")
        self.lo_done = sem("lo_done")
        self.pv_done = sem("pv_done")
        self.pv_copied = sem("pv_copied")
        self.shift_hi = sem("shift_hi")
        self.value_ready = sem("value_ready")
        self.gathered = sem("gathered")




def group(b, g, ahead=0):
    return b + (g + ahead) // GROUPS, (g + ahead) % GROUPS


def number(b, g):
    return b * GROUPS + g


def score_unit(pe, at, b, g, k):
    h, j = divmod(k, 3)
    n = number(b, g)
    if k % (UNITS // 2) == 0:
        pe.wait_ge(at.stacked[h // 2], n * 96 + 96)
    if k == 0:
        at_least(pe, at.shift_copied, n)
    at_least(pe, at.score_read, n * UNITS + k - 1)
    q, key = at.q_stack[g % 2], at.k_stack[g % 2]
    for i, (qt, col, width) in enumerate(QUERY_MAJOR[j]):
        mm = pe.matmul(at.scores_ps[:, k % 2, col:col + width], q[0:96, h, qt * P:qt * P + P],
                       key[0:96, h, 0:(qt + 1) * P], start=(i == 0), stop=True, skip_group_check=True)
    mm.then_inc(at.score_ready, 1)


def score_max(dve, at, rowmask, b, g, k):
    h, j = divmod(k, 3)
    n = number(b, g)
    apart(dve, at.ones_set, at.score_ready, n * UNITS + k + 1)
    if k == 0:
        apart(dve, at.ones_set, at.shift_ready, n)
    apart(dve, at.ones_set, at.score_read, n * UNITS + k - 1)
    for qt, col, width in QUERY_MAJOR[j]:
        last = dve.tensor_tensor_reduce(at.junk[:, k % 2, col:col + width], at.scores_ps[:, k % 2, col:col + width],
                                        rowmask[:, SEQ - width:SEQ], 1.0, 4 * NEG, ALU.add, ALU.max,
                                        at.rowmax[:, qt, h:h + 1])
    last.then_inc(at.score_read, 1)


def shift_split(dve, at, b, g):
    n = number(b, g)
    dve.wait_ge(at.score_read, (n + 1) * UNITS)
    at_least(dve, at.shift_turned, n)
    dve.tensor_scalar(at.shift[:, :, 0:GH], at.rowmax[:, :, :], -1.0, None, ALU.mult).then_inc(at.shift_hi, 1)
    dve.wait_ge(at.shift_hi, n + 1)
    dve.scalar_tensor_tensor(out=at.shift[:, :, GH:2 * GH], in0=at.rowmax[:, :, :], scalar=-1.0,
                             in1=at.shift[:, :, 0:GH], op0=ALU.mult,
                             op1=ALU.subtract).then_inc(at.shift_ready, 1)


def shift_turn(pe, at, eye, b, g):
    n = number(b, g)
    pe.wait_ge(at.shift_ready, n + 1)
    for qt in range(TT):
        mm = pe.transpose(at.scores_ps[0:2 * GH, 0, qt * P:qt * P + P].bitcast(F32R), at.shift[:, qt, :], eye[:, :])
    mm.then_inc(at.shift_turned, 1)


def shift_copy(act, at, b, g):
    n = number(b, g)
    act.wait_ge(at.shift_turned, n + 1)
    at_least(act, at.shifted, n * 16)
    act.activation(at.shift_row[0:2 * GH, :], at.scores_ps[0:2 * GH, 0, :].bitcast(F32R),
                   ACT.Copy).then_inc(at.shift_copied, 1)


def shift_send(act, at, b, g):
    n = number(b, g)
    act.wait_ge(at.shift_copied, n + 1)
    act.dma_start(at.q_stack[g % 2][96:98, :, :].bitcast(F32),
                  at.shift_row[0:2 * GH, :].bitcast(F32)).then_inc(at.shifted, 16)


def stack_send(sp, at, b, g, pair):
    n = number(b, g)
    heads, rows = slice(2 * pair, 2 * pair + 2), slice(2 * HD * pair, 2 * HD * (pair + 1))
    q, key = at.q_stack[g % 2], at.k_stack[g % 2]
    apart(sp, at.ones_set, at.score_t_ready, (n - 2) * UNITS + UNITS // 2 * (pair + 1))
    apart(sp, at.ones_set, at.q_ready, n + 1)
    for r, part in enumerate((0, 0, 1)):
        sp.dma_start(q[32 * r:32 * r + 32, heads, :].bitcast(F32),
                     at.q_split[rows, part, :].bitcast(F32)).then_inc(at.stacked[pair], 16)
    apart(sp, at.ones_set, at.k_ready, n + 1)
    for r, part in enumerate((0, 1, 0)):
        sp.dma_start(key[32 * r:32 * r + 32, heads, :].bitcast(F32),
                     at.k_split[rows, part, :].bitcast(F32)).then_inc(at.stacked[pair], 16)


def score_t_unit(pe, at, eye_bf, colmask, b, g, k):
    h, j = divmod(k, 3)
    n = number(b, g)
    if k == 0:
        pe.wait_ge(at.shifted, n * 16 + 16)
    at_least(pe, at.exp_done, n * UNITS + k - 1)
    q, key = at.q_stack[g % 2], at.k_stack[g % 2]
    for i, (kt, col, width) in enumerate(KEY_MAJOR[j]):
        pe.matmul(at.scores_t_ps[:, k % 2, col:col + width], key[0:98, h, kt * P:kt * P + P],
                  q[0:98, h, kt * P:SEQ], start=(i == 0), stop=False, skip_group_check=True)
    for kt, col, width in KEY_MAJOR[j]:
        mm = pe.matmul(at.scores_t_ps[:, k % 2, col:col + P], eye_bf[:, :], colmask[:, :],
                       start=False, stop=True, skip_group_check=True)
    mm.then_inc(at.score_t_ready, 1)


def exp_unit(act, at, b, g, k):
    u, w = number(b, g) * UNITS + k, WIDTH[k % 3]
    act.wait_ge(at.score_t_ready, u + 1)
    at_least(act, at.lo_done, u - 1)
    act.activation(at.prob[:, k % 2, 0:w], at.scores_t_ps[:, k % 2, 0:w], ACT.Exp, scale=SCALE)
    at_least(act, at.pv_done, u + 1 - at.ring)
    act.activation(at.prob_hi[:, k % at.ring, 0:w], at.scores_t_ps[:, k % 2, 0:w], ACT.Exp,
                   scale=SCALE).then_inc(at.exp_done, 1)


def lo_unit(dve, at, b, g, k):
    u, w = number(b, g) * UNITS + k, WIDTH[k % 3]
    dve.wait_ge(at.exp_done, u + 1)
    dve.tensor_tensor(at.prob_lo[:, k % at.ring, 0:w], at.prob[:, k % 2, 0:w], at.prob_hi[:, k % at.ring, 0:w],
                      ALU.subtract).then_inc(at.lo_done, 1)


def pv_unit(pe, at, b, g, k):
    h, j = divmod(k, 3)
    n = number(b, g)
    pe.wait_ge(at.lo_done, n * UNITS + k + 1)
    if j == 0:
        at_least(pe, at.pv_copied, n * GH + h - 1)
    if g == 0 and h == 0:
        pe.wait_ge(at.value_ready, b * at.value_steps[3] + at.value_steps[j])
    for kt, col, width in KEY_MAJOR[j]:
        for part, prob in enumerate((at.prob_hi, at.prob_lo)):
            mm = pe.matmul(at.pv_ps[0:at.vcols, h % 2, kt * P:SEQ], at.value[:, kt, g * GH + h, :],
                           prob[:, k % at.ring, col:col + width], start=(kt == 0 and part == 0),
                           stop=(kt == TT - 1 and part == 1), skip_group_check=True)
    mm.then_inc(at.pv_done, 1)


def pv_copy(act, at, b, g, h):
    n = number(b, g)
    act.wait_ge(at.pv_done, (n * GH + h + 1) * 3)
    if h == 0:
        at_least(act, at.gathered, n * 48)
    act.activation(at.pv_raw[0:at.vcols, h, :], at.pv_ps[0:at.vcols, h % 2, :], ACT.Copy).then_inc(at.pv_copied, 1)


PROJECTIONS = (((4, 7), (9, 12)), ((7, 10), (9, 12)), ((4, 7), (8, 12)), ((4, 7), (8, 12)))
AHEAD = 3
ROTATED = (4, 5)


def exists(b, g, ahead):
    return not (is_last(b) and g + ahead >= GROUPS)


def leaving(b, g, slot):
    for i, (start, stop) in enumerate(PROJECTIONS[g]):
        if stop == slot and exists(b, g, AHEAD):
            yield *group(b, g, AHEAD), i
    if slot == 0 and not (isinstance(b, int) and b == 0 and g == 0) and exists(b, g, AHEAD - 1):
        for i, (start, stop) in enumerate(PROJECTIONS[g - 1]):
            if stop == UNITS:
                yield *group(b, g, AHEAD - 1), i


def splitting(b, g, slot):
    if slot in ROTATED and exists(b, g, AHEAD - 1):
        yield *group(b, g, AHEAD - 1), ROTATED.index(slot)


SCORE_SLOTS = range(1, 8)


def share(count, slots, slot):
    return range(count * slot // slots, count * (slot + 1) // slots)


def behind(b, g, slot):
    return (b, g, slot - 1) if slot > 0 else (*group(b, g, -1), UNITS - 1)


def score_share(slot):
    return share(UNITS, len(SCORE_SLOTS), slot - SCORE_SLOTS[0]) if slot in SCORE_SLOTS else ()


def attention_layer(nc, both, x_t, wq_t, wk_t, wv_t, a_qkv, b_qkv, starts, consts, wo_t, wq2_t, wk2_t, ln_w,
                    sums_hbm, attn_hbm):
    with ExitStack() as ctx:
        def sb(what, shape, dt=F32):
            return ctx.enter_context(nc.sbuf_tensor(f"a_{what}", shape, dt))

        def sem(what):
            return ctx.enter_context(nc.semaphore(f"a_{what}"))

        at = Attention(nc, ctx, "a", HD, 4, (1, 2, 4, TT))
        lin_ps = ctx.enter_context(nc.psum_tensor("a_lin_ps", [P, 2, SEQ], F32))

        ids, w_split, x_stage, x_split = both.ids, both.w_split, both.stage, both.x_split
        rowmask, eye, eye_bf, colmask = both.rowmask, both.eye, both.eye_bf, both.colmask
        a_stage = sb("a_stage", [P, KC, 3 * RANK])
        a_split = sb("a_split", [P, 2, KC, 3 * RANK], F32R)
        b_stage = sb("b_stage", [P, 3 * D * RANK // P])
        b_split = sb("b_split", [P, 2, 3 * D * RANK // P], F32R)
        b_stack = sb("b_stack", [3 * RANK, 3, D], F32R)
        low_split = sb("low_split", [3 * RANK, 2, SEQ], F32R)
        low_stack = sb("low_stack", [3 * RANK, 3, SEQ], F32R)
        rope_in = [sb(f"rope_in{i}", [P, SEQ]) for i in range(2)]
        rope_turned = [sb(f"rope_turned{i}", [P, SEQ]) for i in range(2)]
        rope_out = [sb(f"rope_out{i}", [P, SEQ]) for i in range(2)]
        cos_sin = sb("cos_sin", [P, 2, SEQ])
        sum_hi = sb("sum_hi", [P, SEQ])
        sum_lo = sb("sum_lo", [P, SEQ])
        sums = sb("sums", [GH * TT, P])
        inverse = sb("inverse", [GH * TT, P])
        inverse_all = sb("inverse_all", [P, SEQ])
        starts_i = sb("starts_i", [1, ADAPTERS], I32)
        starts_f = sb("starts_f", [1, ADAPTERS])
        index = sb("index", [1, BATCH])
        count = sb("count", [1, BATCH])

        const_in = sem("const_in")
        const_ready = sem("const_ready")
        ids_step = sem("ids_step")
        w_in = [sem(f"w{n}_in") for n in "qkv"]
        w_hi = sem("w_hi")
        w_ready = sem("w_ready")
        x_in = sem("x_in")
        x_hi = sem("x_hi")
        x_ready = sem("x_ready")
        ab_in = sem("ab_in")
        ab_hi = sem("ab_hi")
        ab_ready = sem("ab_ready")
        b_stacked = sem("b_stacked")
        low_made = sem("low_made")
        low_hi = sem("low_hi")
        low_ready = sem("low_ready")
        low_stacked = sem("low_stacked")
        lin_ready = [sem(f"lin_ready{i}") for i in range(2)]
        lin_free = [sem(f"lin_free{i}") for i in range(2)]
        turned = [sem(f"turned{i}") for i in range(2)]
        roped = [sem(f"roped{i}") for i in range(2)]
        rope_hi = [sem(f"rope_hi{i}") for i in range(2)]
        value_hi = sem("value_hi")
        inverted = sem("inverted")
        inverse_out = sem("inverse_out")
        inverse_in = sem("inverse_in")
        merged = sem("merged")
        normalised = sem("normalised")
        attn_out = sem("attn_out")

        def qk_use(b, g):
            return b * 6 + (g if g < 3 else 5)

        def v_use(b, t):
            return b * 6 + 3 + t // 2

        square = rope_out[0][:, 0:2 * P].rearrange("p (a n) -> p a n", a=2)
        w_stage = ([at.pv_raw[:, c, :] for c in range(KC)],
                   [rope_in[1][:, :], rope_turned[1][:, :], rope_out[1][:, :], sum_hi[:, :]],
                   [sum_lo[:, :], inverse_all[:, :], at.prob[:, 0, :], at.prob[:, 1, :]])
        rope_stage = [t[:, :] for t in (*rope_in, *rope_turned)]
        through_x = [x_stage[:, c, :] for c in range(KC)]
        following = ((through_x, w_split[0], None, (w_in[0], 32)), (rope_stage, w_split[1], both.lnw, (w_in[1], 128)),
                     (through_x, w_split[2], both.lnw, (w_in[0], 48)), (through_x, x_split, None, (w_in[0], 64)))

        def following_chunks(b, g, slot):
            if is_last(b):
                for n, (step, start) in enumerate(((1, 1), (2, 2), (2, 3), (3, 3))):
                    if g == step and slot in range(start, start + 2 * KC, 2):
                        yield n, (slot - start) // 2

        block = ctx.enter_context(nc.Block())

        @block.sync
        def _(sp):
            sp.dma_start(starts_i[:, :], starts).then_inc(const_in, 16)
            sp.dma_start(index[:, :], consts[0:1, COUNT:COUNT + BATCH]).then_inc(const_in, 16)
            sp.dma_start(cos_sin[:, :, :], consts[:, COS:EYE].rearrange("p (a n) -> p a n", a=2)).then_inc(const_in, 16)
            sp.dma_start(square[:, 0, :], consts[:, EYE:EYE + P]).then_inc(const_in, 16)
            sp.dma_start(square[:, 1, :], consts[:, COLMASK:COLMASK + P]).then_inc(const_in, 16)
            sp.dma_start(rowmask[:, :], consts[:, ROWMASK:ROWMASK + SEQ]).then_inc(const_in, 16)
            sp.dma_start(both.lnw[:, :, :], ln_w).then_inc(const_in, 16)

            def load(b):
                apart(sp, at.ones_set, x_ready, b * KC)
                apart(sp, at.ones_set, ab_ready, b * 2)
                sp.dma_start(x_stage[:, :, :], x_t[:, :, bass.ds(b * SEQ, SEQ)]).then_inc(x_in, 16)
                if isinstance(b, int) and b == 0:
                    sp.wait_ge(ids_step, 2 + ADAPTERS + 1)
                i = sp.value_load(ids[0:1, bass.ds(b, 1)], min_val=0, max_val=ADAPTERS - 1)
                sp.dma_start(a_stage[:, :, :], a_qkv[bass.ds(i, 1)].rearrange("a p c r -> (a p) c r")).then_inc(ab_in, 16)
                sp.dma_start(b_stage[:, :], b_qkv[bass.ds(i, 1)].rearrange("a p n -> (a p) n")).then_inc(ab_in, 16)

            def send_b(b):
                apart(sp, at.ones_set, lin_ready[1], qk_use(b, 0))
                apart(sp, at.ones_set, ab_ready, b * 2 + 2)
                for r, part in enumerate((0, 1, 0)):
                    sp.dma_start(b_stack[RANK * r:RANK * (r + 1), :, :].bitcast(F32),
                                 b_split[:, part, :].bitcast(F32)).then_inc(b_stacked, 16)

            def send_low(b):
                sp.wait_ge(low_ready, b + 1)
                for r, part in enumerate((0, 0, 1)):
                    sp.dma_start(low_stack[RANK * r:RANK * (r + 1), :, :].bitcast(F32),
                                 low_split[:, part, :].bitcast(F32)).then_inc(low_stacked, 16)

            def gather(b, g):
                n = number(b, g)
                apart(sp, at.ones_set, at.pv_copied, (n + 1) * GH)
                apart(sp, at.ones_set, attn_out, n * 16)
                sp.dma_start(sum_hi[:, :], at.pv_raw[0:HD, :, :]).then_inc(at.gathered, 16)
                sp.dma_start(sum_lo[:, :], at.pv_raw[HD:2 * HD, :, :]).then_inc(at.gathered, 16)
                sp.dma_start(sums[:, :], at.pv_raw[2 * HD:2 * HD + 1, :, :]).then_inc(at.gathered, 16)

            def spread(b, g):
                n = number(b, g)
                sp.wait_ge(inverted, n + 1)
                sp.dma_start(sums_hbm.rearrange("h (c n) -> (h c) n", c=TT), inverse[:, :]).then_inc(inverse_out, 16)
                sp.wait_ge(inverse_out, n * 16 + 16)
                sp.dma_start(inverse_all[:, :], sums_hbm.rearrange("(o h) n -> o h n", o=1).broadcast_to(
                    [HD, GH, SEQ])).then_inc(inverse_in, 16)

            def store(b, g):
                n = number(b, g)
                sp.wait_ge(normalised, n + 1)
                sp.dma_start(attn_hbm[:, g, bass.ds(b * SEQ, SEQ)], sum_lo[:, :]).then_inc(attn_out, 16)

            def step(b, g):
                last = is_last(b)
                if g == 0 and not last:
                    load(b + 1)
                first = isinstance(b, int) and b == 0 and g == 0
                if not first:
                    gather(*group(b, g, -1))
                if g == 1 and not last:
                    send_b(b + 1)
                    send_low(b + 1)
                if not first:
                    spread(*group(b, g, -1))
                if not (last and g >= 2):
                    stack_send(sp, at, *group(b, g, 2), 0)
                if not first:
                    store(*group(b, g, -1))
                if not (last and g >= 2):
                    stack_send(sp, at, *group(b, g, 2), 1)
                if last and g == 0:
                    sp.wait_ge(x_ready, BATCH * KC)
                    sp.dma_start(x_stage[:, :, :], wo_t).then_inc(w_in[0], 16)
                if last and g == 1:
                    for i in range(2):
                        sp.wait_ge(roped[i], BATCH * GROUPS * 3)
                    for c in range(KC):
                        sp.dma_start(rope_stage[c], wq2_t[:, c, :]).then_inc(w_in[1], 16)
                    sp.wait_ge(w_ready, 3 * KC + KC)
                    sp.dma_start(x_stage[:, :, :], wk2_t).then_inc(w_in[0], 16)
                if last and g == 2:
                    sp.wait_ge(w_ready, 3 * KC + 3 * KC)
                    sp.dma_start(x_stage[:, :, :], attn_hbm[:, :, 0:SEQ]).then_inc(w_in[0], 16)

            load(0)
            sp.dma_start(at.pv_raw[:, :, :], wq_t).then_inc(w_in[0], 16)
            for n, w in ((1, wk_t), (2, wv_t)):
                for c in range(KC):
                    sp.dma_start(w_stage[n][c], w[:, c, :]).then_inc(w_in[n], 16)
            send_b(0)
            send_low(0)
            for pair in range(2):
                stack_send(sp, at, 0, 0, pair)
            for pair in range(2):
                stack_send(sp, at, 0, 1, pair)

            def body(b):
                for g in range(GROUPS):
                    step(b, g)

            batches(sp, body)
            gather(BATCH - 1, GROUPS - 1)
            spread(BATCH - 1, GROUPS - 1)
            store(BATCH - 1, GROUPS - 1)
            sp.wait_ge(attn_out, BATCH * GROUPS * 16)

        @block.gpsimd
        def _(pool):
            for i in range(2):
                pool.memset(at.k_stack[i][96:98, :, :].bitcast(F32), 1.0).then_inc(at.ones_set, 1)
                pool.wait_ge(at.ones_set, i + 1)
            pool.memset(at.value[:, :, :, 2 * HD:2 * HD + 1].bitcast(F32), 1.0).then_inc(at.ones_set, 1)
            pool.wait_ge(const_in, 112)

            def rope(b, g, i):
                n = number(b, g)
                pool.wait_ge(turned[i], n + 1)
                at_least(pool, at.k_ready if i else at.q_ready, n)
                pool.tensor_tensor(rope_out[i][:, :], rope_in[i][:, :], cos_sin[:, 0, :], ALU.mult).then_inc(roped[i], 1)
                pool.tensor_tensor(rope_turned[i][:, :], rope_turned[i][:, :], cos_sin[:, 1, :],
                                   ALU.mult).then_inc(roped[i], 1)
                pool.wait_ge(roped[i], n * 3 + 2)
                pool.tensor_tensor(rope_out[i][:, :], rope_out[i][:, :], rope_turned[i][:, :],
                                   ALU.add).then_inc(roped[i], 1)

            def merge(b, g):
                n = number(b, g)
                pool.wait_ge(at.gathered, n * 48 + 48)
                pool.tensor_tensor(sum_hi[:, :], sum_hi[:, :], sum_lo[:, :], ALU.add).then_inc(merged, 1)

            def normalise(b, g):
                n = number(b, g)
                pool.wait_ge(merged, n + 1)
                apart(pool, at.ones_set, inverse_in, n * 16 + 16)
                pool.tensor_tensor(sum_lo[:, :], sum_hi[:, :], inverse_all[:, :], ALU.mult).then_inc(normalised, 1)

            def rotated_lo(b, g, i):
                apart(pool, at.ones_set, rope_hi[i], number(b, g) + 1)
                split = at.k_split if i else at.q_split
                pool.tensor_tensor(split[:, 1, :], rope_out[i][:, :], split[:, 0, :],
                                   ALU.subtract).then_inc(at.k_ready if i else at.q_ready, 1)

            def x_chunk(b, c):
                apart(pool, at.ones_set, x_hi, b * KC + c + 1)
                pool.tensor_tensor(x_split[:, 1, c, :], x_stage[:, c, :], x_split[:, 0, c, :],
                                   ALU.subtract).then_inc(x_ready, 1)

            def step(b, g):
                first = isinstance(b, int) and b == 0 and g == 0
                if g == 1 and not is_last(b):
                    for c in range(KC // 2, KC):
                        x_chunk(b + 1, c)
                for tile in leaving(b, g, 0):
                    rope(*tile)
                if not first:
                    merge(*group(b, g, -1))
                for slot in range(UNITS):
                    for tile in splitting(b, g, slot):
                        rotated_lo(*tile)
                if not first:
                    normalise(*group(b, g, -1))
                for slot in range(1, UNITS):
                    for tile in leaving(b, g, slot):
                        rope(*tile)

            rope(0, 0, 0)
            for g in range(2):
                rope(0, g, 1)
                rotated_lo(0, g, 0)
                rope(0, g + 1, 0)
                rotated_lo(0, g, 1)
            rope(0, 2, 1)

            def body(b):
                for g in range(GROUPS):
                    step(b, g)

            batches(pool, body)
            merge(BATCH - 1, GROUPS - 1)
            normalise(BATCH - 1, GROUPS - 1)

        @block.scalar
        def _(act):
            def weights(n):
                act.wait_ge(w_in[n], 64 if n else 16)
                for c in range(KC):
                    act.activation(w_split[n][:, 0, c, :], w_stage[n][c], ACT.Copy).then_inc(w_hi, 1)

            def following_hi(n, c):
                source, to, scale, landed = following[n]
                act.wait_ge(*landed)
                if scale is None:
                    act.activation(to[:, 0, c, :], source[c], ACT.Copy).then_inc(w_hi, 1)
                else:
                    act.wait_ge(const_in, 112)
                    act.activation(to[:, 0, c, :], source[c], ACT.Copy, scale=scale[:, 0, c:c + 1]).then_inc(w_hi, 1)

            def x_chunk(b, c):
                if c == 0:
                    act.wait_ge(x_in, b * 16 + 16)
                    at_least(act, lin_ready[1], qk_use(b, 0))
                act.activation(x_split[:, 0, c, :], x_stage[:, c, :], ACT.Copy).then_inc(x_hi, 1)

            def adapter(b):
                act.wait_ge(ab_in, b * 32 + 32)
                act.activation(a_split[:, 0, :, :], a_stage[:, :, :], ACT.Copy).then_inc(ab_hi, 1)
                at_least(act, b_stacked, b * 48)
                act.activation(b_split[:, 0, :], b_stage[:, :], ACT.Copy).then_inc(ab_hi, 1)

            def low(b):
                act.wait_ge(low_made, b + 1)
                at_least(act, low_stacked, b * 48)
                act.activation(low_split[:, 0, :], lin_ps[0:3 * RANK, 1, :], ACT.Copy).then_inc(low_hi, 1)

            def projected(b, g, i):
                act.wait_ge(lin_ready[i], qk_use(b, g) + 1)
                at_least(act, roped[i], number(b, g) * 3)
                act.activation(rope_in[i][:, :], lin_ps[:, i, :], ACT.Copy).then_inc(lin_free[i], 1)

            def rotated_hi(b, g, i):
                n = number(b, g)
                act.wait_ge(roped[i], n * 3 + 3)
                for pair in range(2):
                    at_least(act, at.stacked[pair], n * 96)
                split = at.k_split if i else at.q_split
                act.activation(split[:, 0, :], rope_out[i][:, :], ACT.Copy).then_inc(rope_hi[i], 1)

            def value(b, t):
                act.wait_ge(lin_ready[t % 2], v_use(b, t) + 1)
                if t == 0:
                    at_least(act, at.pv_done, b * GROUPS * UNITS)
                act.activation(at.value[:, t, :, 0:HD], lin_ps[:, t % 2, :].rearrange("p (h d) -> p h d", d=HD),
                               ACT.Copy).then_inc(value_hi, 1)

            def step(b, g):
                last = is_last(b)
                first = isinstance(b, int) and b == 0 and g == 0
                for slot in range(UNITS):
                    if slot == 2 and not first:
                        pv_copy(act, at, *group(b, g, -1), 3)
                    if slot in (5, 8, 11):
                        pv_copy(act, at, b, g, (slot - 5) // 3)
                    exp_unit(act, at, b, g, slot)
                    if slot == 9 and not (last and g == GROUPS - 1):
                        shift_copy(act, at, *group(b, g, 1))
                        shift_send(act, at, *group(b, g, 1))
                    if g == 0 and 1 <= slot <= TT:
                        value(b, slot - 1)
                    if g == 0 and slot == 9 and not last:
                        adapter(b + 1)
                    if g == 1 and slot < 2 and not last:
                        for c in range(2):
                            x_chunk(b + 1, slot * 2 + c)
                    if g == 1 and slot == 5 and not last:
                        low(b + 1)
                    for tile in leaving(b, g, slot):
                        projected(*tile)
                    for tile in splitting(b, g, slot):
                        rotated_hi(*tile)
                    for chunk in following_chunks(b, g, slot):
                        following_hi(*chunk)

            for c in range(KC):
                x_chunk(0, c)
            adapter(0)
            weights(0)
            low(0)
            for n in range(1, 3):
                weights(n)
            projected(0, 0, 0)
            for g in range(2):
                projected(0, g, 1)
                rotated_hi(0, g, 0)
                projected(0, g + 1, 0)
                rotated_hi(0, g, 1)
            shift_copy(act, at, 0, 0)
            shift_send(act, at, 0, 0)
            projected(0, 2, 1)

            def body(b):
                for g in range(GROUPS):
                    step(b, g)

            batches(act, body)
            pv_copy(act, at, BATCH - 1, GROUPS - 1, 3)

        @block.vector
        def _(dve):
            dve.wait_ge(const_in, 112)
            dve.tensor_copy(starts_f[:, :], starts_i[:, :]).then_inc(ids_step, 1)
            dve.memset(count[:, :], -1.0).then_inc(ids_step, 1)
            for i in range(ADAPTERS):
                dve.wait_ge(ids_step, 2 + i)
                dve.scalar_tensor_tensor(out=count[:, :], in0=index[:, :], scalar=starts_f[0:1, i:i + 1],
                                         in1=count[:, :], op0=ALU.is_ge, op1=ALU.add).then_inc(ids_step, 1)
            dve.wait_ge(ids_step, 2 + ADAPTERS)
            dve.tensor_scalar(ids[:, :], count[:, :], 0.0, None, ALU.max).then_inc(ids_step, 1)
            dve.tensor_copy(eye[:, :], square[:, 0, :]).then_inc(const_ready, 1)
            dve.tensor_copy(eye_bf[:, :], square[:, 0, :]).then_inc(const_ready, 1)
            dve.tensor_copy(colmask[:, :], square[:, 1, :]).then_inc(const_ready, 1)

            def weights(n):
                for c in range(KC):
                    dve.wait_ge(w_hi, n * KC + c + 1)
                    dve.tensor_tensor(w_split[n][:, 1, c, :], w_stage[n][c], w_split[n][:, 0, c, :],
                                      ALU.subtract).then_inc(w_ready, 1)

            def following_lo(nth, n, c):
                source, to, scale, _ = following[n]
                dve.wait_ge(w_hi, 3 * KC + nth + 1)
                if scale is None:
                    dve.tensor_tensor(to[:, 1, c, :], source[c], to[:, 0, c, :], ALU.subtract).then_inc(w_ready, 1)
                else:
                    dve.scalar_tensor_tensor(out=to[:, 1, c, :], in0=source[c], scalar=scale[:, 0, c:c + 1],
                                             in1=to[:, 0, c, :], op0=ALU.mult, op1=ALU.subtract).then_inc(w_ready, 1)

            chunks = [(g, slot, *chunk) for g in range(GROUPS) for slot in range(UNITS)
                      for chunk in following_chunks(BATCH - 1, g, slot)]

            def x_chunk(b, c):
                dve.wait_ge(x_hi, b * KC + c + 1)
                dve.tensor_tensor(x_split[:, 1, c, :], x_stage[:, c, :], x_split[:, 0, c, :],
                                  ALU.subtract).then_inc(x_ready, 1)

            def adapter(b):
                dve.wait_ge(ab_hi, b * 2 + 2)
                dve.tensor_tensor(a_split[:, 1, :, :], a_stage[:, :, :], a_split[:, 0, :, :],
                                  ALU.subtract).then_inc(ab_ready, 1)
                dve.tensor_tensor(b_split[:, 1, :], b_stage[:, :], b_split[:, 0, :],
                                  ALU.subtract).then_inc(ab_ready, 1)

            def low(b):
                dve.wait_ge(low_hi, b + 1)
                dve.tensor_tensor(low_split[:, 1, :], lin_ps[0:3 * RANK, 1, :], low_split[:, 0, :],
                                  ALU.subtract).then_inc(low_ready, 1)

            def exchange(b, g, i):
                apart(dve, at.ones_set, lin_free[i], number(b, g) + 1)
                apart(dve, at.ones_set, roped[i], number(b, g) * 3)
                dve.stream_shuffle(rope_turned[i][:, :], rope_in[i][:, :],
                                   [p ^ 2 for p in range(32)]).then_inc(turned[i], 1)

            def value(b, t):
                dve.wait_ge(value_hi, b * TT + t + 1)
                dve.tensor_tensor(at.value[:, t, :, HD:2 * HD], lin_ps[:, t % 2, :].rearrange("p (h d) -> p h d", d=HD),
                                  at.value[:, t, :, 0:HD],
                                  ALU.subtract).then_inc(at.value_ready, 1)

            def invert(b, g):
                n = number(b, g)
                dve.wait_ge(at.gathered, n * 48 + 48)
                at_least(dve, inverse_out, n * 16)
                dve.reciprocal(inverse[:, :], sums[:, :]).then_inc(inverted, 1)

            def step(b, g):
                last = is_last(b)
                first = isinstance(b, int) and b == 0 and g == 0
                for slot in range(UNITS):
                    if slot > 0:
                        lo_unit(dve, at, b, g, slot - 1)
                    elif not first:
                        lo_unit(dve, at, *group(b, g, -1), UNITS - 1)
                    if not (last and g == GROUPS - 1):
                        for k in score_share(slot):
                            score_max(dve, at, rowmask, *group(b, g, 1), k)
                        if slot == SCORE_SLOTS[-1]:
                            shift_split(dve, at, *group(b, g, 1))
                    if slot == 6 and not first:
                        invert(*group(b, g, -1))
                    if g == 0 and 1 <= slot <= TT:
                        value(b, slot - 1)
                    if g == 0 and slot == 10 and not last:
                        adapter(b + 1)
                    if g == 1 and 1 <= slot < 3 and not last:
                        x_chunk(b + 1, slot - 1)
                    if g == 1 and slot == 6 and not last:
                        low(b + 1)
                    if not (first and slot == 0):
                        for tile in leaving(*behind(b, g, slot)):
                            exchange(*tile)
                    for nth, (step_, slot_, n, c) in enumerate(chunks):
                        if last and (step_, slot_ + 1) == (g, slot):
                            following_lo(nth, n, c)

            for c in range(KC):
                x_chunk(0, c)
            adapter(0)
            weights(0)
            low(0)
            for n in range(1, 3):
                weights(n)
            exchange(0, 0, 0)
            exchange(0, 0, 1)
            exchange(0, 1, 0)
            exchange(0, 1, 1)
            for k in range(UNITS):
                score_max(dve, at, rowmask, 0, 0, k)
                if k == UNITS // 2:
                    exchange(0, 2, 0)
            shift_split(dve, at, 0, 0)
            exchange(0, 2, 1)

            def body(b):
                for g in range(GROUPS):
                    step(b, g)

            batches(dve, body)
            lo_unit(dve, at, BATCH - 1, GROUPS - 1, UNITS - 1)
            invert(BATCH - 1, GROUPS - 1)

        @block.tensor
        def _(pe):
            pe.wait_ge(const_ready, 3)
            pe.wait_ge(at.ones_set, 3)

            def low(b, items):
                for x in items:
                    c, (w, a) = x // 3, PASSES[x % 3]
                    if x == 0:
                        at_least(pe, lin_free[1], b * GROUPS)
                        pe.wait_ge(x_ready, (b + 1) * KC)
                        pe.wait_ge(ab_ready, (b + 1) * 2)
                    mm = pe.matmul(lin_ps[0:3 * RANK, 1, :], a_split[:, w, c, :], x_split[:, a, c, :],
                                   start=(x == 0), stop=(x == 3 * KC - 1))
                    if x == 3 * KC - 1:
                        mm.then_inc(low_made, 1)

            def project(b, g, i, items):
                for x in items:
                    if x == 0:
                        if g == 3:
                            pe.wait_ge(at.value_ready, b * TT + 3 + i)
                        elif g == 0 and i == 1:
                            pe.wait_ge(low_ready, b + 1)
                        else:
                            at_least(pe, lin_free[i], number(b, g))
                    if x < 3 * KC:
                        c, (w, a) = x // 3, PASSES[x % 3]
                        pe.matmul(lin_ps[:, i, :], w_split[i][:, w, c, g * P:g * P + P], x_split[:, a, c, :],
                                  start=(x == 0), stop=False)
                    else:
                        pe.wait_ge(low_stacked, b * 48 + 48)
                        pe.wait_ge(b_stacked, b * 48 + 48)
                        pe.matmul(lin_ps[:, i, :], b_stack[:, i, g * P:g * P + P], low_stack[:, i, :],
                                  start=False, stop=True).then_inc(lin_ready[i], 1)

            def project_value(b, t):
                bank = t % 2
                if t < 2:
                    pe.wait_ge(lin_free[bank], b * GROUPS + 3)
                else:
                    pe.wait_ge(at.value_ready, b * TT + t - 1)
                for x in range(3 * KC):
                    c, (w, a) = x // 3, PASSES[x % 3]
                    pe.matmul(lin_ps[:, bank, :], x_split[:, a, c, t * P:t * P + P], w_split[2][:, w, c, :],
                              start=(x == 0), stop=False)
                pe.matmul(lin_ps[:, bank, :], low_stack[:, 2, t * P:t * P + P], b_stack[:, 2, :],
                          start=False, stop=True).then_inc(lin_ready[bank], 1)

            def step(b, g):
                last = is_last(b)
                first = isinstance(b, int) and b == 0 and g == 0
                for slot in range(UNITS):
                    score_t_unit(pe, at, eye_bf, colmask, b, g, slot)
                    if slot == 9 and not (last and g == GROUPS - 1):
                        shift_turn(pe, at, eye, *group(b, g, 1))
                    if not (last and g == GROUPS - 1):
                        for k in score_share(slot):
                            score_unit(pe, at, *group(b, g, 1), k)
                    if slot < 2 and not first:
                        pv_unit(pe, at, *group(b, g, -1), UNITS - 2 + slot)
                    if g == 0 and slot < TT:
                        project_value(b, slot)
                    if g == 1 and 3 <= slot < 5 and not last:
                        low(b + 1, share(3 * KC, 2, slot - 3))
                    for i, (start, stop) in enumerate(PROJECTIONS[g]):
                        if start <= slot < stop and exists(b, g, AHEAD):
                            project(*group(b, g, AHEAD), i, share(3 * KC + 1, stop - start, slot - start))
                    if slot >= 2:
                        pv_unit(pe, at, b, g, slot - 2)

            low(0, range(3 * KC))
            for g in range(2):
                for i in range(2):
                    if g == 0:
                        pe.wait_ge(w_ready, (i + 1) * KC)
                    project(0, g, i, range(3 * KC + 1))
            project(0, 2, 0, range(3 * KC + 1))
            for k in range(UNITS):
                score_unit(pe, at, 0, 0, k)
            shift_turn(pe, at, eye, 0, 0)
            project(0, 2, 1, range(3 * KC + 1))
            pe.wait_ge(w_ready, 3 * KC)

            def body(b):
                for g in range(GROUPS):
                    step(b, g)

            batches(pe, body)
            for k in range(UNITS - 2, UNITS):
                pv_unit(pe, at, BATCH - 1, GROUPS - 1, k)


MADE_B = (((-2, 6, 8, -2, 8), (-2, 6, 9, -2, 9)), ((-3, 10, 12, -2, 3), (-2, 0, 2, -2, 4)),
          ((-2, 3, 5, -2, 5), (-2, 5, 7, -2, 7)), ((-2, 1, 3, -2, 3), (-2, 3, 5, -2, 5)))
OUT_SLOTS = (7, 5)
OUT_COUNT = (6, 4)
H_LO = 2
VALUE_SLOTS = (5, 8)


def made_b(b, g, slot):
    for to in range(GROUPS):
        for i, (step, start, stop, _, _) in enumerate(MADE_B[to]):
            at = group(b, g, -step)
            if at[1] == to and start <= slot < stop and has(b, (g - step) // GROUPS):
                yield *at, i, share(3 * KC, stop - start, slot - start)


def left_b(b, g, slot):
    for to in range(GROUPS):
        for i, (_, _, _, step, leave) in enumerate(MADE_B[to]):
            at = group(b, g, -step)
            if at[1] == to and leave == slot and has(b, (g - step) // GROUPS):
                yield *at, i


def out_items(g, slot):
    half = TT // 2 * (3 * KC + 1)
    for n in range(2):
        at = g * UNITS + slot - n * UNITS - OUT_SLOTS[n]
        if 0 <= at < OUT_COUNT[n]:
            yield from range(n * half + share(half, OUT_COUNT[n], at).start, n * half + share(half, OUT_COUNT[n], at).stop)


def value_items(b, g, slot):
    for bank, start in enumerate(VALUE_SLOTS):
        at = (g - 3) % GROUPS * UNITS + slot - start
        to = b + 1 if g == 3 else b
        first = isinstance(b, int) and b == 0 and g == 0
        if 0 <= at < 3 and not first and (g != 3 or has(b, 1)):
            yield to, bank, share(2 * 3 * KC, 3, at)


def rsqrt(dve, step, done, out, x, t):
    dve.tensor_scalar(t.bitcast(I32), x.bitcast(I32), 1, None, ALU.logical_shift_right).then_inc(step, 1)
    dve.wait_ge(step, done + 1)
    dve.tensor_scalar(out.bitcast(I32), t.bitcast(I32), -1.0, RSQRT_MAGIC, ALU.mult, ALU.add).then_inc(step, 1)
    for i in range(3):
        dve.wait_ge(step, done + 2 + 3 * i)
        dve.tensor_tensor(t, out, out, ALU.mult).then_inc(step, 1)
        dve.wait_ge(step, done + 3 + 3 * i)
        dve.scalar_tensor_tensor(out=t, in0=t, scalar=-0.5, in1=x, op0=ALU.mult, op1=ALU.mult).then_inc(step, 1)
        dve.wait_ge(step, done + 4 + 3 * i)
        dve.scalar_tensor_tensor(out=out, in0=t, scalar=1.5, in1=out, op0=ALU.add, op1=ALU.mult).then_inc(step, 1)


RSQRT_STEPS = 11


def gate_layer(nc, both, x, attn_hbm, a_o, b_o, wv, wo, low_a, selector, sums_hbm, x1_hbm, h_hbm, z_hbm):
    with ExitStack() as ctx:
        def sb(what, shape, dt=F32):
            return ctx.enter_context(nc.sbuf_tensor(f"b_{what}", shape, dt))

        def sem(what):
            return ctx.enter_context(nc.semaphore(f"b_{what}"))

        at = Attention(nc, ctx, "b", RANK, 3, (1, 1, 2, 3))
        lin_ps = ctx.enter_context(nc.psum_tensor("b_lin_ps", [P, 2, SEQ], F32))
        VW = HEADS * RANK
        EARLY = HEADS - GH
        values = lin_ps[:, :, :].rearrange("p i (t h d) -> p (i t) h d", t=2, d=RANK)

        ids, lnw, rowmask, eye, eye_bf, colmask = both.ids, both.lnw, both.rowmask, both.eye, both.eye_bf, both.colmask
        wo_split, *qk_split = both.w_split
        vw_split = sb("vw_split", [P, 2, KC, VW], F32R)
        low_a_split = sb("low_a_split", [P, 2, KC, RANK], F32R)
        wide = both.stage
        res = sb("res", [P, TT, D])
        attn_split = both.x_split
        h_split = sb("h_split", [P, 2, KC, SEQ], F32R)
        h_turn = wide[:, :, :].rearrange("p t (c n) -> p t c n", c=KC)
        a_stage = sb("a_stage", [P, KC, RANK])
        a_split = sb("a_split", [P, 2, KC, RANK], F32R)
        b_stage = sb("b_stage", [P, D * RANK // P])
        b_split = sb("b_split", [P, 2, D * RANK // P], F32R)
        b_stack = sb("b_stack", [3 * RANK, D], F32R)
        low_split = sb("low_split", [RANK, 2, SEQ], F32R)
        low_stack = sb("low_stack", [3 * RANK, SEQ], F32R)
        sel = sb("sel", [GH * RANK, RANK])
        a_full = at.prob[:, 0, 0:KC * RANK].rearrange("p (c r) -> p c r", c=KC)
        wo_a = at.prob[:, 1, 0:TT * GH * RANK].rearrange("p (t r) -> p t r", t=TT)
        stats = sb("stats", [P, TT, 6])
        mean_var = sb("mean_var", [P, TT, 2])
        squares = sb("squares", [P, 2, TT])
        inv_root = sb("inv_root", [P, 2, TT])
        newton = sb("newton", [P, 2, TT])
        sum_hi = sb("sum_hi", [GH * RANK, SEQ])
        sum_lo = sb("sum_lo", [GH * RANK, SEQ])
        sums = sb("sums", [GH * TT, P])
        inverse = sb("inverse", [GH * TT, P])
        out_sum = sb("out_sum", [GH * RANK, SEQ])
        h_low = sb("h_low", [RANK, SEQ])
        mod = at.shift_row[:, :].bitcast(F32)
        z_split = low_split

        const_in = sem("const_in")
        stage_in = sem("stage_in")
        w_hi = sem("w_hi")
        w_ready = sem("w_ready")
        zeroed = sem("zeroed")
        wo_a_made = sem("wo_a_made")
        wo_a_copied = sem("wo_a_copied")
        vw_made = sem("vw_made")
        in_done = [sem(f"in_done{i}") for i in range(2)]
        attn_hi = sem("attn_hi")
        attn_ready = sem("attn_ready")
        ab_in = sem("ab_in")
        ab_hi = sem("ab_hi")
        ab_ready = sem("ab_ready")
        b_stacked = sem("b_stacked")
        low_made = sem("low_made")
        low_hi = sem("low_hi")
        low_ready = sem("low_ready")
        low_stacked = sem("low_stacked")
        o_made = sem("o_made")
        o_added = sem("o_added")
        stats_done = sem("stats_done")
        ln_step = sem("ln_step")
        x1_ready = sem("x1_ready")
        x1_out = sem("x1_out")
        h_ready = sem("h_ready")
        h_late = sem("h_late")
        h_turned = sem("h_turned")
        h_copied = sem("h_copied")
        h_hi = sem("h_hi")
        h_split_ready = sem("h_split_ready")
        h_out = sem("h_out")
        qk_made = [sem(f"{n}_made") for n in "qk"]
        qk_hi = [sem(f"{n}_hi") for n in "qk"]
        v_made = sem("v_made")
        value_hi = sem("value_hi")
        inverted = sem("inverted")
        inverse_out = sem("inverse_out")
        inverse_in = sem("inverse_in")
        merged = sem("merged")
        normalised = sem("normalised")
        added = sem("added")
        mod_made = sem("mod_made")
        mod_done = sem("mod_done")
        h_low_made = sem("h_low_made")
        h_low_copied = sem("h_low_copied")
        z_made = sem("z_made")
        z_hi = sem("z_hi")
        z_ready = sem("z_ready")
        z_out = sem("z_out")

        LN_STEPS = TT + 4 + RSQRT_STEPS
        qk_ready = (at.q_ready, at.k_ready)
        stage = at.pv_raw

        block = ctx.enter_context(nc.Block())

        @block.sync
        def _(sp):
            def load(b):
                apart(sp, at.ones_set, h_split_ready, b * TT)
                apart(sp, at.ones_set, h_out, b * TT * 16)
                apart(sp, at.ones_set, ab_ready, b * 2)
                if not (isinstance(b, int) and b == 0):
                    sp.dma_start(wide[:, :, :], attn_hbm[:, :, bass.ds(b * SEQ, SEQ)]).then_inc(in_done[0], 16)
                i = sp.value_load(ids[0:1, bass.ds(b, 1)], min_val=0, max_val=ADAPTERS - 1)
                sp.dma_start(a_stage[:, :, :], a_o[bass.ds(i, 1)].rearrange("a p c r -> (a p) c r")).then_inc(ab_in, 16)
                sp.dma_start(b_stage[:, :], b_o[bass.ds(i, 1)].rearrange("a p n -> (a p) n")).then_inc(ab_in, 16)

            def load_x(b):
                if not (isinstance(b, int) and b == 0):
                    apart(sp, at.ones_set, x1_out, b * 16)
                    apart(sp, at.ones_set, h_ready, b * 2)
                    apart(sp, at.ones_set, h_late, b * 2)
                sp.dma_start(res[:, :, :], x[bass.ds(b * SEQ, SEQ), :].rearrange("(t p) d -> p t d", p=P)).then_inc(
                    in_done[1], 16)

            def send_b(b):
                apart(sp, at.ones_set, o_made, b * TT)
                apart(sp, at.ones_set, ab_ready, b * 2 + 2)
                for r, part in enumerate((0, 1, 0)):
                    sp.dma_start(b_stack[RANK * r:RANK * (r + 1), :].bitcast(F32),
                                 b_split[:, part, :].bitcast(F32)).then_inc(b_stacked, 16)

            def send_low(b):
                sp.wait_ge(low_ready, b + 1)
                for r, part in enumerate((0, 0, 1)):
                    sp.dma_start(low_stack[RANK * r:RANK * (r + 1), :].bitcast(F32),
                                 low_split[:, part, :].bitcast(F32)).then_inc(low_stacked, 16)

            def gather(b, g):
                n = number(b, g)
                apart(sp, at.ones_set, at.pv_copied, (n + 1) * GH)
                apart(sp, at.ones_set, added, n)
                sp.dma_start(sum_hi[:, :], at.pv_raw[0:RANK, :, :]).then_inc(at.gathered, 16)
                sp.dma_start(sum_lo[:, :], at.pv_raw[RANK:2 * RANK, :, :]).then_inc(at.gathered, 16)
                sp.dma_start(sums[:, :], at.pv_raw[2 * RANK:2 * RANK + 1, :, :]).then_inc(at.gathered, 16)

            def spread(b, g):
                n = number(b, g)
                sp.wait_ge(inverted, n + 1)
                sp.dma_start(sums_hbm.rearrange("h (c n) -> (h c) n", c=TT), inverse[:, :]).then_inc(inverse_out, 16)
                sp.wait_ge(inverse_out, n * 16 + 16)
                sp.wait_ge(merged, n + 1)
                sp.dma_start(sum_lo[:, :], sums_hbm.rearrange("(o h) n -> o h n", o=1).broadcast_to(
                    [RANK, GH, SEQ])).then_inc(inverse_in, 16)

            def store_x1(b):
                sp.wait_ge(x1_ready, b * TT + TT)
                sp.dma_start(x1_hbm[bass.ds(b * SEQ, SEQ), :].rearrange("(t p) d -> p t d", p=P),
                             res[:, :, :]).then_inc(x1_out, 16)

            def store_h(b, t):
                apart(sp, at.ones_set, h_copied, b * TT + t + 1)
                sp.dma_start(h_hbm[:, :, bass.ds(b * SEQ + t * P, P)], h_turn[:, t, :, :]).then_inc(h_out, 16)

            def store_z(b):
                sp.wait_ge(z_ready, b + 1)
                for part in range(2):
                    sp.dma_start(z_hbm[part, :, bass.ds(b * SEQ, SEQ)],
                                 z_split[:, part, :].bitcast(F32)).then_inc(z_out, 16)

            def step(b, g):
                last = is_last(b)
                zero = isinstance(b, int) and b == 0
                first = zero and g == 0
                if g == 2 and not last:
                    store_h(b + 1, 0)
                    store_h(b + 1, 1)
                if not first:
                    gather(*group(b, g, -1))
                if g == 2 and not last:
                    store_h(b + 1, 2)
                    store_h(b + 1, 3)
                if not first:
                    spread(*group(b, g, -1))
                if g == 2 and has(b, 2):
                    load(b + 2)
                if g == 0 and not last:
                    load_x(b + 1)
                if not (last and g >= 2):
                    stack_send(sp, at, *group(b, g, 2), 0)
                if g == 3 and has(b, 2):
                    send_b(b + 2)
                    send_low(b + 2)
                if g == 1 and not zero:
                    store_z(b - 1)
                if g == 2 and not last:
                    store_x1(b + 1)
                if not (last and g >= 2):
                    stack_send(sp, at, *group(b, g, 2), 1)

            load(0)
            load_x(0)
            sp.dma_start(stage[:, :, :], wo).then_inc(stage_in, 16)
            sp.dma_start(a_full[:, :, :], low_a).then_inc(const_in, 16)
            sp.dma_start(sel[:, :], selector).then_inc(const_in, 16)
            send_b(0)
            send_low(0)
            sp.wait_ge(wo_a_made, 1)
            sp.dma_start(stage[:, :, :], wv).then_inc(stage_in, 16)
            store_x1(0)
            for t in range(TT):
                store_h(0, t)
            for pair in range(2):
                stack_send(sp, at, 0, 0, pair)
            load(1)
            for pair in range(2):
                stack_send(sp, at, 0, 1, pair)
            send_b(1)
            send_low(1)

            def body(b):
                for g in range(GROUPS):
                    step(b, g)

            batches(sp, body, 2)
            gather(BATCH - 1, GROUPS - 1)
            spread(BATCH - 1, GROUPS - 1)
            store_z(BATCH - 1)
            sp.wait_ge(z_out, BATCH * 32)
            sp.wait_ge(x1_out, BATCH * 16)
            sp.wait_ge(h_out, BATCH * TT * 16)

        @block.gpsimd
        def _(pool):
            for i in range(2):
                pool.memset(at.k_stack[i][96:98, :, :].bitcast(F32), 1.0).then_inc(at.ones_set, 1)
                pool.wait_ge(at.ones_set, i + 1)
            pool.memset(at.value[:, :, :, 2 * RANK:2 * RANK + 1].bitcast(F32), 1.0).then_inc(at.ones_set, 1)
            pool.memset(wo_a[:, :, :], 0.0).then_inc(zeroed, 1)

            def merge(b, g):
                n = number(b, g)
                apart(pool, at.ones_set, at.gathered, n * 48 + 48)
                pool.tensor_tensor(sum_hi[:, :], sum_hi[:, :], sum_lo[:, :], ALU.add).then_inc(merged, 1)
                pool.wait_ge(merged, n + 1)
                pool.wait_ge(inverse_in, n * 16 + 16)
                pool.tensor_tensor(sum_hi[:, :], sum_hi[:, :], sum_lo[:, :], ALU.mult).then_inc(normalised, 1)
                apart(pool, at.ones_set, normalised, n + 1)
                if g == 0:
                    apart(pool, at.ones_set, mod_made, b)
                    pool.tensor_copy(out_sum[:, :], sum_hi[:, :]).then_inc(added, 1)
                else:
                    apart(pool, at.ones_set, added, n)
                    pool.tensor_tensor(out_sum[:, :], out_sum[:, :], sum_hi[:, :], ALU.add).then_inc(added, 1)

            def attn_chunk(b, c):
                apart(pool, at.ones_set, attn_hi, (b - 1) * KC + c + 1)
                pool.tensor_tensor(attn_split[:, 1, c, :], wide[:, c, :], attn_split[:, 0, c, :],
                                  ALU.subtract).then_inc(attn_ready, 1)

            def adapter(b):
                apart(pool, at.ones_set, ab_hi, b * 2 + 2)
                pool.tensor_tensor(a_split[:, 1, :, :], a_stage[:, :, :], a_split[:, 0, :, :],
                                  ALU.subtract).then_inc(ab_ready, 1)
                pool.tensor_tensor(b_split[:, 1, :], b_stage[:, :], b_split[:, 0, :],
                                  ALU.subtract).then_inc(ab_ready, 1)

            def normalise_tile(b, t):
                apart(pool, at.ones_set, x1_ready, b * TT + t + 1)
                pool.tensor_scalar(wide[:, t, :], res[:, t, :], inv_root[:, 1, t:t + 1], None, ALU.mult).then_inc(h_late, 1)

            adapter(0)
            for t in range(2, TT):
                normalise_tile(0, t)
            for c in range(KC):
                attn_chunk(1, c)
            adapter(1)

            def body(b):
                for g in range(GROUPS):
                    if g == 2 and has(b, 1):
                        for t in range(2, TT):
                            normalise_tile(b + 1, t)
                    if g == 3 and has(b, 2):
                        for c in range(KC):
                            attn_chunk(b + 2, c)
                        adapter(b + 2)
                    if not (isinstance(b, int) and b == 0 and g == 0):
                        merge(*group(b, g, -1))

            batches(pool, body, 2)
            merge(BATCH - 1, GROUPS - 1)

        @block.scalar
        def _(act):
            def low_a_hi():
                act.wait_ge(const_in, 32)
                for c in range(KC):
                    act.activation(low_a_split[:, 0, c, :], a_full[:, c, :], ACT.Copy,
                                   scale=lnw[:, 1, c:c + 1]).then_inc(w_hi, 1)

            def value_weights_hi():
                act.wait_ge(vw_made, 2)
                for c in range(KC):
                    act.activation(vw_split[:, 0, c, :], at.pv_ps[:, c // 2, (c % 2) * VW:(c % 2 + 1) * VW], ACT.Copy,
                                   scale=lnw[:, 0, c:c + 1]).then_inc(w_hi, 1)

            def attn_chunk(b, c):
                if c == 0:
                    act.wait_ge(in_done[0], b * 16)
                    at_least(act, o_made, b * TT)
                act.activation(attn_split[:, 0, c, :], wide[:, c, :], ACT.Copy).then_inc(attn_hi, 1)

            def adapter(b):
                act.wait_ge(ab_in, b * 32 + 32)
                act.activation(a_split[:, 0, :, :], a_stage[:, :, :], ACT.Copy).then_inc(ab_hi, 1)
                at_least(act, b_stacked, b * 48)
                act.activation(b_split[:, 0, :], b_stage[:, :], ACT.Copy).then_inc(ab_hi, 1)

            def low(b):
                act.wait_ge(low_made, b + 1)
                act.activation(low_split[:, 0, :], at.scores_ps[0:RANK, 1, :], ACT.Copy).then_inc(low_hi, 1)

            def normalise_tile(b, t):
                if t == 0:
                    at_least(act, attn_ready, b * KC)
                act.wait_ge(x1_ready, b * TT + t + 1)
                act.activation(wide[:, t, :], res[:, t, :], ACT.Copy, scale=inv_root[:, 1, t:t + 1]).then_inc(h_ready, 1)

            def h_tile(b, t):
                act.wait_ge(h_turned, b * TT + t + 1)
                bank = lin_ps[:, t % 2, :].rearrange("p (c n) -> p c n", c=KC)
                act.activation(h_turn[:, t, :, :], bank, ACT.Copy).then_inc(h_copied, 1)
                act.activation(h_split[:, 0, :, t * P:t * P + P], bank, ACT.Copy).then_inc(h_hi, 1)

            def projected(b, g, i):
                n = number(b, g)
                act.wait_ge(qk_made[i], n + 1)
                for pair in range(2):
                    at_least(act, at.stacked[pair], n * 96)
                split = at.k_split if i else at.q_split
                act.activation(split[:, 0, :], lin_ps[:, i, :], ACT.Copy).then_inc(qk_hi[i], 1)

            def value(b, bank):
                act.wait_ge(v_made, b * 2 + bank + 1)
                at_least(act, at.pv_done, (b * GROUPS - 1) * UNITS)
                act.activation(at.value[:, 2 * bank:2 * bank + 2, 0:EARLY, 0:RANK], values[:, 2 * bank:2 * bank + 2, 0:EARLY, :],
                               ACT.Copy).then_inc(value_hi, 1)

            def value_rest(b):
                act.wait_ge(at.value_ready, b * 3 + 2)
                at_least(act, at.pv_done, b * GROUPS * UNITS)
                act.activation(at.value[:, :, EARLY:, 0:RANK], values[:, :, EARLY:, :], ACT.Copy).then_inc(value_hi, 1)

            def tanh(b):
                act.wait_ge(mod_made, b + 1)
                act.wait_ge(at.shifted, min(number(b, 6), BATCH * GROUPS) * 16 if isinstance(b, int) else
                            b * GROUPS * 16 + 96)
                act.activation(mod[:, :], at.scores_ps[0:RANK, 1, :], ACT.Tanh).then_inc(mod_done, 1)

            def z_part(b):
                act.wait_ge(z_made, b + 1)
                act.wait_ge(low_stacked, min(b + 3, BATCH) * 48 if isinstance(b, int) else b * 48 + 144)
                act.activation(z_split[:, 0, :], mod[:, :], ACT.Copy).then_inc(z_hi, 1)

            def h_times_a(b):
                act.wait_ge(h_low_made, b + 1)
                at_least(act, z_made, b)
                act.activation(h_low[:, :], at.scores_ps[0:RANK, 1, :], ACT.Copy).then_inc(h_low_copied, 1)

            def step(b, g):
                last = is_last(b)
                zero = isinstance(b, int) and b == 0
                first = zero and g == 0
                for slot in range(UNITS):
                    if slot == 2 and not first:
                        pv_copy(act, at, *group(b, g, -1), 3)
                    if slot in (5, 8, 11):
                        pv_copy(act, at, b, g, (slot - 5) // 3)
                    exp_unit(act, at, b, g, slot)
                    if slot == 9 and not (last and g == GROUPS - 1):
                        if g == 1 and not zero:
                            act.wait_ge(z_ready, b)
                        shift_copy(act, at, *group(b, g, 1))
                        shift_send(act, at, *group(b, g, 1))
                    if g == 3 and slot == 9 and not last:
                        value(b + 1, 0)
                    if g == 0 and not zero:
                        if slot == 0:
                            value(b, 1)
                        if slot == 2:
                            value_rest(b)
                    if g == 3 and has(b, 2):
                        if 3 <= slot < 7:
                            attn_chunk(b + 2, slot - 3)
                        if slot == 5:
                            adapter(b + 2)
                        if slot == 10:
                            if not zero:
                                act.wait_ge(z_out, b * 32)
                            low(b + 2)
                    if g == 1 and not zero:
                        if slot == 0:
                            tanh(b - 1)
                        if slot == 4:
                            z_part(b - 1)
                    if g == 2 and slot == 0:
                        h_times_a(b)
                    if g == 2 and slot == 0 and not last:
                        for t in range(2):
                            normalise_tile(b + 1, t)
                    if g == 2 and 2 <= slot < 6 and not last:
                        h_tile(b + 1, slot - 2)
                    for to in left_b(b, g, slot):
                        projected(*to)

            adapter(0)
            low(0)
            low_a_hi()
            for t in range(2):
                normalise_tile(0, t)
            for t in range(TT):
                h_tile(0, t)
            for g in range(2):
                for i in range(2):
                    projected(0, g, i)
            value_weights_hi()
            for c in range(KC):
                attn_chunk(1, c)
            adapter(1)
            shift_copy(act, at, 0, 0)
            shift_send(act, at, 0, 0)
            for bank in range(2):
                value(0, bank)
            value_rest(0)
            low(1)

            def body(b):
                for g in range(GROUPS):
                    step(b, g)

            batches(act, body, 2)
            pv_copy(act, at, BATCH - 1, GROUPS - 1, 3)
            tanh(BATCH - 1)
            z_part(BATCH - 1)

        @block.vector
        def _(dve):
            def spread_heads():
                dve.wait_ge(wo_a_made, 1)
                dve.wait_ge(zeroed, 1)
                for h in range(GH):
                    rows = slice(h * HD, h * HD + HD)
                    dve.tensor_copy(wo_a[rows, :, h * RANK:(h + 1) * RANK],
                                    at.pv_ps[rows, 0, 0:TT * RANK].rearrange("p (t r) -> p t r", t=TT)).then_inc(wo_a_copied, 1)

            def low_a_lo():
                for c in range(KC):
                    dve.wait_ge(w_hi, c + 1)
                    dve.scalar_tensor_tensor(out=low_a_split[:, 1, c, :], in0=a_full[:, c, :], scalar=lnw[:, 1, c:c + 1],
                                             in1=low_a_split[:, 0, c, :], op0=ALU.mult,
                                             op1=ALU.subtract).then_inc(w_ready, 1)

            def value_weights_lo():
                for c in range(KC):
                    dve.wait_ge(w_hi, KC + c // 2 * 2 + 2)
                    dve.scalar_tensor_tensor(out=vw_split[:, 1, c, :], in0=at.pv_ps[:, c // 2, (c % 2) * VW:(c % 2 + 1) * VW],
                                             scalar=lnw[:, 0, c:c + 1], in1=vw_split[:, 0, c, :], op0=ALU.mult,
                                             op1=ALU.subtract).then_inc(w_ready, 1)

            def low(b):
                dve.wait_ge(low_hi, b + 1)
                dve.tensor_tensor(low_split[:, 1, :], at.scores_ps[0:RANK, 1, :], low_split[:, 0, :],
                                  ALU.subtract).then_inc(low_ready, 1)

            def add_residual(b, t):
                dve.wait_ge(o_made, b * TT + t + 1)
                dve.wait_ge(in_done[1], b * 16 + 16)
                dve.tensor_tensor(res[:, t, :], lin_ps[:, t % 2, :], res[:, t, :], ALU.add).then_inc(o_added, 1)
                dve.wait_ge(o_added, b * TT + t + 1)
                dve.bn_stats(stats[:, t, :], res[:, t, :]).then_inc(stats_done, 1)

            def norm_factors(b):
                done = b * LN_STEPS
                apart(dve, at.ones_set, stats_done, (b + 1) * TT)
                for t in range(TT):
                    dve.bn_aggr(mean_var[:, t, :], stats[:, t, :]).then_inc(ln_step, 1)
                dve.wait_ge(ln_step, done + TT)
                dve.tensor_scalar(squares[:, 0, :], mean_var[:, :, 1], LN_EPS, None, ALU.add).then_inc(ln_step, 1)
                dve.wait_ge(ln_step, done + TT + 1)
                dve.reciprocal(newton[:, 0, :], squares[:, 0, :]).then_inc(ln_step, 1)
                dve.wait_ge(ln_step, done + TT + 2)
                dve.tensor_tensor(newton[:, 1, :], newton[:, 0, :], mean_var[:, :, 1], ALU.mult).then_inc(ln_step, 1)
                dve.wait_ge(ln_step, done + TT + 3)
                dve.tensor_scalar(squares[:, 1, :], newton[:, 1, :], RMS_EPS, None, ALU.add).then_inc(ln_step, 1)
                dve.wait_ge(ln_step, done + TT + 4)
                rsqrt(dve, ln_step, done + TT + 4, inv_root[:, :, :], squares[:, :, :], newton[:, :, :])

            def normalise_tile(b, t):
                dve.wait_ge(ln_step, b * LN_STEPS + TT + 4 + RSQRT_STEPS)
                dve.tensor_scalar(res[:, t, :], res[:, t, :], mean_var[:, t, 0:1], inv_root[:, 0, t:t + 1],
                                  ALU.subtract, ALU.mult).then_inc(x1_ready, 1)

            def h_tile(b, t):
                dve.wait_ge(h_hi, b * TT + t + 1)
                dve.tensor_tensor(h_split[:, 1, :, t * P:t * P + P], h_turn[:, t, :, :],
                                  h_split[:, 0, :, t * P:t * P + P], ALU.subtract).then_inc(h_split_ready, 1)

            def projected(b, g, i):
                dve.wait_ge(qk_hi[i], number(b, g) + 1)
                split = at.k_split if i else at.q_split
                dve.tensor_tensor(split[:, 1, :], lin_ps[:, i, :], split[:, 0, :],
                                  ALU.subtract).then_inc(qk_ready[i], 1)

            def value(b, bank):
                dve.wait_ge(value_hi, b * 3 + bank + 1)
                tiles = slice(2 * bank, 2 * bank + 2)
                dve.tensor_tensor(at.value[:, tiles, 0:EARLY, RANK:2 * RANK], values[:, tiles, 0:EARLY, :],
                                  at.value[:, tiles, 0:EARLY, 0:RANK], ALU.subtract).then_inc(at.value_ready, 1)

            def value_rest(b):
                dve.wait_ge(value_hi, b * 3 + 3)
                dve.tensor_tensor(at.value[:, :, EARLY:, RANK:2 * RANK], values[:, :, EARLY:, :],
                                  at.value[:, :, EARLY:, 0:RANK], ALU.subtract).then_inc(at.value_ready, 1)

            def invert(b, g):
                n = number(b, g)
                dve.wait_ge(at.gathered, n * 48 + 48)
                at_least(dve, inverse_out, n * 16)
                dve.reciprocal(inverse[:, :], sums[:, :]).then_inc(inverted, 1)

            def z_term(b):
                dve.wait_ge(mod_done, b + 1)
                dve.wait_ge(h_low_copied, b + 1)
                dve.scalar_tensor_tensor(out=mod[:, :], in0=mod[:, :], scalar=MOD_SCALE, in1=h_low[:, :],
                                         op0=ALU.mult, op1=ALU.mult).then_inc(z_made, 1)

            def z_part(b):
                dve.wait_ge(z_hi, b + 1)
                dve.tensor_tensor(z_split[:, 1, :], mod[:, :], z_split[:, 0, :], ALU.subtract).then_inc(z_ready, 1)

            def step(b, g):
                last = is_last(b)
                zero = isinstance(b, int) and b == 0
                first = zero and g == 0
                for slot in range(UNITS):
                    if slot > 0:
                        lo_unit(dve, at, b, g, slot - 1)
                    elif not first:
                        lo_unit(dve, at, *group(b, g, -1), UNITS - 1)
                    if not (last and g == GROUPS - 1):
                        for k in score_share(slot):
                            score_max(dve, at, rowmask, *group(b, g, 1), k)
                        if slot == SCORE_SLOTS[-1]:
                            shift_split(dve, at, *group(b, g, 1))
                    if slot == 5 and not first:
                        invert(*group(b, g, -1))
                    if g == 3 and slot == 10 and not last:
                        value(b + 1, 0)
                    if g == 0 and not zero:
                        if slot == 1:
                            value(b, 1)
                        if slot == 2:
                            value_rest(b)
                    if g == 3 and slot == 11 and has(b, 2):
                        low(b + 2)
                    if g == 1 and not zero:
                        if slot == 3:
                            z_term(b - 1)
                        if slot == 5:
                            z_part(b - 1)
                    if g == 0 and slot == 10 and not last:
                        add_residual(b + 1, 0)
                    if g == 1 and not last:
                        if slot in (1, 7, 9):
                            add_residual(b + 1, 1 + (1, 7, 9).index(slot))
                        if slot == 10:
                            norm_factors(b + 1)
                        if slot == 11:
                            normalise_tile(b + 1, 0)
                            normalise_tile(b + 1, 1)
                    if g == 2 and not last:
                        if slot == 0:
                            normalise_tile(b + 1, 2)
                            normalise_tile(b + 1, 3)
                        if H_LO <= slot < H_LO + TT:
                            h_tile(b + 1, slot - H_LO)
                    if slot > 0:
                        for to in left_b(b, g, slot - 1):
                            projected(*to)

            low(0)
            for t in range(TT):
                add_residual(0, t)
            norm_factors(0)
            for t in range(TT):
                normalise_tile(0, t)
            spread_heads()
            low_a_lo()
            for t in range(TT):
                h_tile(0, t)
            for g in range(2):
                for i in range(2):
                    projected(0, g, i)
            value_weights_lo()
            for k in range(UNITS):
                score_max(dve, at, rowmask, 0, 0, k)
            shift_split(dve, at, 0, 0)
            for bank in range(2):
                value(0, bank)
            value_rest(0)
            low(1)

            def body(b):
                for g in range(GROUPS):
                    step(b, g)

            batches(dve, body, 2)
            lo_unit(dve, at, BATCH - 1, GROUPS - 1, UNITS - 1)
            invert(BATCH - 1, GROUPS - 1)
            z_term(BATCH - 1)
            z_part(BATCH - 1)

        @block.tensor
        def _(pe):
            def output_times_a():
                pe.wait_ge(const_in, 32)
                pe.wait_ge(stage_in, 16)
                for t in range(TT):
                    for c in range(KC):
                        mm = pe.matmul(at.pv_ps[:, 0, t * RANK:(t + 1) * RANK], stage[:, c, t * P:t * P + P], a_full[:, c, :],
                                       start=(t == 0 and c == 0), stop=(c == KC - 1), skip_group_check=True)
                mm.then_inc(wo_a_made, 1)

            def merge_values():
                pe.wait_ge(wo_a_copied, GH)
                pe.wait_ge(stage_in, 32)
                for c in range(KC):
                    for t in range(TT):
                        mm = pe.matmul(at.pv_ps[:, c // 2, (c % 2) * VW + t * GH * RANK:(c % 2) * VW + (t + 1) * GH * RANK],
                                       stage[:, t, c * P:c * P + P], wo_a[:, t, :], start=(c % 2 == 0 and t == 0),
                                       stop=True, skip_group_check=True)
                    if c % 2 == 1:
                        mm.then_inc(vw_made, 1)

            pe.wait_ge(at.ones_set, 3)

            def low(b, items):
                for x in items:
                    c, (w, a) = x // 3, PASSES[x % 3]
                    if x == 0:
                        at_least(pe, at.score_read, ((b - 1) * GROUPS + 1) * UNITS)
                        at_least(pe, attn_ready, b * KC)
                        pe.wait_ge(ab_ready, (b + 1) * 2)
                    mm = pe.matmul(at.scores_ps[0:RANK, 1, :], a_split[:, w, c, :], attn_split[:, a, c, :],
                                   start=(x == 0), stop=(x == 3 * KC - 1))
                    if x == 3 * KC - 1:
                        mm.then_inc(low_made, 1)

            def project_out(b, items):
                for x in items:
                    t, y = divmod(x, 3 * KC + 1)
                    bank = t % 2
                    if y == 0 and not (isinstance(b, int) and b == 0):
                        pe.wait_ge(qk_ready[bank], b * GROUPS - 1 + t // 2)
                    elif y == 0 and t >= 2:
                        pe.wait_ge(o_added, b * TT + t - 1)
                    if y < 3 * KC:
                        c, (w, a) = y // 3, PASSES[y % 3]
                        pe.matmul(lin_ps[:, bank, :], attn_split[:, a, c, t * P:t * P + P], wo_split[:, w, c, :],
                                  start=(y == 0), stop=False)
                    else:
                        pe.wait_ge(low_stacked, b * 48 + 48)
                        pe.wait_ge(b_stacked, b * 48 + 48)
                        pe.matmul(lin_ps[:, bank, :], low_stack[:, t * P:t * P + P], b_stack[:, :],
                                  start=False, stop=True).then_inc(o_made, 1)

            def turn_h(b, t):
                bank = t % 2
                pe.wait_ge(*((h_ready, b * 2 + t + 1) if t < 2 else (h_late, b * 2 + t - 1)))
                if t >= 2:
                    pe.wait_ge(h_hi, b * TT + t - 1)
                else:
                    pe.wait_ge(o_added, b * TT + 3 + t)
                for c in range(KC):
                    mm = pe.transpose(lin_ps[:, bank, c * P:c * P + P], wide[:, t, c * P:c * P + P], eye[:, :].bitcast(F32))
                mm.then_inc(h_turned, 1)

            def project(b, g, i, items):
                for x in items:
                    if x == 0:
                        if g == 0:
                            pe.wait_ge(h_hi, (b + 1) * TT)
                        elif g == 2:
                            pe.wait_ge(at.value_ready, b * 3 + 3)
                        elif g == 3 and not is_last(b):
                            pe.wait_ge(o_added, (b + 1) * TT + 1 + i)
                        else:
                            pe.wait_ge(qk_ready[i], number(b, g))
                    (w, a), c = HI_FIRST[x // KC], x % KC
                    if x == 2 * KC and g == 0:
                        pe.wait_ge(h_split_ready, (b + 1) * TT)
                    mm = pe.matmul(lin_ps[:, i, :], qk_split[i][:, w, c, g * P:g * P + P], h_split[:, a, c, :],
                                   start=(x == 0), stop=(x == 3 * KC - 1))
                    if x == 3 * KC - 1:
                        mm.then_inc(qk_made[i], 1)

            def project_value(b, bank, items):
                for x in items:
                    if x == 0:
                        pe.wait_ge(qk_ready[bank], b * GROUPS + 2)
                    t, y = divmod(x, 3 * KC)
                    c, (w, a) = y // 3, PASSES[y % 3]
                    rows = (2 * bank + t) * P
                    mm = pe.matmul(lin_ps[:, bank, t * VW:(t + 1) * VW], h_split[:, a, c, rows:rows + P], vw_split[:, w, c, :],
                                   start=(x == 0), stop=(y == 3 * KC - 1), skip_group_check=True)
                    if x == 2 * 3 * KC - 1:
                        mm.then_inc(v_made, 1)

            def h_times_a(b, items):
                for x in items:
                    if x == 0:
                        pe.wait_ge(at.score_read, (b * GROUPS + 3) * UNITS)
                    c, (w, a) = x // 3, PASSES[x % 3]
                    mm = pe.matmul(at.scores_ps[0:RANK, 1, :], low_a_split[:, w, c, :], h_split[:, a, c, :],
                                   start=(x == 0), stop=(x == 3 * KC - 1))
                    if x == 3 * KC - 1:
                        mm.then_inc(h_low_made, 1)

            def modulation(b):
                apart(pe, at.ones_set, added, (b + 1) * GROUPS)
                apart(pe, at.ones_set, at.score_read, min(number(b, 6), BATCH * GROUPS) * UNITS if isinstance(b, int) else
                      (b * GROUPS + 6) * UNITS)
                pe.matmul(at.scores_ps[0:RANK, 1, :], sel[:, :], out_sum[:, :], start=True, stop=True).then_inc(mod_made, 1)

            def step(b, g):
                last = is_last(b)
                zero = isinstance(b, int) and b == 0
                first = zero and g == 0
                for slot in range(UNITS):
                    score_t_unit(pe, at, eye_bf, colmask, b, g, slot)
                    if slot == 9 and not (last and g == GROUPS - 1):
                        shift_turn(pe, at, eye, *group(b, g, 1))
                    if slot == 2 and g == 0 and not last:
                        pe.wait_ge(low_ready, b + 2)
                    if slot == 2 and g == 1 and not zero:
                        pe.wait_ge(mod_done, b)
                    if slot == 2 and g == 2:
                        pe.wait_ge(h_low_copied, b + 1)
                    if not (last and g == GROUPS - 1):
                        for k in score_share(slot):
                            score_unit(pe, at, *group(b, g, 1), k)
                    if slot >= 2:
                        pv_unit(pe, at, b, g, slot - 2)
                    if slot < 2 and not first:
                        pv_unit(pe, at, *group(b, g, -1), UNITS - 2 + slot)
                    if g == 1 and slot == 0 and not zero:
                        modulation(b - 1)
                    if g < 2 and not last:
                        project_out(b + 1, out_items(g, slot))
                    if g == 1 and slot in (10, 11):
                        h_times_a(b, share(3 * KC, 2, slot - 10))
                    if g == 2 and 1 <= slot < 5 and not last:
                        turn_h(b + 1, slot - 1)
                    if g == 3 and slot in (8, 9) and has(b, 2):
                        low(b + 2, share(3 * KC, 2, slot - 8))
                    for to in made_b(b, g, slot):
                        project(*to)
                    for to in value_items(b, g, slot):
                        project_value(*to)

            low(0, range(3 * KC))
            project_out(0, range(TT * (3 * KC + 1)))
            output_times_a()
            for t in range(TT):
                turn_h(0, t)
            for g in range(2):
                for i in range(2):
                    project(0, g, i, range(3 * KC))
            merge_values()
            for k in range(UNITS):
                score_unit(pe, at, 0, 0, k)
            shift_turn(pe, at, eye, 0, 0)
            pe.wait_ge(w_ready, 2 * KC)
            for bank in range(2):
                project_value(0, bank, range(2 * 3 * KC))
            low(1, range(3 * KC))

            def body(b):
                for g in range(GROUPS):
                    step(b, g)

            batches(pe, body, 2)
            for k in range(UNITS - 2, UNITS):
                pv_unit(pe, at, BATCH - 1, GROUPS - 1, k)
            modulation(BATCH - 1)


FT = F // 2 // P
W_COLS = 2 * KC * P + D


class Run:

    def __init__(self, n, pair, used):
        self.n, self.pair, self.used = n, pair, used

    def next(self):
        return Run(self.n + 1, 1 - self.pair, self.used + self.pair)

    def former(self):
        return Run(self.n - 1, 1 - self.pair, self.used + self.pair - 1)

    def is_(self, n):
        return isinstance(self.n, int) and self.n == n


def runs(eng, body):
    for second in range(2):
        first = second * BATCH
        body(Run(first, 0, first // 2), second)
        with eng.Fori(0, BATCH // 2 - 1) as i:
            body(Run(i * 2 + (first + 1), 1, i + first // 2), second)
            body(Run(i * 2 + (first + 2), 0, i + (first // 2 + 1)), second)
        body(Run(first + BATCH - 1, 1, (first + BATCH) // 2 - 1), second)


def mlp_layer(nc, mlp_w, low_b, ln_w, x1_hbm, h_hbm, z_hbm, out):
    with ExitStack() as ctx:
        def sb(what, shape, dt=F32):
            return ctx.enter_context(nc.sbuf_tensor(f"c_{what}", shape, dt))

        def sem(what):
            return ctx.enter_context(nc.semaphore(f"c_{what}"))

        gate_ps = ctx.enter_context(nc.psum_tensor("c_gate_ps", [P, 2, SEQ], F32))
        up_ps = ctx.enter_context(nc.psum_tensor("c_up_ps", [P, 2, SEQ], F32))
        down_ps = ctx.enter_context(nc.psum_tensor("c_down_ps", [P, TT, D], F32))

        w_split = sb("w_split", [P, 2, FT, W_COLS], F32R)
        w_stage = sb("w_stage", [P, 2, W_COLS])
        lnw = sb("lnw", [P, 2, KC])
        low_b_stage = sb("low_b_stage", [P, RANK * F // P])
        low_b_split = sb("low_b_split", [P, 2, RANK * F // P], F32R)
        low_b_stack = sb("low_b_stack", [3 * RANK, F], F32R)
        z_stack = [sb(f"z_stack{i}", [3 * RANK, SEQ], F32R) for i in range(2)]
        h_stage = sb("h_stage", [P, KC, SEQ])
        h_split = [sb(f"h_split{i}", [P, 2, KC, SEQ], F32R) for i in range(2)]
        res = [sb(f"res{i}", [P, TT, D]) for i in range(2)]
        gate = sb("gate", [P, 2, SEQ])
        product = sb("product", [P, 2, SEQ])
        product_split = sb("product_split", [P, 2, 2, SEQ], F32R)
        stats = sb("stats", [P, TT, 6])
        mean_var = sb("mean_var", [P, TT, 2])
        var_eps = sb("var_eps", [P, TT])
        inv_root = sb("inv_root", [P, TT])
        newton = sb("newton", [P, TT])

        const_in = sem("const_in")
        b_hi = sem("b_hi")
        b_ready = sem("b_ready")
        b_stacked = sem("b_stacked")
        w_in = [sem(f"w_in{i}") for i in range(2)]
        w_hi = sem("w_hi")
        w_ready = sem("w_ready")
        h_in = sem("h_in")
        h_hi = sem("h_hi")
        h_ready = sem("h_ready")
        z_in = [sem(f"z_in{i}") for i in range(2)]
        res_in = [sem(f"res_in{i}") for i in range(2)]
        res_out = [sem(f"res_out{i}") for i in range(2)]
        gate_made = sem("gate_made")
        up_made = sem("up_made")
        gate_done = sem("gate_done")
        product_done = sem("product_done")
        product_hi = sem("product_hi")
        product_ready = sem("product_ready")
        down_done = sem("down_done")
        res_added = sem("res_added")
        ln_step = sem("ln_step")
        normalised = sem("normalised")

        LN_STEPS = 2 * TT + 1 + RSQRT_STEPS
        RUNS = 2 * BATCH

        block = ctx.enter_context(nc.Block())

        @block.gpsimd
        def _(pool):
            for k in range(2 * FT):
                if k >= 2:
                    pool.wait_ge(w_ready, k - 1)
                pool.dma_start(w_stage[:, k % 2, :], mlp_w[k]).then_inc(w_in[k % 2], 16)

        @block.sync
        def _(sp):
            def load_h(run, rows):
                at_least(sp, h_ready, run.n * KC)
                sp.dma_start(h_stage[:, :, :], h_hbm[:, :, rows]).then_inc(h_in, 16)

            def load_z(run, rows):
                at_least(sp, gate_made, (run.n - 1) * FT)
                for r, part in enumerate((0, 0, 1)):
                    sp.dma_start(z_stack[run.pair][RANK * r:RANK * (r + 1), :].bitcast(F32),
                                 z_hbm[part, :, rows]).then_inc(z_in[run.pair], 16)

            def load_res(run, rows):
                at_least(sp, res_out[run.pair], run.used * 16)
                sp.dma_start(res[run.pair][:, :, :],
                             x1_hbm[rows, :].rearrange("(t p) d -> p t d", p=P)).then_inc(res_in[run.pair], 16)

            def store(run, rows, second):
                if second:
                    sp.wait_ge(normalised, (run.n - BATCH + 1) * TT)
                else:
                    sp.wait_ge(res_added, (run.n + 1) * TT)
                sp.dma_start((out if second else x1_hbm)[rows, :].rearrange("(t p) d -> p t d", p=P),
                             res[run.pair][:, :, :]).then_inc(res_out[run.pair], 16)

            def rows_of(n, second):
                return bass.ds((n - BATCH) * SEQ if second else n * SEQ, SEQ)

            def body(run, second):
                following = run.next()
                next_second = second or run.is_(BATCH - 1)
                if not run.is_(RUNS - 1):
                    load_h(following, rows_of(following.n, next_second))
                    load_z(following, rows_of(following.n, next_second))
                if not run.is_(0):
                    former = run.former()
                    former_second = second and not run.is_(BATCH)
                    store(former, rows_of(former.n, former_second), former_second)
                if not run.is_(RUNS - 1):
                    load_res(following, rows_of(following.n, next_second))

            start = Run(0, 0, 0)
            load_h(start, bass.ds(0, SEQ))
            sp.dma_start(lnw[:, :, :], ln_w).then_inc(const_in, 16)
            sp.dma_start(low_b_stage[:, :], low_b).then_inc(const_in, 16)
            load_z(start, bass.ds(0, SEQ))
            sp.wait_ge(b_ready, 1)
            for r, part in enumerate((0, 1, 0)):
                sp.dma_start(low_b_stack[RANK * r:RANK * (r + 1), :].bitcast(F32),
                             low_b_split[:, part, :].bitcast(F32)).then_inc(b_stacked, 16)
            load_res(start, bass.ds(0, SEQ))
            runs(sp, body)
            end = Run(RUNS - 1, 1, BATCH - 1)
            store(end, rows_of(end.n, True), True)
            for i in range(2):
                sp.wait_ge(res_out[i], BATCH * 16)

        def weight_splits(run, ft):
            if run.is_(0) and ft + 2 < FT:
                return (ft + 2,)
            if run.is_(BATCH - 1) and ft >= 2:
                return (FT + ft - 2,)
            if run.is_(BATCH) and ft < 2:
                return (2 * FT - 2 + ft,)
            return ()

        @block.scalar
        def _(act):
            def weights(k):
                act.wait_ge(w_in[k % 2], (k // 2 + 1) * 16)
                kt = k % FT
                if k >= FT:
                    act.wait_ge(down_done, ((BATCH - 1) * FT + kt + 1) * TT)
                for c in range(KC):
                    cols = slice(c * 2 * P, (c + 1) * 2 * P)
                    act.activation(w_split[:, 0, kt, cols], w_stage[:, k % 2, cols], ACT.Copy, scale=lnw[:, 1, c:c + 1])
                act.activation(w_split[:, 0, kt, 2 * KC * P:], w_stage[:, k % 2, 2 * KC * P:],
                               ACT.Copy).then_inc(w_hi, 1)

            def h_chunk(run, c):
                if c == 0:
                    act.wait_ge(h_in, run.n * 16 + 16)
                    at_least(act, up_made, (run.n - 1) * FT)
                act.activation(h_split[run.pair][:, 0, c, :], h_stage[:, c, :], ACT.Copy).then_inc(h_hi, 1)

            def body(run, second):
                for ft in range(FT):
                    p = run.n * FT + ft
                    bank = ft % 2
                    act.wait_ge(gate_made, p + 1)
                    at_least(act, product_done, p - 1)
                    act.activation(gate[:, bank, :], gate_ps[:, bank, :], ACT.Silu).then_inc(gate_done, 1)
                    act.wait_ge(product_done, p + 1)
                    at_least(act, down_done, (p - 1) * TT)
                    act.activation(product_split[:, bank, 0, :], product[:, bank, :], ACT.Copy).then_inc(product_hi, 1)
                    if 2 <= ft < 2 + KC and not run.is_(RUNS - 1):
                        h_chunk(run.next(), ft - 2)
                    for k in weight_splits(run, ft):
                        weights(k)

            start = Run(0, 0, 0)
            act.wait_ge(const_in, 32)
            for c in range(KC):
                h_chunk(start, c)
            act.activation(low_b_split[:, 0, :], low_b_stage[:, :], ACT.Copy).then_inc(b_hi, 1)
            weights(0)
            weights(1)
            runs(act, body)

        @block.vector
        def _(dve):
            def weights(k):
                dve.wait_ge(w_hi, k + 1)
                kt = k % FT
                for c in range(KC):
                    cols = slice(c * 2 * P, (c + 1) * 2 * P)
                    dve.scalar_tensor_tensor(out=w_split[:, 1, kt, cols], in0=w_stage[:, k % 2, cols],
                                             scalar=lnw[:, 1, c:c + 1], in1=w_split[:, 0, kt, cols], op0=ALU.mult,
                                             op1=ALU.subtract)
                dve.tensor_tensor(w_split[:, 1, kt, 2 * KC * P:], w_stage[:, k % 2, 2 * KC * P:],
                                  w_split[:, 0, kt, 2 * KC * P:], ALU.subtract).then_inc(w_ready, 1)

            def h_chunk(run, c):
                dve.wait_ge(h_hi, run.n * KC + c + 1)
                dve.tensor_tensor(h_split[run.pair][:, 1, c, :], h_stage[:, c, :], h_split[run.pair][:, 0, c, :],
                                  ALU.subtract).then_inc(h_ready, 1)

            def add(run, second):
                dve.wait_ge(res_in[run.pair], run.used * 16 + 16)
                for t in range(TT):
                    dve.wait_ge(down_done, ((run.n + 1) * FT - 1) * TT + t + 1)
                    dve.scalar_tensor_tensor(out=res[run.pair][:, t, :], in0=res[run.pair][:, t, :],
                                             scalar=1.0 if second else 2.0, in1=down_ps[:, t, :], op0=ALU.mult,
                                             op1=ALU.add).then_inc(res_added, 1)

            def norm_factors(run):
                m = run.n - BATCH
                done = m * LN_STEPS
                for t in range(TT):
                    dve.wait_ge(res_added, run.n * TT + t + 1)
                    dve.bn_stats(stats[:, t, :], res[run.pair][:, t, :]).then_inc(ln_step, 1)
                apart(dve, const_in, ln_step, done + TT)
                for t in range(TT):
                    dve.bn_aggr(mean_var[:, t, :], stats[:, t, :]).then_inc(ln_step, 1)
                dve.wait_ge(ln_step, done + 2 * TT)
                dve.tensor_scalar(var_eps[:, :], mean_var[:, :, 1], LN_EPS, None, ALU.add).then_inc(ln_step, 1)
                dve.wait_ge(ln_step, done + 2 * TT + 1)
                rsqrt(dve, ln_step, done + 2 * TT + 1, inv_root[:, :], var_eps[:, :], newton[:, :])

            def normalise(run):
                m = run.n - BATCH
                dve.wait_ge(ln_step, (m + 1) * LN_STEPS)
                for t in range(TT):
                    dve.tensor_scalar(res[run.pair][:, t, :], res[run.pair][:, t, :], mean_var[:, t, 0:1],
                                      inv_root[:, t:t + 1], ALU.subtract, ALU.mult).then_inc(normalised, 1)

            def body(run, second):
                former_second = second and not run.is_(BATCH)
                for ft in range(FT):
                    p = run.n * FT + ft
                    bank = ft % 2
                    if ft == 1 and not run.is_(0):
                        add(run.former(), former_second)
                    dve.wait_ge(gate_done, p + 1)
                    dve.wait_ge(up_made, p + 1)
                    dve.tensor_tensor(product[:, bank, :], up_ps[:, bank, :], gate[:, bank, :],
                                      ALU.mult).then_inc(product_done, 1)
                    dve.wait_ge(product_hi, p + 1)
                    dve.tensor_tensor(product_split[:, bank, 1, :], product[:, bank, :], product_split[:, bank, 0, :],
                                      ALU.subtract).then_inc(product_ready, 1)
                    if former_second and ft == 1:
                        norm_factors(run.former())
                    if former_second and ft == 2:
                        normalise(run.former())
                    if 2 <= ft < 2 + KC and not run.is_(RUNS - 1):
                        h_chunk(run.next(), ft - 2)
                    for k in weight_splits(run, ft):
                        weights(k)

            start = Run(0, 0, 0)
            dve.wait_ge(const_in, 32)
            for c in range(KC):
                h_chunk(start, c)
            dve.wait_ge(b_hi, 1)
            dve.tensor_tensor(low_b_split[:, 1, :], low_b_stage[:, :], low_b_split[:, 0, :],
                              ALU.subtract).then_inc(b_ready, 1)
            weights(0)
            weights(1)
            runs(dve, body)
            end = Run(RUNS - 1, 1, BATCH - 1)
            add(end, True)
            norm_factors(end)
            normalise(end)

        @block.tensor
        def _(pe):
            def down(p, kt, n):
                pe.wait_ge(product_ready, p + 1)
                for t in range(TT):
                    if kt == 0:
                        at_least(pe, res_added, (n - 1) * TT + t + 1)
                    for i, (w, a) in enumerate(PASSES):
                        mm = pe.matmul(down_ps[:, t, :], product_split[:, kt % 2, a, t * P:t * P + P],
                                       w_split[:, w, kt, 2 * KC * P:], start=(kt == 0 and i == 0),
                                       stop=(kt == FT - 1 and i == 2), skip_group_check=True)
                    mm.then_inc(down_done, 1)

            def body(run, second):
                for ft in range(FT):
                    p = run.n * FT + ft
                    bank = ft % 2
                    if ft == 0:
                        pe.wait_ge(h_ready, run.n * KC + KC)
                    if run.is_(0) or run.is_(BATCH):
                        pe.wait_ge(w_ready, second * FT + ft + 1)
                    at_least(pe, gate_done, p - 1)
                    for c in range(KC):
                        for w, a in PASSES:
                            pe.matmul(gate_ps[:, bank, :], w_split[:, w, ft, c * 2 * P:c * 2 * P + P],
                                      h_split[run.pair][:, a, c, :], start=(c == 0 and w == 0 and a == 0), stop=False)
                    if ft == 0:
                        pe.wait_ge(z_in[run.pair], run.used * 48 + 48)
                        if run.is_(0):
                            pe.wait_ge(b_stacked, 48)
                    k = second * FT + ft
                    pe.matmul(gate_ps[:, bank, :], low_b_stack[:, k * P:k * P + P], z_stack[run.pair][:, :],
                              start=False, stop=True).then_inc(gate_made, 1)
                    at_least(pe, product_done, p - 1)
                    for c in range(KC):
                        for w, a in PASSES:
                            mm = pe.matmul(up_ps[:, bank, :], w_split[:, w, ft, c * 2 * P + P:(c + 1) * 2 * P],
                                           h_split[run.pair][:, a, c, :], start=(c == 0 and w == 0 and a == 0),
                                           stop=(c == KC - 1 and (w, a) == PASSES[2]))
                    mm.then_inc(up_made, 1)
                    if ft > 0:
                        down(p - 1, ft - 1, run.n)
                    elif not run.is_(0):
                        down(p - 1, FT - 1, run.n - 1)

            runs(pe, body)
            down(RUNS * FT - 1, FT - 1, RUNS - 1)


def tables():
    inv_freq = np.float32(10000.0) ** (-np.arange(0, HD, 2, dtype=np.float32) / np.float32(HD))
    angle = np.arange(SEQ, dtype=np.float32)[None, :] * inv_freq[:, None].astype(np.float32)
    dim = np.arange(P) % (2 * HD) // 2
    out = np.zeros((P, CONSTS), np.float32)
    out[:, COS:COS + SEQ] = np.cos(angle)[dim // 2]
    out[:, SIN:SIN + SEQ] = np.sin(angle)[dim // 2] * np.where(dim % 2 == 0, -1.0, 1.0)[:, None]
    out[:, EYE:EYE + P] = np.eye(P)
    out[:, ROWMASK + SEQ - P:ROWMASK + SEQ] = np.triu(np.full((P, P), NEG), 1)
    out[:, COLMASK:COLMASK + P] = np.tril(np.full((P, P), NEG), -1)
    out[:, COUNT:COUNT + 8] = np.arange(8)
    return out


def chunked(w):
    return w.reshape(-1, P, w.shape[1]).transpose(1, 0, 2)


def by_dimension(w):
    return w.reshape(GROUPS, GH, -1, w.shape[1]).transpose(0, 2, 1, 3).reshape(w.shape)


def by_pair(w):
    return w.reshape(HEADS // 2, 2, -1, w.shape[1]).transpose(0, 2, 1, 3).reshape(w.shape)


def layout(**t):
    a = {k: np.asarray(v) for k, v in t.items()}
    one = {k[len("L0_attn_"):]: v for k, v in a.items() if k.startswith("L0_attn_")}
    two = {k[len("L0_ffn_"):]: v for k, v in a.items() if k.startswith("L0_ffn_")}
    b_q, b_k = (np.stack([by_pair(m) for m in one[n]]) for n in ("Bq", "Bk"))
    out = {
        "x_t": chunked(one["x"].reshape(-1, D).T),
        "wq_t": chunked(by_pair(one["Wq"]).T),
        "wk_t": chunked(by_pair(one["Wk"]).T),
        "wv_t": chunked(one["Wv"].T),
        "a_qkv": np.stack([one["Aq"], one["Ak"], one["Av"]], 2).transpose(0, 3, 1, 2).reshape(
            ADAPTERS, KC, P, 3 * RANK).transpose(0, 2, 1, 3),
        "b_qkv": np.stack([b_q, b_k, one["Bv"]], 1).transpose(0, 3, 1, 2).reshape(ADAPTERS, P, -1),
        "starts": one["lora_start_indices"].reshape(1, -1),
        "x": one["x"].reshape(-1, D),
        "wo_t": chunked(by_dimension(one["Wo"].T)),
        "a_o": np.stack([chunked(by_dimension(m.T)) for m in one["Ao"]]),
        "b_o": one["Bo"].transpose(0, 2, 1).reshape(ADAPTERS, P, -1),
        "wq2_t": chunked(by_pair(two["Wq"]).T),
        "wk2_t": chunked(by_pair(two["Wk"]).T),
        "wv2": chunked(two["Wv"]),
        "wo2": chunked(two["Wo"]),
        "low_a": chunked(two["A"]),
        "mlp_w": np.concatenate([np.stack([chunked(two[n].T).reshape(P, KC, F // P, P) for n in (
            "W_in_base", "W_up_base")], 3).transpose(2, 0, 1, 3, 4).reshape(F // P, P, -1),
            two["W_down"].T.reshape(F // P, P, D)], 2),
        "low_b": two["B"].reshape(P, -1),
        "ln_w": np.stack([two["ln1_w"].reshape(KC, P).T, two["ln2_w"].reshape(KC, P).T], 1),
        "selector": np.repeat(np.eye(RANK, dtype=np.float32), GH, 0),
        "consts": tables(),
    }
    return {k: np.ascontiguousarray(v) for k, v in out.items()}


def build(nc, t, out):
    def scratch(name, shape):
        return nc.dram_tensor(name, shape, F32, kind="Internal").ap()

    sums = scratch("softmax_sums", [GH, SEQ])
    attn = scratch("attention_t", [P, KC, BATCH * SEQ])
    x1 = scratch("x1", [BATCH * SEQ, D])
    h = scratch("h_t", [P, KC, BATCH * SEQ])
    z = scratch("z", [2, RANK, BATCH * SEQ])
    with ExitStack() as ctx:
        both = Shared(nc, ctx)
        attention_layer(nc, both, t["x_t"], t["wq_t"], t["wk_t"], t["wv_t"], t["a_qkv"], t["b_qkv"], t["starts"],
                        t["consts"], t["wo_t"], t["wq2_t"], t["wk2_t"], t["ln_w"], sums, attn)
        gate_layer(nc, both, t["x"], attn, t["a_o"], t["b_o"], t["wv2"], t["wo2"], t["low_a"], t["selector"], sums,
                   x1, h, z)
    mlp_layer(nc, t["mlp_w"], t["low_b"], t["ln_w"], x1, h, z, out)


def kernel(**inputs):
    import concourse.bacc as bacc
    from concourse.bass_utils import run_bass_kernel_spmd

    arrays = {f"in_{k}": v for k, v in layout(**inputs).items()}
    nc = bacc.Bacc("TRN2", target_bir_lowering=False, num_devices=1)
    t = {k[len("in_"):]: nc.dram_tensor(k, v.shape, mybir.dt.from_np(v.dtype), kind="ExternalInput").ap()
         for k, v in arrays.items()}
    out = nc.dram_tensor("out_0_dram", [BATCH * SEQ, D], F32, kind="ExternalOutput").ap()
    build(nc, t, out)
    r = run_bass_kernel_spmd(nc, [arrays], core_ids=[0])
    return r.results[0]["out_0_dram"].reshape(BATCH, SEQ, D)
```
